# Optimizing a Trainium2 kernel written in Bass

```python
import numpy as np
import jax
import jax.numpy as jnp

def _softmax(x, axis=-1):
    return jax.nn.softmax(x, axis=axis)

def _gelu(x):
    return jax.nn.gelu(x, approximate=True)

def _silu(x):
    return jax.nn.silu(x)

def _sigmoid(x):
    return jax.nn.sigmoid(x)

def _layernorm(x, axis=-1, eps=1e-05):
    m = jnp.mean(x, axis=axis, keepdims=True)
    v = jnp.var(x, axis=axis, keepdims=True)
    return (x - m) / jnp.sqrt(v + eps)

def _scatter_add(tgt, idx, src, axis=0):
    return tgt.at[idx].add(src)

def _segment_sum(src, seg, n):
    return jax.ops.segment_sum(src, seg, n)
kernel_name = 'mk_xattn_ffn_d2_seqx_r4_de960b'

def setup_inputs(seed: int=0):
    np.random.seed(seed)
    _w = jnp.asarray

    def _rec_inputs():
        import jax
        import jax.numpy as jnp
        _rk = jax.random.key(seed)
        x = -0.0002928 + 1 * jax.random.normal(jax.random.fold_in(_rk, 1), (8, 256, 256), jnp.float32)
        _lenS = 256 - jax.random.randint(jax.random.fold_in(_rk, 7), (8,), 0, max(1, 256 // 4) + 1, jnp.int32)
        _lenS2 = 256 - jax.random.randint(jax.random.fold_in(_rk, 8), (8,), 0, max(1, 256 // 4) + 1, jnp.int32)
        _ctx_1024P = jax.random.normal(jax.random.fold_in(_rk, 11), (8, 16, 256), jnp.float32)
        _ctx_1024c = jax.random.dirichlet(jax.random.fold_in(_rk, 511), 0.3 * jnp.ones((16,), jnp.float32), (8, 256))
        _ctx_1024t = jnp.einsum('bsk,bkd->bsd', _ctx_1024c, _ctx_1024P)
        _ctx_1024t = _ctx_1024t * jax.lax.rsqrt(jnp.mean(jnp.square(_ctx_1024t)) + 1e-12) * 0.953939
        ctx_1024 = -1.39393e-06 + 0.999914 * (_ctx_1024t + 0.3 * jax.random.normal(jax.random.fold_in(_rk, 611), (8, 256, 256), jnp.float32))
        return (x, ctx_1024)
    x, ctx_1024 = _rec_inputs()

    def _L0_xattn_setup():
        import jax, jax.numpy as jnp
        import numpy as np
        EMBED_DIM = 256
        NUM_HEADS = 16
        HEAD_DIM = EMBED_DIM // NUM_HEADS
        SEG_LENS = [256, 512, 1024]
        DIL_RATIOS = [1, 2, 4]
        NEG = -100000000.0

        def _branch(q, k, v, sl, dr, L):
            B = q.shape[0]
            H, D = (NUM_HEADS, HEAD_DIM)
            sl = min(sl, L)
            pad = -L % sl
            if pad:
                pw = ((0, 0), (0, pad), (0, 0), (0, 0))
                q, k, v = (jnp.pad(q, pw), jnp.pad(k, pw), jnp.pad(v, pw))
            n = (L + pad) // sl
            qs = q.reshape(B * n, sl, H, D)
            ks = k.reshape(B * n, sl, H, D)
            vs = v.reshape(B * n, sl, H, D)
            hg = H // dr
            g = sl // dr
            grp = jnp.arange(H) // hg
            pos = jnp.arange(g)[:, None] * dr + grp[None]
            hidx = jnp.arange(H)[None, :]
            sp = lambda x: x[:, pos, hidx, :]
            qd, kd, vd = (sp(qs), sp(ks), sp(vs))
            scores = jnp.einsum('bqhd,bkhd->bhqk', qd, kd) * D ** (-0.5)
            mask = jnp.tril(jnp.ones((g, g), bool))
            scores = jnp.where(mask, scores, -jnp.inf)
            lse = jax.nn.logsumexp(scores, axis=-1)
            o = jnp.einsum('bhqk,bkhd->bqhd', jnp.exp(scores - lse[..., None]), vd)
            hcol = jnp.arange(H)[:, None]
            od = jnp.zeros((B * n, H, sl, D), o.dtype).at[:, hcol, pos.T].set(o.transpose(0, 2, 1, 3))
            ld = jnp.zeros((B * n, H, sl), lse.dtype).at[:, hcol, pos.T].set(lse)
            ld = jnp.where(ld == 0.0, NEG, ld)
            od = od.reshape(B, n, H, sl, D).transpose(0, 2, 1, 3, 4)
            od = od.reshape(B, H, n * sl, D)[:, :, :L]
            ld = ld.reshape(B, n, H, sl).transpose(0, 2, 1, 3).reshape(B, H, n * sl)[:, :, :L]
            return (od, ld)
        root = jax.random.key(seed)
        ks = jax.random.split(root, 12)
        B, L, E = (1, 1024, EMBED_DIM)
        s = 0.02
        return {'query': jax.random.normal(ks[0], (B, L, E), jnp.float32), 'key': jax.random.normal(ks[1], (B, L, E), jnp.float32), 'value': jax.random.normal(ks[2], (B, L, E), jnp.float32), 'Wq': jax.random.normal(ks[3], (E, E), jnp.float32) * s, 'bq': jnp.zeros((E,), jnp.float32), 'Wk': jax.random.normal(ks[4], (E, E), jnp.float32) * s, 'bk': jnp.zeros((E,), jnp.float32), 'Wv': jax.random.normal(ks[5], (E, E), jnp.float32) * s, 'bv': jnp.zeros((E,), jnp.float32), 'Wo': jax.random.normal(ks[6], (E, E), jnp.float32) * s, 'bo': jnp.zeros((E,), jnp.float32)}
    _L0_xattn_all = _L0_xattn_setup()
    _L0_xattn_in = {k: v for k, v in _L0_xattn_all.items() if k in ('Wq', 'bq', 'Wk', 'bk', 'Wv', 'bv', 'Wo', 'bo')}
    del _L0_xattn_all

    def _L0_ffn_setup():
        import jax, jax.numpy as jnp
        import numpy as np
        HIDDEN = 256
        N_ROUTED = 16
        N_SHARED = 2
        TOP_K = 2
        MID_R = HIDDEN // 4
        MID_S = HIDDEN // 2
        key = jax.random.key(seed)
        ks = jax.random.split(key, 8)
        s = 0.02
        return {'x': jax.random.normal(ks[0], (2, 256, HIDDEN), dtype=jnp.float32), 'router_w': jax.random.normal(ks[1], (HIDDEN, N_ROUTED), dtype=jnp.float32) * s, 'wg_r': jax.random.normal(ks[2], (N_ROUTED, HIDDEN, MID_R), dtype=jnp.float32) * s, 'wu_r': jax.random.normal(ks[3], (N_ROUTED, HIDDEN, MID_R), dtype=jnp.float32) * s, 'wd_r': jax.random.normal(ks[4], (N_ROUTED, MID_R, HIDDEN), dtype=jnp.float32) * s, 'wg_s': jax.random.normal(ks[5], (N_SHARED, HIDDEN, MID_S), dtype=jnp.float32) * s, 'wu_s': jax.random.normal(ks[6], (N_SHARED, HIDDEN, MID_S), dtype=jnp.float32) * s, 'wd_s': jax.random.normal(ks[7], (N_SHARED, MID_S, HIDDEN), dtype=jnp.float32) * s}
    _L0_ffn_all = _L0_ffn_setup()
    _L0_ffn_in = {k: v for k, v in _L0_ffn_all.items() if k in ('router_w', 'wg_r', 'wu_r', 'wd_r', 'wg_s', 'wu_s', 'wd_s')}
    del _L0_ffn_all

    def _L1_xattn_setup():
        import jax, jax.numpy as jnp
        import numpy as np
        DIM = 256
        NUM_HEADS = 16
        DIM_HEAD = 64
        INNER = NUM_HEADS * DIM_HEAD
        SCALE = DIM_HEAD ** (-0.5)

        def _layernorm(x, gamma, beta, eps=1e-05):
            mu = jnp.mean(x, axis=-1, keepdims=True)
            var = jnp.mean(jnp.square(x - mu), axis=-1, keepdims=True)
            return (x - mu) * jax.lax.rsqrt(var + eps) * gamma + beta
        key = jax.random.key(seed)
        ks = jax.random.split(key, 8)
        B, SQ, SK = (2, 512, 1024)
        x = jax.random.normal(ks[0], (B, SQ, DIM), dtype=jnp.float32)
        context = jax.random.normal(ks[1], (B, SK, DIM), dtype=jnp.float32)
        ln_gamma = jnp.ones((DIM,), jnp.float32)
        ln_beta = jnp.zeros((DIM,), jnp.float32)
        w_q = jax.random.normal(ks[2], (DIM, INNER), dtype=jnp.float32) / np.sqrt(DIM)
        w_kv = jax.random.normal(ks[3], (DIM, 2 * INNER), dtype=jnp.float32) / np.sqrt(DIM)
        w_out = jax.random.normal(ks[4], (INNER, DIM), dtype=jnp.float32) / np.sqrt(INNER)
        b_out = jnp.zeros((DIM,), jnp.float32)
        gate = jnp.array([0.5], jnp.float32)
        return {'x': x, 'context': context, 'ln_gamma': ln_gamma, 'ln_beta': ln_beta, 'w_q': w_q, 'w_kv': w_kv, 'w_out': w_out, 'b_out': b_out, 'gate': gate}
    _L1_xattn_all = _L1_xattn_setup()
    _L1_xattn_in = {k: v for k, v in _L1_xattn_all.items() if k in ('ln_gamma', 'ln_beta', 'w_q', 'w_kv', 'w_out', 'b_out', 'gate')}
    del _L1_xattn_all

    def _L1_ffn_setup():
        import jax, jax.numpy as jnp
        import numpy as np
        TOP_K = 2
        key = jax.random.key(seed)
        ks = jax.random.split(key, 5)
        B, T, D, F, E = (4, 512, 256, 1024, 8)
        s = 0.02
        return {'x': jax.random.normal(ks[0], (B, T, D), jnp.float32), 'gate_w': jax.random.normal(ks[1], (D, E), jnp.float32) * s, 'w1': jax.random.normal(ks[2], (E, D, F), jnp.float32) * s, 'w3': jax.random.normal(ks[3], (E, D, F), jnp.float32) * s, 'w2': jax.random.normal(ks[4], (E, F, D), jnp.float32) * s}
    _L1_ffn_all = _L1_ffn_setup()
    _L1_ffn_in = {k: v for k, v in _L1_ffn_all.items() if k in ('gate_w', 'w1', 'w3', 'w2')}
    del _L1_ffn_all
    return {'x': x, 'ctx_1024': ctx_1024, 'L0_xattn_Wq': _L0_xattn_in['Wq'], 'L0_xattn_bq': _L0_xattn_in['bq'], 'L0_xattn_Wk': _L0_xattn_in['Wk'], 'L0_xattn_bk': _L0_xattn_in['bk'], 'L0_xattn_Wv': _L0_xattn_in['Wv'], 'L0_xattn_bv': _L0_xattn_in['bv'], 'L0_xattn_Wo': _L0_xattn_in['Wo'], 'L0_xattn_bo': _L0_xattn_in['bo'], 'L0_ffn_router_w': _L0_ffn_in['router_w'], 'L0_ffn_wg_r': _L0_ffn_in['wg_r'], 'L0_ffn_wu_r': _L0_ffn_in['wu_r'], 'L0_ffn_wd_r': _L0_ffn_in['wd_r'], 'L0_ffn_wg_s': _L0_ffn_in['wg_s'], 'L0_ffn_wu_s': _L0_ffn_in['wu_s'], 'L0_ffn_wd_s': _L0_ffn_in['wd_s'], 'L1_xattn_ln_gamma': _L1_xattn_in['ln_gamma'], 'L1_xattn_ln_beta': _L1_xattn_in['ln_beta'], 'L1_xattn_w_q': _L1_xattn_in['w_q'], 'L1_xattn_w_kv': _L1_xattn_in['w_kv'], 'L1_xattn_w_out': _L1_xattn_in['w_out'], 'L1_xattn_b_out': _L1_xattn_in['b_out'], 'L1_xattn_gate': _L1_xattn_in['gate'], 'L1_ffn_gate_w': _L1_ffn_in['gate_w'], 'L1_ffn_w1': _L1_ffn_in['w1'], 'L1_ffn_w3': _L1_ffn_in['w3'], 'L1_ffn_w2': _L1_ffn_in['w2']}

def reference(x, ctx_1024, L0_xattn_Wq, L0_xattn_bq, L0_xattn_Wk, L0_xattn_bk, L0_xattn_Wv, L0_xattn_bv, L0_xattn_Wo, L0_xattn_bo, L0_ffn_router_w, L0_ffn_wg_r, L0_ffn_wu_r, L0_ffn_wd_r, L0_ffn_wg_s, L0_ffn_wu_s, L0_ffn_wd_s, L1_xattn_ln_gamma, L1_xattn_ln_beta, L1_xattn_w_q, L1_xattn_w_kv, L1_xattn_w_out, L1_xattn_b_out, L1_xattn_gate, L1_ffn_gate_w, L1_ffn_w1, L1_ffn_w3, L1_ffn_w2):
    import jax
    import jax.numpy as jnp

    def _L0_xattn_ref(query, key, value, Wq, bq, Wk, bk, Wv, bv, Wo, bo):
        import jax, jax.numpy as jnp
        import numpy as np
        EMBED_DIM = 256
        NUM_HEADS = 16
        HEAD_DIM = EMBED_DIM // NUM_HEADS
        SEG_LENS = [256, 512, 1024]
        DIL_RATIOS = [1, 2, 4]
        NEG = -100000000.0

        def _branch(q, k, v, sl, dr, L):
            B = q.shape[0]
            H, D = (NUM_HEADS, HEAD_DIM)
            sl = min(sl, L)
            pad = -L % sl
            if pad:
                pw = ((0, 0), (0, pad), (0, 0), (0, 0))
                q, k, v = (jnp.pad(q, pw), jnp.pad(k, pw), jnp.pad(v, pw))
            n = (L + pad) // sl
            qs = q.reshape(B * n, sl, H, D)
            ks = k.reshape(B * n, sl, H, D)
            vs = v.reshape(B * n, sl, H, D)
            hg = H // dr
            g = sl // dr
            grp = jnp.arange(H) // hg
            pos = jnp.arange(g)[:, None] * dr + grp[None]
            hidx = jnp.arange(H)[None, :]
            sp = lambda x: x[:, pos, hidx, :]
            qd, kd, vd = (sp(qs), sp(ks), sp(vs))
            scores = jnp.einsum('bqhd,bkhd->bhqk', qd, kd) * D ** (-0.5)
            mask = jnp.tril(jnp.ones((g, g), bool))
            scores = jnp.where(mask, scores, -jnp.inf)
            lse = jax.nn.logsumexp(scores, axis=-1)
            o = jnp.einsum('bhqk,bkhd->bqhd', jnp.exp(scores - lse[..., None]), vd)
            hcol = jnp.arange(H)[:, None]
            od = jnp.zeros((B * n, H, sl, D), o.dtype).at[:, hcol, pos.T].set(o.transpose(0, 2, 1, 3))
            ld = jnp.zeros((B * n, H, sl), lse.dtype).at[:, hcol, pos.T].set(lse)
            ld = jnp.where(ld == 0.0, NEG, ld)
            od = od.reshape(B, n, H, sl, D).transpose(0, 2, 1, 3, 4)
            od = od.reshape(B, H, n * sl, D)[:, :, :L]
            ld = ld.reshape(B, n, H, sl).transpose(0, 2, 1, 3).reshape(B, H, n * sl)[:, :, :L]
            return (od, ld)
        B, L, E = query.shape
        H, D = (NUM_HEADS, HEAD_DIM)
        q = (query @ Wq.T + bq).reshape(B, L, H, D)
        k = (key @ Wk.T + bk).reshape(B, L, H, D)
        v = (value @ Wv.T + bv).reshape(B, L, H, D)
        outs, lses = ([], [])
        for sl, dr in zip(SEG_LENS, DIL_RATIOS):
            o, l = _branch(q, k, v, sl, dr, L)
            outs.append(o)
            lses.append(l)
        lse_all = jnp.stack(lses, 0)[..., None]
        m = lse_all.max(0)
        w = jnp.exp(lse_all - m)
        w = w / w.sum(0)
        w = jax.lax.stop_gradient(w)
        out = sum((o * wi.astype(o.dtype) for o, wi in zip(outs, w)))
        out = out.transpose(0, 2, 1, 3).reshape(B, L, E)
        return out @ Wo.T + bo

    def _L0_ffn_ref(x, router_w, wg_r, wu_r, wd_r, wg_s, wu_s, wd_s):
        import jax, jax.numpy as jnp
        import numpy as np
        HIDDEN = 256
        N_ROUTED = 16
        N_SHARED = 2
        TOP_K = 2
        MID_R = HIDDEN // 4
        MID_S = HIDDEN // 2
        orig_shape = x.shape
        flat = x.reshape(-1, orig_shape[-1])
        gs = jnp.einsum('td,ndm->tnm', flat, wg_s)
        us = jnp.einsum('td,ndm->tnm', flat, wu_s)
        out = jnp.einsum('tnm,nmd->td', jax.nn.silu(gs) * us, wd_s)
        logits = (flat @ router_w).astype(jnp.float32)
        probs = jax.nn.softmax(logits, axis=-1)
        weights, indices = jax.lax.top_k(probs, TOP_K)
        weights = weights / (weights.sum(axis=-1, keepdims=True) + 1e-09)
        weights = weights.astype(x.dtype)
        comb = jnp.sum(jax.nn.one_hot(indices, N_ROUTED, dtype=x.dtype) * weights[..., None], axis=1)
        g = jnp.einsum('td,edm->tem', flat, wg_r)
        u = jnp.einsum('td,edm->tem', flat, wu_r)
        h = jax.nn.silu(g) * u
        h = h * comb[:, :, None]
        out = out + jnp.einsum('tem,emd->td', h, wd_r)
        return out.reshape(orig_shape)

    def _L1_xattn_ref(x, context, ln_gamma, ln_beta, w_q, w_kv, w_out, b_out, gate):
        import jax, jax.numpy as jnp
        import numpy as np
        DIM = 256
        NUM_HEADS = 16
        DIM_HEAD = 64
        INNER = NUM_HEADS * DIM_HEAD
        SCALE = DIM_HEAD ** (-0.5)

        def _layernorm(x, gamma, beta, eps=1e-05):
            mu = jnp.mean(x, axis=-1, keepdims=True)
            var = jnp.mean(jnp.square(x - mu), axis=-1, keepdims=True)
            return (x - mu) * jax.lax.rsqrt(var + eps) * gamma + beta
        B, SQ, _ = x.shape
        SK = context.shape[1]
        xn = _layernorm(x, ln_gamma, ln_beta)
        q = (xn @ w_q).reshape(B, SQ, NUM_HEADS, DIM_HEAD)
        kv = context @ w_kv
        k, v = jnp.split(kv, 2, axis=-1)
        k = k.reshape(B, SK, NUM_HEADS, DIM_HEAD)
        v = v.reshape(B, SK, NUM_HEADS, DIM_HEAD)
        scores = jnp.einsum('bqhd,bkhd->bhqk', q * SCALE, k)
        attn = jax.nn.softmax(scores, axis=-1)
        out = jnp.einsum('bhqk,bkhd->bqhd', attn, v).reshape(B, SQ, INNER)
        out = out @ w_out + b_out
        return out * jnp.tanh(gate[0])

    def _L1_ffn_ref(x, gate_w, w1, w3, w2):
        import jax, jax.numpy as jnp
        import numpy as np
        TOP_K = 2
        logits = jnp.einsum('btd,de->bte', x, gate_w)
        probs = jax.nn.softmax(logits, axis=-1)
        expert_weights, expert_indices = jax.lax.top_k(probs, TOP_K)
        expert_weights = expert_weights / expert_weights.sum(-1, keepdims=True)
        E = w1.shape[0]
        out = jnp.zeros_like(x)
        for i in range(E):
            wi = jnp.where(expert_indices == i, expert_weights, 0.0).sum(-1)
            h = jax.nn.silu(jnp.einsum('btd,df->btf', x, w1[i])) * jnp.einsum('btd,df->btf', x, w3[i])
            out = out + jnp.einsum('btf,fd->btd', h, w2[i]) * wi[..., None]
        return out
    x = x + _L0_xattn_ref(_layernorm(x, axis=-1), ctx_1024, ctx_1024, L0_xattn_Wq, L0_xattn_bq, L0_xattn_Wk, L0_xattn_bk, L0_xattn_Wv, L0_xattn_bv, L0_xattn_Wo, L0_xattn_bo)
    x = x + _L0_ffn_ref(_layernorm(x, axis=-1), L0_ffn_router_w, L0_ffn_wg_r, L0_ffn_wu_r, L0_ffn_wd_r, L0_ffn_wg_s, L0_ffn_wu_s, L0_ffn_wd_s)
    x = x + _L1_xattn_ref(_layernorm(x, axis=-1), ctx_1024, L1_xattn_ln_gamma, L1_xattn_ln_beta, L1_xattn_w_q, L1_xattn_w_kv, L1_xattn_w_out, L1_xattn_b_out, L1_xattn_gate)
    x = x + _L1_ffn_ref(_layernorm(x, axis=-1), L1_ffn_gate_w, L1_ffn_w1, L1_ffn_w3, L1_ffn_w2)
    return x

_drawn_inputs = setup_inputs


def setup_inputs(seed=0):
    import zlib

    import numpy as np

    out = dict(_drawn_inputs(seed))
    spreads = {'L0_xattn_bq': (0.0, 0.8),
     'L0_xattn_bk': (0.0, 2.0),
     'L0_xattn_bv': (0.0, 0.1),
     'L0_xattn_bo': (0.0, 0.1),
     'L1_xattn_ln_gamma': (1.0, 0.6),
     'L1_xattn_ln_beta': (0.0, 2.0),
     'L1_xattn_b_out': (0.0, 0.769)}
    factors = {'L0_xattn_Wq': 8.0,
     'L0_xattn_Wk': 8.0,
     'L0_ffn_router_w': 8.0,
     'L0_ffn_wg_r': 8.0,
     'L0_ffn_wu_r': 8.0,
     'L0_ffn_wd_r': 8.0,
     'L0_ffn_wg_s': 3.468,
     'L0_ffn_wu_s': 3.403,
     'L0_ffn_wd_s': 3.414,
     'L1_ffn_gate_w': 22.728,
     'L1_ffn_w1': 8.0,
     'L1_ffn_w3': 8.0,
     'L1_ffn_w2': 8.0}
    for name, (base, spread) in spreads.items():
        noise = np.random.default_rng([zlib.crc32(name.encode()), seed]).standard_normal(out[name].shape)
        drawn = base * np.exp(spread * noise) if base else spread * noise
        out[name] = jnp.asarray(drawn.astype(out[name].dtype))
    for name, factor in factors.items():
        out[name] = (out[name] * factor).astype(out[name].dtype)
    return out
```

```python
from contextlib import ExitStack

import concourse.bass as bass
from concourse import mybir

F32 = mybir.dt.float32
BF16 = mybir.dt.bfloat16
I32 = mybir.dt.int32
U32 = mybir.dt.uint32
ALU = mybir.AluOpType
ACT = mybir.ActivationFunctionType
AX = mybir.AxisListType

P = 128
B, L, D = 8, 256, 256
T = L // P
KD = D // P
EPS = 1e-5

H0, DH0 = 16, 16
G0 = P // DH0
HG = 4
NBR = 3
E0N, M0R, M0S = 16, 64, 256
F0 = E0N * M0R + M0S
F0T = F0 // P
CH0 = [(0, 512), (512, 512), (1024, 256)]

H1, DH1 = 16, 64
I1 = H1 * DH1
I1T = I1 // P

E1N, F1 = 8, 1024
F1T = F1 // P
TOP = 2
NTOK = B * L
CAP = NTOK + P
ROW = D + 2
NBLK = (TOP * NTOK) // P + E1N - 1
WE1 = 2 * KD * F1 + F1T * D
SLOTS = 3

C_F32 = {}
W_F32 = {}


def columns(table, parts):
    at = 0
    for name, n in parts:
        table[name] = (at, n)
        at += n
    return at


NC32 = columns(C_F32, [("ident", P), ("head", G0), ("cover", NBR * T * H0), ("class2", H0 * 4), ("class4", H0 * 4),
                       ("iota", 16), ("region", E1N), ("neghalf", T), ("blocks", NBLK + 1)])
NW32 = columns(W_F32, [("wq0", KD * D), ("wk0", KD * D), ("wv0", KD * D), ("wo0", KD * D),
                       ("router", KD * E0N), ("wg0", KD * F0), ("wu0", KD * F0), ("wd0", F0T * D),
                       ("wq1", KD * I1), ("wk1", KD * I1), ("wv1", KD * I1), ("wo1", I1T * D), ("gate1", KD * E1N),
                       ("bq0", KD), ("bk0", KD), ("gamma", KD), ("beta", KD), ("gate", 1),
                       ("bv0", D), ("bo0", D), ("bo1", D)])
NCB = 4 * P


class Signal:

    def __init__(self, sem, per, start=None):
        self.sem, self.per, self.start = sem, per, per if start is None else start

    def at(self, turn, n):
        return turn * self.per + (self.start + n)


class Ring:

    def __init__(self, banks, full, empty):
        self.banks, self.full, self.empty = banks, full, empty


class Turn:

    def __init__(self, eng, ring, turn):
        self.eng, self.ring, self.turn, self.n = eng, ring, turn, 0

    def claim(self):
        self.n += 1
        self.eng.wait_ge(self.ring.empty.sem, self.ring.empty.at(self.turn, self.n - len(self.ring.banks)))
        return self.ring.banks[(self.n - 1) % len(self.ring.banks)]

    def take(self):
        self.n += 1
        self.eng.wait_ge(self.ring.full.sem, self.ring.full.at(self.turn, self.n))
        return self.ring.banks[(self.n - 1) % len(self.ring.banks)]


PD_K0, PD_V0, PD_Q0, PD_K1, PD_AV0, PD_O0, PD_ROUTER, PD_U, PD_DOWN, PD_Q1, PD_AV1, PD_O1, PD_LOGIT, PD_RANK = (
    1, 2, 3, 4, 6, 7, 8, 9, 15, 16, 18, 26, 27, 28)
PA_K1, PA_V1, PA_G, PA_Q1 = 1, 3, 7, 13
TA_XN0, TA_P0, TA_X1, TA_H, TA_X2, TA_P1, TA_X3 = 1, 2, 8, 9, 12, 13, 21
TD_P0, TD_H, TD_P1 = 1, 7, 10
N_PD, N_PA, N_TA, N_TD = 28, 14, 21, 17
N_S0 = H0 // HG + H0 // 2
N_S = N_S0 + I1T * T
N_STEP = 68


def layers(nc, cst, counts_sb, cf32, cb16, w32, tok0, x, ctxT, acc, rows):
    with ExitStack() as ctx:
        def sb(name, shape, dt=F32):
            return ctx.enter_context(nc.sbuf_tensor(name, shape, dt))

        def sem(name):
            return ctx.enter_context(nc.semaphore(name))

        def bank(name):
            return ctx.enter_context(nc.psum_tensor(name, [P, 512], F32))

        cbf = sb("cbf", [P, NCB], BF16)
        wts = sb("wts", [P, NW32])

        def c(name):
            return cst[:, C_F32[name][0]:sum(C_F32[name])]

        def w(name, k=1):
            ap = wts[:, W_F32[name][0]:sum(W_F32[name])]
            return ap.rearrange("p (k n) -> p k n", k=k) if k > 1 else ap

        ident = c("ident")
        identb, causal, below, onesb = (cbf[:, i * P:(i + 1) * P] for i in range(4))
        cover = c("cover").rearrange("p (r n) -> p r n", r=NBR)
        class2 = c("class2").rearrange("p (h c) -> p h c", c=4)
        class4 = c("class4").rearrange("p (h c) -> p h c", c=4)
        wq0, wk0, wv0, wo0 = (w(n, KD) for n in ("wq0", "wk0", "wv0", "wo0"))
        router, wg0, wu0, wd0 = w("router", KD), w("wg0", KD), w("wu0", KD), w("wd0", F0T)
        wq1, wk1, wv1, wo1, gate1 = w("wq1", KD), w("wk1", KD), w("wv1", KD), w("wo1", I1T), w("gate1", KD)
        bq0, bk0, gamma, beta = w("bq0"), w("bk0"), w("gamma"), w("beta")
        bv0, bo0, bo1 = w("bv0"), w("bo0"), w("bo1")

        x_in = sb("x_in", [P, T, D])
        ctx_in = sb("ctx_in", [P, KD, L])
        xb = sb("xb", [P, T, D])
        xn = sb("xn", [P, T, D])
        xnT = sb("xnT", [P, KD, L])
        x1 = sb("x1", [P, T, D])
        kT0 = sb("kT0", [P, KD, L])
        qT0 = sb("qT0", [P, KD, L])
        kpad0 = sb("kpad0", [P, H0, L])
        vpad0 = sb("vpad0", [P, T, H0, P])
        kpad1 = sb("kpad1", [P, H1, L])
        vpad1 = sb("vpad1", [P, T, H1, P])
        big = sb("big", [P, 6144])
        e0a = big[:, 0:H0 * P].rearrange("p (h k) -> p h k", h=H0)
        e0b = big[:, H0 * P:3 * H0 * P].rearrange("p (h k) -> p h k", h=H0)
        hid = big[:, 0:T * F0].rearrange("p (t f) -> p t f", t=T)
        hidT = big[:, T * F0:T * F0 + F0T * L].rearrange("p (f t) -> p f t", f=F0T)
        p1 = big[:, 0:2048].rearrange("p (r h k) -> p r h k", r=4, h=2)
        pT1 = big[:, 2048:4096].rearrange("p (r k h q) -> p r k h q", r=2, k=T, h=2)
        avT1 = big[:, 4096:6144].rearrange("p (m t) -> p m t", m=I1T)
        mid = sb("mid", [P, 3072])
        pT0a = mid[:, 0:2048].rearrange("p (r h q) -> p r h q", r=2, h=HG)
        pT0b = mid[:, 2048:3072].rearrange("p (r h q) -> p r h q", r=2, h=HG)
        qT1 = mid[:, 0:2048].rearrange("p (m t) -> p m t", m=I1T)
        avT0 = sb("avT0", [P, KD, L])
        hs = sb("hs", [P, 2, 512])
        pay = sb("pay", [P, T, TOP, ROW])
        stats = sb("stats", [P, T, 6])
        mv = sb("mv", [P, T, 2])
        vpe = sb("vpe", [P, T])
        rstd = sb("rstd", [P, T])
        negm0 = sb("negm0", [P, T, H0])
        sums = sb("sums", [P, NBR, T * H0])
        expnm = sb("expnm", [P, T * H0])
        keep = sb("keep", [P, NBR, T * H0])
        ks = sb("ks", [P, NBR, T * H0])
        den = sb("den", [P, T * H0])
        isz = sb("isz", [P, T * H0])
        rden = sb("rden", [P, T * H0])
        coef = sb("coef", [P, NBR, T * H0])
        cfa = sb("cfa", [P, T * H0, 4])
        cfb = sb("cfb", [P, T * H0, 4])
        negm1 = sb("negm1", [P, 4, 2])
        z1 = sb("z1", [P, 4, 2])
        r1 = sb("r1", [P, 4, 2])
        lg = sb("lg", [P, T, 16])
        pr = sb("pr", [P, T, 16])
        lnm = sb("lnm", [P, T])
        lsum = sb("lsum", [P, T])
        top8 = sb("top8", [P, T, 8])
        idx8 = sb("idx8", [P, T, 8], U32)
        idxf = sb("idxf", [P, T, TOP])
        wsum = sb("wsum", [P, T])
        wtop = sb("wtop", [P, T, TOP])
        comb = sb("comb", [P, T, E0N])
        comb2 = sb("comb2", [P, T, E0N])
        hot = sb("hot", [P, T, TOP, E1N])
        both = sb("both", [P, T, E1N], BF16)
        rank = sb("rank", [P, T, E1N])
        hotr = sb("hotr", [P, T, TOP, E1N])
        posf = sb("posf", [P, T, TOP])
        pos = sb("pos", [P, T, TOP], I32)
        run = sb("run", [P, E1N])
        tok = sb("tok", [P, T], I32)
        tgate = sb("tgate", [P, 1])
        gbo1 = sb("gbo1", [P, D])

        score_banks = [bank(f"score{i}") for i in range(2)]
        turn_a, turn_d = bank("turn_a"), bank("turn_d")
        prod_d = [bank(f"prod_d{i}") for i in range(2)]
        prod_a = [bank(f"prod_a{i}") for i in range(2)]

        signals = {}

        def signal(name, per, owner):
            s = Signal(sem(name), per)
            signals.setdefault(owner, []).append(s)
            return s

        x_loaded = signal("x_loaded", 16, "sp")
        ctx_loaded = signal("ctx_loaded", 16, "sp")
        stored = signal("stored", 16, "act")
        pd = Ring(prod_d, signal("prod_d_full", N_PD, "pe"), signal("prod_d_empty", N_PD, "dve"))
        pa = Ring(prod_a, signal("prod_a_full", N_PA, "pe"), signal("prod_a_empty", N_PA, "act"))
        ta = Ring([turn_a], signal("turn_a_full", N_TA, "pe"), signal("turn_a_empty", N_TA, "act"))
        td = Ring([turn_d], signal("turn_d_full", N_TD, "pe"), signal("turn_d_empty", N_TD, "dve"))
        sc = Ring(score_banks, signal("score_full", N_S, "pe"), signal("score_empty", N_S, "act"))
        av0_used = signal("av0_used", 3, "pe")
        maxed = signal("maxed", N_S, "dve")
        x_used = signal("x_used", 1, "dve")
        var_ready = signal("var_ready", 5, "dve")
        rstd_ready = signal("rstd_ready", 5, "pool")
        normed = signal("normed", 4, "dve")
        guard_exp = signal("guard_exp", 1, "act")
        coef_ready = signal("coef_ready", 1, "dve")
        weighed_d = signal("weighed_d", HG + 1, "dve")
        weighed_p = signal("weighed_p", HG - 1, "pool")
        kpadded = signal("kpadded", KD, "pool")
        lexp = signal("lexp", 2, "act")
        comb_ready = signal("comb_ready", 1, "dve")
        hid_weighed = signal("hid_weighed", 4, "pool")
        recip1 = signal("recip1", I1T * T, "dve")
        p1_ready = signal("p1_ready", I1T * T, "pool")
        both_ready = signal("both_ready", 1, "dve")
        pos_ready = signal("pos_ready", 1, "dve")
        scattered = Signal(sem("scattered"), 16 * T * TOP, 16)
        step = signal("step", N_STEP, "dve")
        kraw = signal("kraw", 1, "dve")

        c_loaded, w_loaded, setup_act, setup_dve = (sem(n) for n in ("c_loaded", "w_loaded", "setup_act", "setup_dve"))
        pads = sem("pads")
        spare = sem("spare")

        def prime(eng, owner):
            for s in signals[owner]:
                eng.sem_inc(s.sem, s.per)

        block = ctx.enter_context(nc.Block())

        @block.sync
        def _(sp):
            prime(sp, "sp")
            sp.dma_start(cst[:, :], cf32).then_inc(c_loaded, 16)
            sp.dma_start(cbf[:, :], cb16).then_inc(c_loaded, 16)
            sp.dma_start(wts[:, :], w32).then_inc(w_loaded, 16)
            with sp.Fori(0, B) as b:
                sp.wait_ge(x_used.sem, x_used.at(b, 0))
                sp.dma_start(x_in[:, :, :], x[bass.ds(b, 1)].rearrange("b (t p) d -> p (b t) d", p=P)).then_inc(x_loaded.sem, 16)
                sp.wait_ge(pa.full.sem, pa.full.at(b, PA_V1 + 3 - N_PA))
                sp.dma_start(ctx_in[:, :, :], ctxT[bass.ds(b, 1)].rearrange("b (k p) t -> p (b k) t", p=P)).then_inc(ctx_loaded.sem, 16)

        @block.gpsimd
        def _(pool):
            prime(pool, "pool")
            pool.dma_start(tok[:, :], tok0).then_inc(scattered.sem, 16)
            nc.gpsimd.memset(vpad0[:, :, :, :], 0.0).then_inc(pads, 1)
            nc.gpsimd.memset(kpad1[:, :, :], 0.0).then_inc(pads, 1)
            nc.gpsimd.memset(vpad1[:, :, :, :], 0.0).then_inc(pads, 1)
            pool.wait_ge(c_loaded, 32)
            with pool.Fori(0, B) as b:
                n_rstd = [0]

                def rsqrt():
                    n_rstd[0] += 1
                    pool.wait_ge(var_ready.sem, var_ready.at(b, n_rstd[0]))
                    nc.gpsimd.tensor_tensor(rstd[:, :], vpe[:, :], c("neghalf"), ALU.pow).then_inc(rstd_ready.sem, 1)

                rsqrt()
                for k in range(KD):
                    pool.wait_ge(*((kraw.sem, kraw.at(b, 1)) if k == 0 else (pd.empty.sem, pd.empty.at(b, PD_K0))))
                    if k == 0:
                        pool.wait_ge(sc.full.sem, sc.full.at(b, N_S0 - N_S))
                    pool.sem_inc(spare, 1)
                    for h in range(G0):
                        ins = nc.gpsimd.tensor_scalar(kpad0[:, k * G0 + h, :], kT0[:, k, :], c("head")[:, h:h + 1], 1.0,
                                                      ALU.mult, ALU.mult)
                    ins.then_inc(kpadded.sem, 1)
                pool.wait_ge(coef_ready.sem, coef_ready.at(b, 1))
                for g in range(1, H0 // HG):
                    v = e0b[:, g * HG:(g + 1) * HG, :].rearrange("p h (k c) -> p h k c", c=4)
                    cf = cfa[:, H0 + g * HG:H0 + (g + 1) * HG, :]
                    nc.gpsimd.tensor_tensor(v, v, cf.rearrange("p h (o c) -> p h o c", o=1).to_broadcast([P, HG, L // 4, 4]),
                                            ALU.mult).then_inc(weighed_p.sem, 1)
                rsqrt()
                n = 0
                for t in range(T):
                    for ci, (f0, fn) in enumerate(CH0[:2]):
                        n += 1
                        pool.wait_ge(pd.empty.sem, pd.empty.at(b, PD_U + t * 3 + ci))
                        pool.wait_ge(comb_ready.sem, comb_ready.at(b, 1))
                        v = hid[:, t, f0:f0 + fn].rearrange("p (e m) -> p e m", m=M0R)
                        ne = fn // M0R
                        cw = comb[:, t, f0 // M0R:f0 // M0R + ne]
                        nc.gpsimd.tensor_tensor(v, v, cw.rearrange("p (e o) -> p e o", o=1).to_broadcast([P, ne, M0R]),
                                                ALU.mult).then_inc(hid_weighed.sem, 1)
                rsqrt()
                rsqrt()
                for i in range(I1T * T):
                    pool.wait_ge(recip1.sem, recip1.at(b, i + 1))
                    pool.sem_inc(spare, 1)
                    for h in range(2):
                        ins = nc.gpsimd.tensor_scalar(p1[:, i % 4, h, :], p1[:, i % 4, h, :], r1[:, i % 4, h:h + 1], 1.0,
                                                      ALU.mult, ALU.mult)
                    ins.then_inc(p1_ready.sem, 1)
                rsqrt()
                pool.wait_ge(pos_ready.sem, pos_ready.at(b, 1))
                pool.sem_inc(spare, 1)
                for t in range(T):
                    for k in range(TOP):
                        pool.indirect_dma_start(rows, bass.IndirectOffsetOnAxis(ap=pos[:, t, k:k + 1], axis=0),
                                                pay[:, t, k, :], None).then_inc(scattered.sem, 16)
            pool.wait_ge(scattered.sem, 16 * T * TOP * B + 16)

        @block.scalar
        def _(act):
            prime(act, "act")
            act.wait_ge(w_loaded, 16)
            nc.scalar.activation(tgate[:, :], w("gate"), ACT.Tanh).then_inc(setup_act, 1)
            act.wait_ge(pads, 3)
            with act.Fori(0, B) as b:
                tra, proda, score = Turn(act, ta, b), Turn(act, pa, b), Turn(act, sc, b)

                def copy_turned(dst):
                    src = tra.take()
                    nc.scalar.activation(dst, src[:, 0:512].rearrange("p (a n) -> p a n", n=dst.shape[-1]), ACT.Copy).then_inc(ta.empty.sem, 1)

                act.wait_ge(pd.full.sem, pd.full.at(b, PD_LOGIT - N_PD))
                copy_turned(xnT[:, :, :])
                for i in range(N_S0):
                    src = score.take()
                    act.wait_ge(maxed.sem, maxed.at(b, i + 1))
                    if i == 0:
                        act.wait_ge(pd.full.sem, pd.full.at(b, PD_O1 - N_PD))
                    t, nh = (0, HG) if i < H0 // HG else (1, 2)
                    h0 = i * HG if t == 0 else (i - H0 // HG) * 2
                    for h in range(nh):
                        e = e0a[:, h0 + h, :] if t == 0 else e0b[:, h0 + h, :]
                        n = (t + 1) * P
                        ins = nc.scalar.activation(e, src[:, h * n:(h + 1) * n], ACT.Exp, bias=negm0[:, t, h0 + h:h0 + h + 1],
                                                   accum_out=sums[:, 0, t * H0 + h0 + h:t * H0 + h0 + h + 1])
                    ins.then_inc(sc.empty.sem, 1)
                nc.scalar.activation(expnm[:, :], negm0[:, :, :].rearrange("p t h -> p (t h)"), ACT.Exp).then_inc(guard_exp.sem, 1)
                for _k in range(2):
                    src = proda.take()
                    if _k == 0:
                        act.wait_ge(sc.full.sem, sc.full.at(b, 0))
                    m = 4 * _k
                    v = src[:, :].rearrange("p (m n) -> p m n", m=2)
                    kp = kpad1[:, :, :].rearrange("p (m e) n -> p m e n", e=2)
                    nc.scalar.activation(kp[0:64, m:m + 2, 0, :], v[0:64], ACT.Copy)
                    nc.scalar.activation(kp[64:P, m:m + 2, 1, :], v[64:P], ACT.Copy).then_inc(pa.empty.sem, 1)
                for i in range(0, 12, 2):
                    g, seg = i // 3, i % 3
                    if g >= 2:
                        act.wait_ge(av0_used.sem, av0_used.at(b, g - 1))
                    dst = pT0b[:, g % 2] if seg == 2 else pT0a[:, g % 2, :, seg * P:(seg + 1) * P]
                    copy_turned(dst)
                for i in range(4):
                    t, half = i // 2, i % 2
                    src = proda.take()
                    if i == 0:
                        act.wait_ge(pd.full.sem, pd.full.at(b, PD_AV1 + 7 - N_PD))
                    dst = vpad1[:, t, :, :].rearrange("p (m e) (f n) -> p m e f n", e=2, f=2)
                    v = src[:, :].rearrange("p (m e n) -> p m e n", e=2, n=DH1)
                    nc.scalar.activation(dst[:, half * 4:half * 4 + 4, 0, 0, :], v[:, :, 0, :], ACT.Copy)
                    nc.scalar.activation(dst[:, half * 4:half * 4 + 4, 1, 1, :], v[:, :, 1, :], ACT.Copy).then_inc(pa.empty.sem, 1)
                act.wait_ge(pd.full.sem, pd.full.at(b, PD_Q0))
                copy_turned(xnT[:, :, :])
                act.wait_ge(pd.empty.sem, pd.empty.at(b, PD_ROUTER))
                nc.scalar.activation(pr[:, :, :], lg[:, :, :], ACT.Exp).then_inc(lexp.sem, 1)
                for i in range(6):
                    t, (f0, fn) = i // 3, CH0[i % 3]
                    src = proda.take()
                    if i >= 2:
                        act.wait_ge(pd.empty.sem, pd.empty.at(b, PD_U + i - 2))
                    nc.scalar.activation(hs[:, i % 2, 0:fn], src[:, 0:fn], ACT.Silu).then_inc(pa.empty.sem, 1)
                for i in range(1, 6, 2):
                    t, (f0, fn) = i // 3, CH0[i % 3]
                    src = tra.take()
                    nf = fn // P
                    nc.scalar.activation(hidT[:, f0 // P:f0 // P + nf, t * P:(t + 1) * P],
                                         src[:, 0:fn].rearrange("p (f n) -> p f n", n=P), ACT.Copy).then_inc(ta.empty.sem, 1)
                src = tra.take()
                act.wait_ge(pa.full.sem, pa.full.at(b, PA_G + 5))
                act.wait_ge(pd.full.sem, pd.full.at(b, PD_U + 5))
                nc.scalar.activation(xnT[:, 0, :], src[:, 0:L], ACT.Identity, bias=beta[:, 0:1], scale=gamma[:, 0:1])
                nc.scalar.activation(xnT[:, 1, :], src[:, L:2 * L], ACT.Identity, bias=beta[:, 1:2], scale=gamma[:, 1:2]).then_inc(ta.empty.sem, 1)
                for _k in range(2):
                    src = proda.take()
                    nc.scalar.activation(qT1[:, 4 * _k:4 * _k + 2, :], src[:, :].rearrange("p (m n) -> p m n", m=2),
                                         ACT.Copy, scale=DH1 ** -0.5).then_inc(pa.empty.sem, 1)

                def copy_p1(i):
                    pair, t = i // 2, i % 2
                    src = tra.take()
                    if pair >= 2:
                        act.wait_ge(pd.full.sem, pd.full.at(b, PD_AV1 + pair - 2))
                    nc.scalar.activation(pT1[:, pair % 2, :, :, t * P:(t + 1) * P],
                                         src[:, :].rearrange("p (k h n) -> p k h n", k=2, h=2), ACT.Copy).then_inc(ta.empty.sem, 1)

                for i in range(I1T * T + 2):
                    if i < I1T * T:
                        src = score.take()
                        act.wait_ge(maxed.sem, maxed.at(b, N_S0 + i + 1))
                        if i >= 4:
                            j = i - 4
                            r, n = (ta, TA_P1 + j // 2) if j % 2 == 0 else (td, TD_P1 + j // 2)
                            act.wait_ge(r.full.sem, r.full.at(b, n))
                            act.wait_ge(recip1.sem, recip1.at(b, j + 1))
                        for h in range(2):
                            ins = nc.scalar.activation(p1[:, i % 4, h, :], src[:, h * L:(h + 1) * L], ACT.Exp,
                                                       bias=negm1[:, i % 4, h:h + 1], accum_out=z1[:, i % 4, h:h + 1])
                        ins.then_inc(sc.empty.sem, 1)
                    if i >= 2 and i % 2 == 0:
                        copy_p1(i - 2)
                act.wait_ge(pd.empty.sem, pd.empty.at(b, PD_O1))
                act.dma_start(acc[bass.ds(b, 1)].rearrange("b (t p) d -> p (b t) d", p=P), x1[:, :, :]).then_inc(stored.sem, 16)
                act.wait_ge(pd.full.sem, pd.full.at(b, PD_Q1 + 1))
                act.wait_ge(pa.full.sem, pa.full.at(b, PA_Q1 + 1))
                copy_turned(xnT[:, :, :])
                act.wait_ge(pd.empty.sem, pd.empty.at(b, PD_LOGIT))
                nc.scalar.activation(pr[:, :, 0:E1N], lg[:, :, 0:E1N], ACT.Exp).then_inc(lexp.sem, 1)
                assert (tra.n, proda.n, score.n) == (N_TA, N_PA, N_S), (tra.n, proda.n, score.n)
            act.wait_ge(stored.sem, 16 * (B + 1))

        @block.vector
        def _(dve):
            prime(dve, "dve")
            dve.wait_ge(c_loaded, 32)
            dve.wait_ge(w_loaded, 16)
            dve.wait_ge(setup_act, 1)
            dve.wait_ge(pads, 3)
            nc.vector.tensor_scalar(gbo1[:, :], bo1, tgate[:, 0:1], None, ALU.mult).then_inc(setup_dve, 1)
            nc.vector.tensor_copy(run[:, :], c("region")).then_inc(setup_dve, 1)
            dve.wait_ge(setup_dve, 2)
            with dve.Fori(0, B) as b:
                trd, prodd = Turn(dve, td, b), Turn(dve, pd, b)
                n_step, n_rstd, n_l = [0], [0], [0]

                def then(ins):
                    n_step[0] += 1
                    ins.then_inc(step.sem, 1)
                    dve.wait_ge(step.sem, step.at(b, n_step[0]))

                def apart():
                    dve.sem_inc(spare, 1)

                def release(ins, place):
                    ins.then_inc(place.ring.empty.sem, 1)
                    dve.wait_ge(place.ring.empty.sem, place.ring.empty.at(b, place.n))

                def norm(src, dst, signal_=None):
                    n_rstd[0] += 1
                    nc.vector.bn_stats(stats[:, 0, :], src[:, 0, :])
                    then(nc.vector.bn_stats(stats[:, 1, :], src[:, 1, :]))
                    apart()
                    nc.vector.bn_aggr(mv[:, 0, :], stats[:, 0, :])
                    then(nc.vector.bn_aggr(mv[:, 1, :], stats[:, 1, :]))
                    nc.vector.tensor_scalar(vpe[:, :], mv[:, :, 1], EPS, None, ALU.add).then_inc(var_ready.sem, 1)
                    dve.wait_ge(rstd_ready.sem, rstd_ready.at(b, n_rstd[0]))
                    for t in range(T):
                        ins = nc.vector.tensor_scalar(dst[:, t, :], src[:, t, :], mv[:, t, 0:1], rstd[:, t:t + 1], ALU.subtract, ALU.mult)
                    if signal_ is not None:
                        ins.then_inc(signal_.sem, 1)
                    else:
                        then(ins)

                def choose(n_experts, eps):
                    n_l[0] += 1
                    src = prodd.take()
                    v = src[:, 0:T * n_experts].rearrange("p (t e) -> p t e", t=T)
                    then(nc.vector.tensor_reduce(lnm[:, :], v, AX.X, ALU.max, negate=True))
                    release(nc.vector.tensor_tensor(lg[:, :, 0:n_experts], v, lnm[:, :].rearrange("p (t o) -> p t o", o=1).to_broadcast([P, T, n_experts]), ALU.add), prodd)
                    dve.wait_ge(lexp.sem, lexp.at(b, n_l[0]))
                    p = pr[:, :, 0:n_experts]
                    then(nc.vector.tensor_reduce(lsum[:, :], p, AX.X, ALU.add))
                    then(nc.vector.reciprocal(lsum[:, :], lsum[:, :]))
                    then(nc.vector.tensor_tensor(p, p, lsum[:, :].rearrange("p (t o) -> p t o", o=1).to_broadcast([P, T, n_experts]), ALU.mult))
                    apart()
                    nc.vector.max(top8[:, 0, :], pr[:, 0, 0:n_experts])
                    then(nc.vector.max(top8[:, 1, :], pr[:, 1, 0:n_experts]))
                    apart()
                    nc.vector.max_index(idx8[:, 0, :], top8[:, 0, :], pr[:, 0, 0:n_experts])
                    then(nc.vector.max_index(idx8[:, 1, :], top8[:, 1, :], pr[:, 1, 0:n_experts]))
                    then(nc.vector.tensor_copy(idxf[:, :, :], idx8[:, :, 0:TOP]))
                    then(nc.vector.tensor_reduce(wsum[:, :], top8[:, :, 0:TOP], AX.X, ALU.add))
                    if eps:
                        then(nc.vector.tensor_scalar(wsum[:, :], wsum[:, :], eps, None, ALU.add))
                    then(nc.vector.reciprocal(wsum[:, :], wsum[:, :]))
                    then(nc.vector.tensor_tensor(wtop[:, :, :], top8[:, :, 0:TOP], wsum[:, :].rearrange("p (t o) -> p t o", o=1).to_broadcast([P, T, TOP]), ALU.mult))

                def copy_turned(dst, n=512, inner=P):
                    src = trd.take()
                    v = src[:, 0:n]
                    v = v.rearrange("p (a n) -> p a n", n=inner) if len(dst.shape) == 3 else v.rearrange("p (k h n) -> p k h n", k=2, h=2)
                    nc.vector.tensor_copy(dst, v).then_inc(td.empty.sem, 1)

                dve.wait_ge(x_loaded.sem, x_loaded.at(b, 16))
                dve.wait_ge(pos_ready.sem, pos_ready.at(b, 0))
                norm(x_in, xn, normed)
                nc.vector.tensor_tensor(xb[:, :, :], x_in[:, :, :], bo0.rearrange("p (o n) -> p o n", o=1).to_broadcast([P, T, D]), ALU.add).then_inc(x_used.sem, 1)
                src = prodd.take()
                dve.wait_ge(kpadded.sem, kpadded.at(b, 0))
                for k, done in enumerate((kraw, pd.empty)):
                    nc.vector.tensor_scalar(kT0[:, k, :], src[:, k * L:(k + 1) * L], bk0[:, k:k + 1], None, ALU.add).then_inc(done.sem, 1)
                src = prodd.take()
                for t in range(T):
                    for k in range(KD):
                        dst = vpad0[:, t, k * G0:(k + 1) * G0, :].rearrange("p h (g n) -> p (h g) n", n=DH0)[:, 0:G0 * G0:G0 + 1, :]
                        v = src[:, t * D + k * P:t * D + (k + 1) * P].rearrange("p (h n) -> p h n", n=DH0)
                        bias = bv0[:, k * P:(k + 1) * P].rearrange("p (h n) -> p h n", n=DH0)
                        ins = nc.vector.tensor_tensor(dst, v, bias, ALU.add)
                ins.then_inc(pd.empty.sem, 1)
                src = prodd.take()
                for k in range(KD):
                    ins = nc.vector.tensor_scalar(qT0[:, k, :], src[:, k * L:(k + 1) * L], bq0[:, k:k + 1], DH0 ** -0.5, ALU.add, ALU.mult)
                ins.then_inc(pd.empty.sem, 1)
                score = Turn(dve, sc, b)
                for i in range(N_S0):
                    src = score.take()
                    t, nh = (0, HG) if i < H0 // HG else (1, 2)
                    h0 = i * HG if t == 0 else (i - H0 // HG) * 2
                    nc.vector.tensor_reduce(negm0[:, t, h0:h0 + nh], src[:, :].rearrange("p (h n) -> p h n", h=nh), AX.X, ALU.max,
                                            negate=True).then_inc(maxed.sem, 1)
                for t, e, done in ((0, e0a, H0 // HG), (1, e0b, N_S0)):
                    dve.wait_ge(sc.empty.sem, sc.empty.at(b, done))
                    for r, step_ in ((1, 2), (2, 4)):
                        nh = H0 // step_
                        for g in range(step_):
                            v = e[:, g * nh:(g + 1) * nh, :].rearrange("p h (k c) -> p h k c", c=step_)[:, :, :, g]
                            ins = (nc.vector.tensor_reduce(sums[:, r, t * H0 + g * nh:t * H0 + (g + 1) * nh], v, AX.X, ALU.add))
                then(ins)
                for _k in range(2):
                    src = prodd.take()
                    m = 4 * _k + 2
                    v = src[:, :].rearrange("p (m n) -> p m n", m=2)
                    kp = kpad1[:, :, :].rearrange("p (m e) n -> p m e n", e=2)
                    nc.vector.tensor_copy(kp[0:64, m:m + 2, 0, :], v[0:64])
                    nc.vector.tensor_copy(kp[64:P, m:m + 2, 1, :], v[64:P]).then_inc(pd.empty.sem, 1)
                dve.wait_ge(guard_exp.sem, guard_exp.at(b, 1))
                bc = lambda ap: ap.rearrange("p (o n) -> p o n", o=1).to_broadcast([P, NBR, T * H0])
                then(nc.vector.tensor_tensor(keep[:, :, :], sums[:, :, :], bc(expnm[:, :]), ALU.not_equal))
                then(nc.vector.tensor_tensor(keep[:, :, :], keep[:, :, :], cover, ALU.mult))
                then(nc.vector.tensor_tensor(ks[:, :, :], keep[:, :, :], sums[:, :, :], ALU.mult))
                then(nc.vector.tensor_reduce(den[:, :], ks[:, :, :].rearrange("p r n -> p n r"), AX.X, ALU.add))
                then(nc.vector.tensor_scalar(isz[:, :], den[:, :], 0.0, None, ALU.is_equal))
                then(nc.vector.tensor_tensor(den[:, :], den[:, :], isz[:, :], ALU.add))
                then(nc.vector.reciprocal(rden[:, :], den[:, :]))
                then(nc.vector.tensor_tensor(coef[:, :, :], keep[:, :, :], bc(rden[:, :]), ALU.mult))
                then(nc.vector.tensor_scalar(ks[:, :, :], sums[:, :, :], 1e-30, float(NBR), ALU.max, ALU.mult))
                then(nc.vector.reciprocal(ks[:, :, :], ks[:, :, :]))
                then(nc.vector.tensor_tensor(keep[:, :, :], ks[:, :, :], bc(isz[:, :]), ALU.mult))
                then(nc.vector.tensor_tensor(keep[:, :, :], keep[:, :, :], cover, ALU.mult))
                then(nc.vector.tensor_tensor(coef[:, :, :], coef[:, :, :], keep[:, :, :], ALU.add))
                c4 = lambda r: coef[:, r, :].rearrange("p (n o) -> p n o", o=1).to_broadcast([P, T * H0, 4])
                for t in range(T):
                    s = slice(t * H0, (t + 1) * H0)
                    c4 = lambda r: coef[:, r, s].rearrange("p (n o) -> p n o", o=1).to_broadcast([P, H0, 4])
                    then(nc.vector.tensor_tensor(cfa[:, s, :], class2, c4(1), ALU.mult))
                    then(nc.vector.tensor_tensor(cfb[:, s, :], class4, c4(2), ALU.mult))
                    then(nc.vector.tensor_tensor(cfa[:, s, :], cfa[:, s, :], cfb[:, s, :], ALU.add))
                    ins = nc.vector.tensor_tensor(cfa[:, s, :], cfa[:, s, :], c4(0), ALU.add)
                    if t == 0:
                        then(ins)
                ins.then_inc(coef_ready.sem, 1)
                dve.wait_ge(coef_ready.sem, coef_ready.at(b, 1))
                for g in range(H0 // HG):
                    for t, e in ((0, e0a), (1, e0b)):
                        if t == 1 and g > 0:
                            continue
                        v = e[:, g * HG:(g + 1) * HG, :].rearrange("p h (k c) -> p h k c", c=4)
                        cf = cfa[:, t * H0 + g * HG:t * H0 + (g + 1) * HG, :]
                        nc.vector.tensor_tensor(v, v, cf.rearrange("p h (o c) -> p h o c", o=1).to_broadcast([P, HG, (t + 1) * P // 4, 4]),
                                                ALU.mult).then_inc(weighed_d.sem, 1)
                for i in range(1, 12, 2):
                    g, seg = i // 3, i % 3
                    if g >= 2:
                        dve.wait_ge(av0_used.sem, av0_used.at(b, g - 1))
                    dst = pT0b[:, g % 2] if seg == 2 else pT0a[:, g % 2, :, seg * P:(seg + 1) * P]
                    copy_turned(dst)
                src = prodd.take()
                nc.vector.tensor_copy(avT0[:, :, :], src[:, :].rearrange("p (k n) -> p k n", k=KD)).then_inc(pd.empty.sem, 1)
                src = prodd.take()
                dve.wait_ge(stored.sem, stored.at(b, 0))
                release(nc.vector.tensor_tensor(x1[:, :, :], src[:, :].rearrange("p (t n) -> p t n", t=T), xb[:, :, :], ALU.add), prodd)
                norm(x1, xn, normed)
                choose(E0N, 1e-9)
                io = c("iota")
                for t in range(T):
                    then(nc.vector.tensor_scalar(comb[:, t, :], io, idxf[:, t, 0:1], wtop[:, t, 0:1], ALU.is_equal, ALU.mult))
                    then(nc.vector.tensor_scalar(comb2[:, t, :], io, idxf[:, t, 1:2], wtop[:, t, 1:2], ALU.is_equal, ALU.mult))
                nc.vector.tensor_tensor(comb[:, :, :], comb[:, :, :], comb2[:, :, :], ALU.add).then_inc(comb_ready.sem, 1)
                for i in range(6):
                    t, (f0, fn) = i // 3, CH0[i % 3]
                    src = prodd.take()
                    dve.wait_ge(pa.empty.sem, pa.empty.at(b, PA_G + i))
                    nc.vector.tensor_tensor(hid[:, t, f0:f0 + fn], src[:, 0:fn], hs[:, i % 2, 0:fn], ALU.mult).then_inc(pd.empty.sem, 1)
                for i in range(0, 6, 2):
                    t, (f0, fn) = i // 3, CH0[i % 3]
                    copy_turned(hidT[:, f0 // P:(f0 + fn) // P, t * P:(t + 1) * P], fn)
                src = prodd.take()
                release(nc.vector.tensor_tensor(x1[:, :, :], src[:, :].rearrange("p (t n) -> p t n", t=T), x1[:, :, :], ALU.add), prodd)
                norm(x1, xn)
                norm(xn, xn, normed)
                nc.vector.tensor_tensor(xb[:, :, :], x1[:, :, :], gbo1[:, :].rearrange("p (o n) -> p o n", o=1).to_broadcast([P, T, D]), ALU.add)
                for _k in range(2):
                    src = prodd.take()
                    nc.vector.tensor_scalar(qT1[:, 4 * _k + 2:4 * _k + 4, :], src[:, :].rearrange("p (m n) -> p m n", m=2),
                                            DH1 ** -0.5, None, ALU.mult).then_inc(pd.empty.sem, 1)

                def av1(pair):
                    src = prodd.take()
                    nc.vector.tensor_copy(avT1[:, pair, :], src[:, 0:L]).then_inc(pd.empty.sem, 1)

                for i in range(I1T * T + 5):
                    if i < I1T * T:
                        src = score.take()
                        if i >= 4:
                            dve.wait_ge(sc.empty.sem, sc.empty.at(b, N_S0 + i - 3))
                        nc.vector.tensor_reduce(negm1[:, i % 4, :], src[:, :].rearrange("p (h n) -> p h n", h=2), AX.X, ALU.max,
                                                negate=True).then_inc(maxed.sem, 1)
                    if 1 <= i <= I1T * T:
                        j = i - 1
                        dve.wait_ge(sc.empty.sem, sc.empty.at(b, N_S0 + j + 1))
                        if j >= 4:
                            dve.wait_ge(p1_ready.sem, p1_ready.at(b, j - 3))
                        nc.vector.reciprocal(r1[:, j % 4, :], z1[:, j % 4, :]).then_inc(recip1.sem, 1)
                    if i >= 3 and i % 2 == 1 and i - 2 < I1T * T:
                        j = i - 2
                        pair = j // 2
                        if pair >= 2:
                            dve.wait_ge(pd.full.sem, pd.full.at(b, PD_AV1 + pair - 2))
                        copy_turned(pT1[:, pair % 2, :, :, (j % 2) * P:(j % 2 + 1) * P])
                    if i >= 5 and i % 2 == 1 and (i - 5) // 2 < I1T:
                        av1((i - 5) // 2)
                if prodd.n < PD_O1 - 1:
                    av1(I1T - 1)
                src = prodd.take()
                release(nc.vector.scalar_tensor_tensor(out=x1[:, :, :], in0=src[:, :].rearrange("p (t n) -> p t n", t=T), scalar=tgate[:, 0:1],
                                                       in1=xb[:, :, :], op0=ALU.mult, op1=ALU.add), prodd)
                dve.wait_ge(scattered.sem, scattered.at(b, 0))
                norm(x1, pay[:, :, 0, 0:D], normed)
                nc.vector.tensor_scalar(pay[:, 0, 1, 0:D], x1[:, 0, :], mv[:, 0, 0:1], rstd[:, 0:1], ALU.subtract, ALU.mult)
                nc.vector.tensor_scalar(pay[:, 1, 1, 0:D], x1[:, 1, :], mv[:, 1, 0:1], rstd[:, 1:2], ALU.subtract, ALU.mult)
                choose(E1N, 0.0)
                for t in range(T):
                    for k in range(TOP):
                        then(nc.vector.tensor_scalar(hot[:, t, k, :], io[:, 0:E1N], idxf[:, t, k:k + 1], None, ALU.is_equal))
                nc.vector.tensor_tensor(both[:, :, :], hot[:, :, 0, :], hot[:, :, 1, :], ALU.add).then_inc(both_ready.sem, 1)
                payi = pay[:, :, :, :].bitcast(I32)
                for k in range(TOP):
                    nc.vector.tensor_copy(pay[:, :, k, D], wtop[:, :, k])
                    then(nc.vector.tensor_copy(payi[:, :, k, D + 1], tok[:, :]))
                then(nc.vector.tensor_scalar(tok[:, :], tok[:, :], L, None, ALU.add))
                src = prodd.take()
                then(nc.vector.tensor_tensor(rank[:, :, :], src[:, 0:T * E1N].rearrange("p (t e) -> p t e", t=T),
                                             run[:, :].rearrange("p (o e) -> p o e", o=1).to_broadcast([P, T, E1N]), ALU.add))
                release(nc.vector.tensor_tensor(run[:, :], src[:, T * E1N:(T + 1) * E1N], run[:, :], ALU.add), prodd)
                for k in range(TOP):
                    then(nc.vector.tensor_tensor(hotr[:, :, k, :], hot[:, :, k, :], rank[:, :, :], ALU.mult))
                then(nc.vector.tensor_reduce(posf[:, :, :], hotr[:, :, :, :], AX.X, ALU.add))
                nc.vector.tensor_copy(pos[:, :, :], posf[:, :, :]).then_inc(pos_ready.sem, 1)
                assert (trd.n, prodd.n, score.n) == (N_TD, N_PD, N_S), (trd.n, prodd.n, score.n)
                assert n_step[0] == N_STEP, n_step
            nc.vector.tensor_tensor(counts_sb[:, :], run[:, :], c("region"), ALU.subtract).then_inc(setup_dve, 1)
            dve.wait_ge(setup_dve, 3)

        @block.tensor
        def _(pe):
            prime(pe, "pe")
            pe.wait_ge(c_loaded, 32)
            pe.wait_ge(w_loaded, 16)
            pe.wait_ge(pads, 3)
            mm = nc.tensor.matmul
            with pe.Fori(0, B) as b:
                tra, trd, prodd, proda, score = (Turn(pe, r, b) for r in (ta, td, pd, pa, sc))

                def turn(ring, tiles):
                    dst = ring.claim()
                    for i, src in enumerate(tiles):
                        ins = nc.tensor.transpose(dst[:, i * P:(i + 1) * P], src, ident)
                    ins.then_inc(ring.ring.full.sem, 1)

                def features_out(ring, wk, xT, ms):
                    dst = ring.claim()
                    for i, m in enumerate(ms):
                        for k in range(KD):
                            ins = mm(dst[:, i * L:(i + 1) * L], wk[:, k, m * P:(m + 1) * P], xT[:, k, :], start=(k == 0), stop=(k == KD - 1))
                    ins.then_inc(ring.ring.full.sem, 1)

                def tokens_out(ring, xT, wk, nk, n, ts=range(T), c0=0):
                    dst = ring.claim()
                    for i, t in enumerate(ts):
                        for k in range(nk):
                            ins = mm(dst[:, i * n:(i + 1) * n], xT[:, k, t * P:(t + 1) * P], wk[:, k, c0:c0 + n], start=(k == 0), stop=(k == nk - 1))
                    ins.then_inc(ring.ring.full.sem, 1)

                pe.wait_ge(ctx_loaded.sem, ctx_loaded.at(b, 16))
                features_out(prodd, wk0, ctx_in, (0, 1))
                tokens_out(prodd, ctx_in, wv0, KD, D)
                pe.wait_ge(normed.sem, normed.at(b, 1))
                turn(tra, [xn[:, t, k * P:(k + 1) * P] for k in range(KD) for t in range(T)])
                pe.wait_ge(ta.empty.sem, ta.empty.at(b, TA_XN0))
                features_out(prodd, wq0, xnT, (0, 1))
                pe.wait_ge(pd.empty.sem, pd.empty.at(b, PD_Q0))
                for i in range(N_S0):
                    t, nh = (0, HG) if i < H0 // HG else (1, 2)
                    h0 = i * HG if t == 0 else (i - H0 // HG) * 2
                    k = h0 // G0
                    pe.wait_ge(kpadded.sem, kpadded.at(b, k + 1))
                    dst = score.claim()
                    n = (t + 1) * P
                    v = dst[:, :].rearrange("p (h n) -> p h n", h=nh)
                    mm(v, qT0[:, k, t * P:(t + 1) * P], kpad0[:, h0:h0 + nh, 0:n], start=True, stop=True)
                    for h in range(nh):
                        ins = mm(v[:, h, t * P:(t + 1) * P], identb, causal, start=False, stop=True, skip_group_check=True)
                    ins.then_inc(sc.full.sem, 1)
                for m in range(4):
                    features_out((proda, prodd)[m % 2], wk1, ctx_in, (2 * m, 2 * m + 1))

                def turn_p0(g):
                    pe.wait_ge(weighed_d.sem, weighed_d.at(b, g + 1 + (g > 0) if g else 2))
                    if g:
                        pe.wait_ge(weighed_p.sem, weighed_p.at(b, g))
                    hh = range(g * HG, (g + 1) * HG)
                    for seg in range(3):
                        src = e0a if seg == 0 else e0b
                        k0 = P if seg == 2 else 0
                        turn((tra, trd)[(g * 3 + seg) % 2], [src[:, h, k0:k0 + P] for h in hh])

                def av_p0(g, dst):
                    last = 3 * g + 2
                    for i in (last - 1, last):
                        r, n = (ta, TA_P0 + i // 2) if i % 2 == 0 else (td, TD_P0 + i // 2)
                        pe.wait_ge(r.empty.sem, r.empty.at(b, n))
                    k = g // 2
                    for i in range(HG):
                        h = g * HG + i
                        mm(dst[:, k * L:(k + 1) * L], vpad0[:, 0, h, :], pT0a[:, g % 2, i, :], start=(h % G0 == 0), stop=(h % G0 == G0 - 1), skip_group_check=True)
                        ins = mm(dst[:, k * L + P:(k + 1) * L], vpad0[:, 1, h, :], pT0b[:, g % 2, i, :], start=False, stop=(h % G0 == G0 - 1), skip_group_check=True)
                    if g < 3:
                        ins.then_inc(av0_used.sem, 1)
                    else:
                        ins.then_inc(pd.full.sem, 1)

                turn_p0(0)
                turn_p0(1)
                dst = prodd.claim()
                av_p0(0, dst)
                turn_p0(2)
                av_p0(1, dst)
                turn_p0(3)
                av_p0(2, dst)
                av_p0(3, dst)
                pe.wait_ge(pd.empty.sem, pd.empty.at(b, PD_AV0))
                tokens_out(prodd, avT0, wo0, KD, D)
                for i in range(4):
                    t, half = i // 2, i % 2
                    tokens_out(proda, ctx_in, wv1, KD, 512, ts=(t,), c0=half * 512)
                pe.wait_ge(normed.sem, normed.at(b, 2))
                turn(tra, [xn[:, t, k * P:(k + 1) * P] for k in range(KD) for t in range(T)])
                pe.wait_ge(ta.empty.sem, ta.empty.at(b, TA_X1))
                tokens_out(prodd, xnT, router, KD, E0N)
                for i in range(6):
                    t, (f0, fn) = i // 3, CH0[i % 3]
                    tokens_out(proda, xnT, wg0, KD, fn, ts=(t,), c0=f0)
                    tokens_out(prodd, xnT, wu0, KD, fn, ts=(t,), c0=f0)
                for i in range(6):
                    t, (f0, fn) = i // 3, CH0[i % 3]
                    if i % 3 < 2:
                        pe.wait_ge(hid_weighed.sem, hid_weighed.at(b, 2 * t + i % 3 + 1))
                    else:
                        pe.wait_ge(pd.empty.sem, pd.empty.at(b, PD_U + i))
                    turn((trd, tra)[i % 2], [hid[:, t, f0 + j * P:f0 + (j + 1) * P] for j in range(fn // P)])
                pe.wait_ge(ta.empty.sem, ta.empty.at(b, TA_H + 2))
                pe.wait_ge(td.empty.sem, td.empty.at(b, TD_H + 2))
                tokens_out(prodd, hidT, wd0, F0T, D)
                pe.wait_ge(normed.sem, normed.at(b, 3))
                turn(tra, [xn[:, t, k * P:(k + 1) * P] for k in range(KD) for t in range(T)])
                pe.wait_ge(ta.empty.sem, ta.empty.at(b, TA_X2))
                for m in range(4):
                    features_out((proda, prodd)[m % 2], wq1, xnT, (2 * m, 2 * m + 1))
                pe.wait_ge(pa.empty.sem, pa.empty.at(b, PA_Q1 + 1))
                pe.wait_ge(pd.empty.sem, pd.empty.at(b, PD_Q1 + 1))

                def av_p1(pair):
                    for r, n in ((ta, TA_P1 + pair), (td, TD_P1 + pair)):
                        pe.wait_ge(r.empty.sem, r.empty.at(b, n))
                    dst = prodd.claim()
                    for e in range(2):
                        for k in range(T):
                            ins = mm(dst[:, 0:L], vpad1[:, k, 2 * pair + e, :], pT1[:, pair % 2, k, e, :],
                                     start=(e == 0 and k == 0), stop=(e == 1 and k == T - 1))
                    ins.then_inc(pd.full.sem, 1)

                for i in range(I1T * T + 4):
                    if i < I1T * T:
                        pair, t = i // 2, i % 2
                        dst = score.claim()
                        mm(dst[:, :], qT1[:, pair, t * P:(t + 1) * P], kpad1[:, 2 * pair:2 * pair + 2, :], start=True, stop=True).then_inc(sc.full.sem, 1)
                    if 2 <= i < I1T * T + 2:
                        j = i - 2
                        pe.wait_ge(p1_ready.sem, p1_ready.at(b, j + 1))
                        turn((tra, trd)[j % 2], [p1[:, j % 4, e, k * P:(k + 1) * P] for k in range(T) for e in range(2)])
                    if i >= 4 and i % 2 == 0:
                        av_p1((i - 4) // 2)
                if prodd.n < PD_O1 - 1:
                    av_p1(I1T - 1)
                pe.wait_ge(pd.empty.sem, pd.empty.at(b, PD_AV1 + 7))
                tokens_out(prodd, avT1, wo1, I1T, D)
                pe.wait_ge(normed.sem, normed.at(b, 4))
                turn(tra, [pay[:, t, 0, k * P:(k + 1) * P] for k in range(KD) for t in range(T)])
                pe.wait_ge(ta.empty.sem, ta.empty.at(b, TA_X3))
                tokens_out(prodd, xnT, gate1, KD, E1N)
                pe.wait_ge(both_ready.sem, both_ready.at(b, 1))
                dst = prodd.claim()
                mm(dst[:, 0:E1N], below, both[:, 0, :], start=True, stop=True)
                mm(dst[:, E1N:2 * E1N], below, both[:, 1, :], start=True, stop=False)
                mm(dst[:, E1N:2 * E1N], onesb, both[:, 0, :], start=False, stop=True)
                mm(dst[:, 2 * E1N:3 * E1N], onesb, both[:, 0, :], start=True, stop=False)
                mm(dst[:, 2 * E1N:3 * E1N], onesb, both[:, 1, :], start=False, stop=True).then_inc(pd.full.sem, 1)
                assert (tra.n, trd.n, prodd.n, proda.n, score.n) == (N_TA, N_TD, N_PD, N_PA, N_S)


def experts(nc, cst, counts_sb, pad_ids, we1, rows, acc, out):
    with ExitStack() as ctx:
        def sb(name, shape, dt=F32):
            return ctx.enter_context(nc.sbuf_tensor(name, shape, dt))

        def sem(name):
            return ctx.enter_context(nc.semaphore(name))

        def bank(name):
            return ctx.enter_context(nc.psum_tensor(name, [P, 512], F32))

        def c(name):
            return cst[:, C_F32[name][0]:sum(C_F32[name])]

        N = NBLK + 1
        ident = c("ident")
        wts = sb("wts_e", [P, SLOTS * WE1])
        pad = sb("pad", [P, ROW])
        xs = sb("xs", [P, ROW])
        xT = sb("xT", [P, KD, P])
        hs = sb("hs_e", [P, 2, 512])
        hid = sb("hid_e", [P, F1])
        hidT = sb("hidT_e", [P, F1T, P])
        y = sb("y", [P, D])
        wt_next, wt_now = sb("wt_next", [P, 1]), sb("wt_now", [P, 1])
        id_next, id_now = sb("id_next", [P, 1], I32), sb("id_now", [P, 1], I32)
        fl, nb, cum, prior = (sb(n, [P, E1N]) for n in ("fl", "nb", "cum", "prior"))
        cnt_i = sb("cnt_i", [P, E1N], I32)
        tail_i = sb("tail_i", [P, E1N], I32)
        cum_i = sb("cum_i", [P, E1N], I32)
        le = sb("le", [P, N, E1N])
        le2 = sb("le2", [P, N, E1N])
        eid, rowf, tmp, slotf = (sb(n, [P, N]) for n in ("eid", "rowf", "tmp", "slotf"))
        needf = sb("needf", [P, SLOTS, N])
        row_i, slot_i = sb("row_i", [P, N], I32), sb("slot_i", [P, N], I32)
        need_i = sb("need_i", [P, SLOTS, N], I32)

        turn_a, turn_d, acc_bank = bank("turn_a2"), bank("turn_d2"), bank("acc_bank")
        prod_d = [bank(f"prod_d2{i}") for i in range(2)]
        prod_a = [bank(f"prod_a2{i}") for i in range(2)]
        signals = {}

        def signal(name, per, owner):
            s = Signal(sem(name), per)
            signals.setdefault(owner, []).append(s)
            return s

        pd = Ring(prod_d, signal("up_full", 2, "pe"), signal("up_empty", 2, "dve"))
        pa = Ring(prod_a, signal("gate_full", 2, "pe"), signal("gate_empty", 2, "act"))
        ta = Ring([turn_a], Signal(sem("turn_a2_full"), 2), Signal(sem("turn_a2_empty"), 2))
        td = Ring([turn_d], signal("turn_d2_full", 1, "pe"), signal("turn_d2_empty", 1, "dve"))
        ya = Ring([acc_bank], signal("y_full", 1, "pe"), signal("y_empty", 1, "dve"))
        xs_loaded = Signal(sem("xs_loaded"), 16)
        added = Signal(sem("added"), 16)
        meta = Signal(sem("meta"), 1)
        moved = signal("moved", 1, "dve")
        slot_loaded = [sem(f"slot_loaded{i}") for i in range(SLOTS)]
        tables, tails, chain, copied = (sem(n) for n in ("tables", "tails", "chain", "copied"))
        spare = sem("spare2")

        def prime(eng, owner):
            for s in signals[owner]:
                eng.sem_inc(s.sem, s.per)

        block = ctx.enter_context(nc.Block())

        @block.sync
        def _(sp):
            for s in slot_loaded:
                sp.sem_inc(s, 16)
            for e in range(SLOTS):
                sp.dma_start(wts[:, e * WE1:(e + 1) * WE1], we1[e]).then_inc(slot_loaded[e], 16)
            sp.wait_ge(added.sem, 16)
            sp.wait_ge(tables, 1)
            for e in range(E1N):
                at = sp.value_load(tail_i[0:1, e:e + 1], min_val=0, max_val=E1N * CAP - P)
                sp.dma_start(rows[bass.ds(at, P), :], pad[:, :]).then_inc(tails, 16)
            sp.dma_start(rows[E1N * CAP:, :], pad[:, :]).then_inc(tails, 16)
            sp.dma_start(acc[NTOK:, :], pad[:, 0:D]).then_inc(tails, 16)
            for e in range(SLOTS, E1N):
                done = sp.value_load(cum_i[0:1, e - SLOTS:e - SLOTS + 1], min_val=0, max_val=NBLK)
                sp.wait_ge(ya.full.sem, done + 1)
                sp.dma_start(wts[:, (e % SLOTS) * WE1:(e % SLOTS + 1) * WE1], we1[e]).then_inc(slot_loaded[e % SLOTS], 16)
            sp.wait_ge(added.sem, 16 * (NBLK + 1))
            sp.dma_start(out.rearrange("b t d -> (b t) d"), acc[0:NTOK, :]).then_inc(copied, 16)
            sp.wait_ge(copied, 16)

        @block.gpsimd
        def _(pool):
            pool.dma_start(pad[:, :], pad_ids).then_inc(added.sem, 16)
            pool.wait_ge(tables, 1)
            pool.wait_ge(tails, 16 * (E1N + 2))
            at = pool.value_load(row_i[0:1, 0:1], min_val=0, max_val=E1N * CAP)
            pool.dma_start(xs[:, :], rows[bass.ds(at, P), :]).then_inc(xs_loaded.sem, 16)
            with pool.Fori(0, NBLK) as j:
                pool.wait_ge(meta.sem, meta.at(j, 0))
                pool.wait_ge(ta.full.sem, ta.full.at(j, -1))
                at = pool.value_load(row_i[0:1, bass.ds(j + 1, 1)], min_val=0, max_val=E1N * CAP)
                pool.dma_start(xs[:, :], rows[bass.ds(at, P), :]).then_inc(xs_loaded.sem, 16)
                pool.wait_ge(ya.empty.sem, ya.empty.at(j, 1))
                pool.sem_inc(spare, 1)
                pool.indirect_dma_start(acc, bass.IndirectOffsetOnAxis(ap=id_now[:, 0:1], axis=0), y[:, :], None,
                                        compute_op=ALU.add).then_inc(added.sem, 16)
            pool.wait_ge(added.sem, 16 * (NBLK + 1))

        @block.scalar
        def _(act):
            prime(act, "act")
            act.wait_ge(ta.full.sem, 2)
            nc.scalar.activation(xT[:, :, :], turn_a[:, 0:KD * P].rearrange("p (k n) -> p k n", k=KD), ACT.Copy).then_inc(ta.empty.sem, 2)
            with act.Fori(0, NBLK) as j:
                tra, proda = Turn(act, ta, j), Turn(act, pa, j)
                for i in range(2):
                    src = proda.take()
                    act.wait_ge(pd.empty.sem, pd.empty.at(j, i + 1 - 2))
                    nc.scalar.activation(hs[:, i, :], src[:, :], ACT.Silu).then_inc(pa.empty.sem, 1)
                src = tra.take()
                nc.scalar.activation(xT[:, :, :], src[:, 0:KD * P].rearrange("p (k n) -> p k n", k=KD), ACT.Copy).then_inc(ta.empty.sem, 1)
                src = tra.take()
                nc.scalar.activation(hidT[:, 4:8, :], src[:, :].rearrange("p (f n) -> p f n", n=P), ACT.Copy).then_inc(ta.empty.sem, 1)

        @block.vector
        def _(dve):
            prime(dve, "dve")
            n = [0]

            def then(ins):
                n[0] += 1
                ins.then_inc(chain, 1)
                dve.wait_ge(chain, n[0])

            then(nc.vector.tensor_scalar(fl[:, :], counts_sb[:, :], float(P - 1), None, ALU.add))
            then(nc.vector.tensor_copy(cnt_i[:, :], fl[:, :]))
            then(nc.vector.tensor_single_scalar(cnt_i[:, :], cnt_i[:, :], 7, ALU.arith_shift_right))
            then(nc.vector.tensor_copy(nb[:, :], cnt_i[:, :]))
            then(nc.vector.tensor_copy(cum[:, :], nb[:, :]))
            for e in range(1, E1N):
                then(nc.vector.tensor_tensor(cum[:, e:e + 1], cum[:, e - 1:e], nb[:, e:e + 1], ALU.add))
            then(nc.vector.tensor_copy(cum_i[:, :], cum[:, :]))
            then(nc.vector.tensor_tensor(fl[:, :], counts_sb[:, :], c("region"), ALU.add))
            then(nc.vector.tensor_copy(tail_i[:, :], fl[:, :]))
            row = lambda ap: ap.rearrange("p (o e) -> p o e", o=1).to_broadcast([P, N, E1N])
            then(nc.vector.tensor_tensor(le[:, :, :], row(cum[:, :]), c("blocks").rearrange("p (n o) -> p n o", o=1).to_broadcast([P, N, E1N]), ALU.is_le))
            then(nc.vector.tensor_tensor(le2[:, :, :], le[:, :, :], row(nb[:, :]), ALU.mult))
            then(nc.vector.tensor_reduce(eid[:, :], le[:, :, :], AX.X, ALU.add))
            then(nc.vector.tensor_reduce(tmp[:, :], le2[:, :, :], AX.X, ALU.add))
            then(nc.vector.tensor_tensor(tmp[:, :], c("blocks"), tmp[:, :], ALU.subtract))
            then(nc.vector.tensor_scalar(tmp[:, :], tmp[:, :], float(P), None, ALU.mult))
            then(nc.vector.tensor_scalar(rowf[:, :], eid[:, :], float(CAP), None, ALU.mult))
            then(nc.vector.tensor_tensor(rowf[:, :], rowf[:, :], tmp[:, :], ALU.add))
            then(nc.vector.tensor_scalar(rowf[:, :], rowf[:, :], float(E1N * CAP), None, ALU.min))
            then(nc.vector.tensor_copy(row_i[:, :], rowf[:, :]))
            then(nc.vector.tensor_scalar(eid[:, :], eid[:, :], float(E1N - 1), None, ALU.min))
            then(nc.vector.tensor_copy(slotf[:, :], eid[:, :]))
            for e in range(SLOTS, E1N, SLOTS):
                then(nc.vector.tensor_scalar(tmp[:, :], eid[:, :], float(e), float(-SLOTS), ALU.is_ge, ALU.mult))
                then(nc.vector.tensor_tensor(slotf[:, :], slotf[:, :], tmp[:, :], ALU.add))
            then(nc.vector.tensor_copy(slot_i[:, :], slotf[:, :]))
            for s in range(SLOTS):
                then(nc.vector.tensor_scalar(needf[:, s, :], eid[:, :], 0.0, 16.0, ALU.mult, ALU.add))
                for e in range(s, E1N, SLOTS):
                    then(nc.vector.tensor_scalar(tmp[:, :], eid[:, :], float(e), 16.0, ALU.is_ge, ALU.mult))
                    then(nc.vector.tensor_tensor(needf[:, s, :], needf[:, s, :], tmp[:, :], ALU.add))
            nc.vector.tensor_copy(need_i[:, :, :], needf[:, :, :]).then_inc(tables, 1)
            dve.wait_ge(xs_loaded.sem, 16)
            then(nc.vector.tensor_copy(wt_next[:, :], xs[:, D:D + 1]))
            nc.vector.tensor_copy(id_next[:, :], xs[:, D + 1:D + 2].bitcast(I32)).then_inc(meta.sem, 1)
            with dve.Fori(0, NBLK) as j:
                trd, prodd, acc_t = Turn(dve, td, j), Turn(dve, pd, j), Turn(dve, ya, j)
                for i in range(2):
                    src = prodd.take()
                    dve.wait_ge(pa.empty.sem, pa.empty.at(j, i + 1))
                    nc.vector.tensor_tensor(hid[:, i * 512:(i + 1) * 512], src[:, :], hs[:, i, :], ALU.mult).then_inc(pd.empty.sem, 1)
                dve.wait_ge(added.sem, added.at(j, 0))
                dve.wait_ge(meta.sem, meta.at(j, 0))
                nc.vector.tensor_copy(wt_now[:, :], wt_next[:, :])
                nc.vector.tensor_copy(id_now[:, :], id_next[:, :]).then_inc(moved.sem, 1)
                dve.wait_ge(moved.sem, moved.at(j, 1))
                dve.wait_ge(xs_loaded.sem, xs_loaded.at(j, 16))
                nc.vector.tensor_copy(wt_next[:, :], xs[:, D:D + 1])
                nc.vector.tensor_copy(id_next[:, :], xs[:, D + 1:D + 2].bitcast(I32)).then_inc(meta.sem, 1)
                src = trd.take()
                nc.vector.tensor_copy(hidT[:, 0:4, :], src[:, :].rearrange("p (f n) -> p f n", n=P)).then_inc(td.empty.sem, 1)
                src = acc_t.take()
                nc.vector.tensor_scalar(y[:, :], src[:, 0:D], wt_now[:, 0:1], None, ALU.mult).then_inc(ya.empty.sem, 1)

        @block.tensor
        def _(pe):
            prime(pe, "pe")
            mm = nc.tensor.matmul
            pe.wait_ge(xs_loaded.sem, 16)
            for k in range(KD):
                ins = nc.tensor.transpose(turn_a[:, k * P:(k + 1) * P], xs[:, k * P:(k + 1) * P], ident)
            ins.then_inc(ta.full.sem, 2)
            with pe.Fori(0, NBLK) as j:
                tra, trd, prodd, proda, acc_t = (Turn(pe, r, j) for r in (ta, td, pd, pa, ya))
                for s in range(SLOTS):
                    need = pe.value_load(need_i[0:1, s, bass.ds(j, 1)], min_val=16, max_val=16 * E1N)
                    pe.wait_ge(slot_loaded[s], need)
                slot = pe.value_load(slot_i[0:1, bass.ds(j, 1)], min_val=0, max_val=SLOTS - 1)
                base = slot * WE1

                def half(ring, which, i):
                    dst = ring.claim()
                    for k in range(KD):
                        ins = mm(dst[:, :], xT[:, k, :], wts[:, bass.ds(base + (which * KD + k) * F1 + i * 512, 512)], start=(k == 0), stop=(k == KD - 1))
                    ins.then_inc(ring.ring.full.sem, 1)

                pe.wait_ge(ta.empty.sem, ta.empty.at(j, -1))
                for i in range(2):
                    half(proda, 0, i)
                    half(prodd, 1, i)
                dst = tra.claim()
                pe.wait_ge(xs_loaded.sem, xs_loaded.at(j, 16))
                for k in range(KD):
                    ins = nc.tensor.transpose(dst[:, k * P:(k + 1) * P], xs[:, k * P:(k + 1) * P], ident)
                ins.then_inc(ta.full.sem, 1)

                def down(f0, dst):
                    for f in range(f0, f0 + 4):
                        ins = mm(dst[:, 0:D], hidT[:, f, :], wts[:, bass.ds(base + 2 * KD * F1 + f * D, D)], start=(f == 0), stop=(f == F1T - 1))
                    return ins

                dst = trd.claim()
                pe.wait_ge(pd.empty.sem, pd.empty.at(j, 1))
                for f in range(4):
                    ins = nc.tensor.transpose(dst[:, f * P:(f + 1) * P], hid[:, f * P:(f + 1) * P], ident)
                ins.then_inc(td.full.sem, 1)
                dst = tra.claim()
                pe.wait_ge(pd.empty.sem, pd.empty.at(j, 2))
                for f in range(4):
                    ins = nc.tensor.transpose(dst[:, f * P:(f + 1) * P], hid[:, (f + 4) * P:(f + 5) * P], ident)
                ins.then_inc(ta.full.sem, 1)
                dst = acc_t.claim()
                pe.wait_ge(td.empty.sem, td.empty.at(j, 1))
                down(0, dst)
                pe.wait_ge(ta.empty.sem, ta.empty.at(j, 2))
                down(4, dst).then_inc(ya.full.sem, 1)


def build(nc, cf32, cb16, w32, tok0, pad_ids, x, ctxT, we1, out):
    acc = nc.dram_tensor("acc", [NTOK + P, D], F32, kind="Internal").ap()
    rows = nc.dram_tensor("rows", [E1N * CAP + P, ROW], F32, kind="Internal").ap()
    with ExitStack() as ctx:
        cst = ctx.enter_context(nc.sbuf_tensor("cst", [P, NC32], F32))
        counts_sb = ctx.enter_context(nc.sbuf_tensor("counts_sb", [P, E1N], F32))
        layers(nc, cst, counts_sb, cf32, cb16, w32, tok0, x, ctxT,
               acc[0:NTOK, :].rearrange("(b l) d -> b l d", b=B), rows)
        experts(nc, cst, counts_sb, pad_ids, we1, rows, acc, out)


def kernel(**inputs):
    import numpy as np
    import ml_dtypes
    import concourse.bacc as bacc
    from concourse.bass_utils import run_bass_kernel_spmd as run_spmd

    f32 = np.float32
    a = {k: np.asarray(v) for k, v in inputs.items()}

    p = np.arange(P)
    cf = np.zeros((P, NC32), f32)

    def put(table, dst, name, value):
        at, n = table[name]
        dst[:, at:at + n] = np.reshape(value, (-1, n)) if np.ndim(value) else value

    heads = np.arange(H0)
    put(C_F32, cf, "ident", np.eye(P, dtype=f32))
    put(C_F32, cf, "head", p[:, None] // DH0 == np.arange(G0)[None])
    cover = np.zeros((P, NBR, T, H0), f32)
    for r, dil in enumerate((1, 2, 4)):
        cover[:, r] = (p[:, None] % dil == heads[None] // (H0 // dil))[:, None]
    put(C_F32, cf, "cover", cover)
    for name, dil in (("class2", 2), ("class4", 4)):
        put(C_F32, cf, name, np.tile((np.arange(4)[None] % dil == heads[:, None] // (H0 // dil)).reshape(1, -1), (P, 1)))
    put(C_F32, cf, "iota", np.tile(np.arange(16), (P, 1)))
    put(C_F32, cf, "region", np.tile(np.arange(E1N) * CAP, (P, 1)))
    put(C_F32, cf, "neghalf", -0.5)
    put(C_F32, cf, "blocks", np.tile(np.arange(NBLK + 1), (P, 1)))
    cb = np.zeros((P, NCB), ml_dtypes.bfloat16)
    cb[:, 0:P] = np.eye(P)
    cb[:, P:2 * P] = np.where(p[None] <= p[:, None], 0.0, -1e30)
    cb[:, 2 * P:3 * P] = p[:, None] < p[None]
    cb[:, 3 * P:] = 1.0
    pad_ids = np.zeros((P, ROW), f32)
    pad_ids[:, D + 1] = (NTOK + p).astype(np.int32).view(f32)
    tok0 = (p[:, None] + P * np.arange(T)[None]).astype(np.int32)

    w = np.zeros((P, NW32), f32)
    tiles = lambda m: m.reshape(-1, P, m.shape[-1]).transpose(1, 0, 2).reshape(P, -1)
    wide = lambda r, s: np.concatenate([r.transpose(1, 0, 2).reshape(D, -1), s.transpose(1, 0, 2).reshape(D, -1)], 1)
    for name, key in (("wq0", "Wq"), ("wk0", "Wk"), ("wv0", "Wv"), ("wo0", "Wo")):
        put(W_F32, w, name, tiles(a["L0_xattn_" + key].T))
    put(W_F32, w, "router", tiles(a["L0_ffn_router_w"]))
    put(W_F32, w, "wg0", tiles(wide(a["L0_ffn_wg_r"], a["L0_ffn_wg_s"])))
    put(W_F32, w, "wu0", tiles(wide(a["L0_ffn_wu_r"], a["L0_ffn_wu_s"])))
    put(W_F32, w, "wd0", tiles(np.concatenate([a["L0_ffn_wd_r"].reshape(-1, D), a["L0_ffn_wd_s"].reshape(-1, D)])))
    put(W_F32, w, "wq1", tiles(a["L1_xattn_w_q"]))
    put(W_F32, w, "wk1", tiles(a["L1_xattn_w_kv"][:, :I1]))
    put(W_F32, w, "wv1", tiles(a["L1_xattn_w_kv"][:, I1:]))
    put(W_F32, w, "wo1", tiles(a["L1_xattn_w_out"]))
    put(W_F32, w, "gate1", tiles(a["L1_ffn_gate_w"]))
    for name, key in (("bq0", "L0_xattn_bq"), ("bk0", "L0_xattn_bk"), ("gamma", "L1_xattn_ln_gamma"), ("beta", "L1_xattn_ln_beta")):
        put(W_F32, w, name, a[key].reshape(KD, P).T)
    put(W_F32, w, "gate", np.tile(a["L1_xattn_gate"], (P, 1)))
    for name, key in (("bv0", "L0_xattn_bv"), ("bo0", "L0_xattn_bo"), ("bo1", "L1_xattn_b_out")):
        put(W_F32, w, name, np.tile(a[key], (P, 1)))
    we1 = np.concatenate([
        a["L1_ffn_w1"].reshape(E1N, KD, P, F1).transpose(0, 2, 1, 3).reshape(E1N, P, -1),
        a["L1_ffn_w3"].reshape(E1N, KD, P, F1).transpose(0, 2, 1, 3).reshape(E1N, P, -1),
        a["L1_ffn_w2"].reshape(E1N, F1T, P, D).transpose(0, 2, 1, 3).reshape(E1N, P, -1)], 2)
    ctxT = a["ctx_1024"].transpose(0, 2, 1)

    arrays = {"cf32": cf, "cb16": cb, "w32": w, "tok0": tok0, "pad_ids": pad_ids, "x": a["x"], "ctxT": ctxT, "we1": we1}
    arrays = {k: np.ascontiguousarray(v) for k, v in arrays.items()}
    nc = bacc.Bacc("TRN2", target_bir_lowering=False, num_devices=1)
    aps = {k: nc.dram_tensor(k + "_dram", v.shape, mybir.dt.from_np(v.dtype), kind="ExternalInput").ap() for k, v in arrays.items()}
    out = nc.dram_tensor("out_dram", (B, L, D), F32, kind="ExternalOutput").ap()
    build(nc, out=out, **aps)
    r = run_spmd(nc, [{k + "_dram": v for k, v in arrays.items()}], core_ids=[0])
    return r.results[0]["out_dram"]
```

```python
from contextlib import ExitStack

import concourse.bass as bass
import numpy as np
from concourse import mybir

F32 = mybir.dt.float32
BF16 = mybir.dt.bfloat16
I32 = mybir.dt.int32
U32 = mybir.dt.uint32
ALU = mybir.AluOpType
ACT = mybir.ActivationFunctionType
AX = mybir.AxisListType

P = 128
B, L, D = 8, 256, 256
T = L // P
KD = D // P
EPS = 1e-5

H0, DH0 = 16, 16
G0 = P // DH0
HG = 4
NBR = 3
E0N, M0R, M0S = 16, 64, 256
F0 = E0N * M0R + M0S
F0T = F0 // P
CH0 = [(0, 512), (512, 512), (1024, 256)]

H1, DH1 = 16, 64
I1 = H1 * DH1
I1T = I1 // P

E1N, F1 = 8, 1024
F1T = F1 // P
TOP = 2
NTOK = B * L
CAP = NTOK + P
ROW = D + 2
NBLK = (TOP * NTOK) // P + E1N - 1
WE1 = 2 * KD * F1 + F1T * D
STEPS = 3
assert NBLK % STEPS == 0

C_F32 = {}
W_F32 = {}


def columns(table, parts):
    at = 0
    for name, n in parts:
        table[name] = (at, n)
        at += n
    return at


NC32 = columns(C_F32, [("ident", P), ("head", G0), ("cover", NBR * T * H0), ("class2", H0 * 4), ("class4", H0 * 4),
                       ("iota", 16), ("region", E1N), ("neghalf", T), ("blocks", NBLK + 1), ("upto", E1N * E1N)])
NW32 = columns(W_F32, [("wq0", KD * D), ("wk0", KD * D), ("wv0", KD * D), ("wo0", KD * D),
                       ("router", KD * E0N), ("wg0", KD * F0), ("wu0", KD * F0), ("wd0", F0T * D),
                       ("wk1", KD * I1), ("wv1", KD * I1), ("wq1", KD * I1), ("wo1", I1T * D), ("gate1", KD * E1N),
                       ("bq0", KD), ("bk0", KD), ("gamma", KD), ("beta", KD), ("gate", 1),
                       ("bv0", D), ("bo0", D), ("bo1", D)])
NW_L0 = W_F32["router"][0]
NW_BIAS = W_F32["bq0"][0]
assert WE1 <= W_F32["wk1"][0] and 2 * WE1 <= W_F32["wq1"][0]
NCB = 4 * P


class Signal:

    def __init__(self, sem, per, start=None):
        self.sem, self.per, self.start = sem, per, per if start is None else start

    def at(self, turn, n):
        return turn * self.per + (self.start + n)


class Ring:

    def __init__(self, banks, full, empty):
        self.banks, self.full, self.empty = banks, full, empty


class Turn:

    def __init__(self, eng, ring, turn):
        self.eng, self.ring, self.turn, self.n = eng, ring, turn, 0

    def claim(self):
        self.n += 1
        before = self.ring.empty.at(self.turn, self.n - len(self.ring.banks))
        if not isinstance(before, int) or before > 0:
            self.eng.wait_ge(self.ring.empty.sem, before)
        return self.ring.banks[(self.n - 1) % len(self.ring.banks)]

    def take(self):
        self.n += 1
        self.eng.wait_ge(self.ring.full.sem, self.ring.full.at(self.turn, self.n))
        return self.ring.banks[(self.n - 1) % len(self.ring.banks)]

    def skip(self, signal, n):
        skip(self.eng, signal, self.turn, self.n, n)
        self.n += n


def skip(eng, signal, turn, done, n):
    before = signal.at(turn, done)
    if not isinstance(before, int) or before > 0:
        eng.wait_ge(signal.sem, before)
    eng.sem_inc(signal.sem, n)


PD_AV0, PD_O0, PD_K0, PD_V0, PD_ROUTER, PD_U, PD_DOWN, PD_Q1, PD_AV1, PD_Q0, PD_AV7, PD_O1, PD_LOGIT, PD_RANK = (
    1, 2, 3, 4, 5, 6, 12, 13, 15, 21, 23, 24, 25, 26)
N_S0 = H0 // HG + H0 // 2
N_S1 = I1T * T
N_S = N_S0 + N_S1
PA_K1, PA_G, PA_V1, PA_Q1, PA_S1 = 1, 7, 13, 15, 17
PA_S0 = PA_S1 + N_S1
TA_P0, TA_X1, TA_H, TA_X2, TA_X3 = 1, 7, 8, 11, 21
TD_P0, TD_H, TD_P1 = 1, 7, 10
N_PD, N_PA, N_TA, N_TD = 26, 44, 21, 17
N_STEP = 48
AHEAD_NORM, AHEAD_TURN = 7, 14
RANK_AFTER = 9


def ta_p1(j):
    return 12 + j // 2 + (j > AHEAD_TURN - 3)


def layers(nc, cst, wts, counts_sb, expert_loaded, cf32, cb16, w32, tok0, x, ctxT, we1, acc, rows):
    with ExitStack() as ctx:
        def sb(name, shape, dt=F32):
            return ctx.enter_context(nc.sbuf_tensor(name, shape, dt))

        def sem(name):
            return ctx.enter_context(nc.semaphore(name))

        def bank(name):
            return ctx.enter_context(nc.psum_tensor(name, [P, 512], F32))

        cbf = sb("cbf", [P, NCB], BF16)
        def c(name):
            return cst[:, C_F32[name][0]:sum(C_F32[name])]

        def w(name, k=1):
            ap = wts[:, W_F32[name][0]:sum(W_F32[name])]
            return ap.rearrange("p (k n) -> p k n", k=k) if k > 1 else ap

        ident = c("ident")
        identb, causal, below, onesb = (cbf[:, i * P:(i + 1) * P] for i in range(4))
        cover = c("cover").rearrange("p (r n) -> p r n", r=NBR)
        class2 = c("class2").rearrange("p (h c) -> p h c", c=4)
        class4 = c("class4").rearrange("p (h c) -> p h c", c=4)
        wq0, wk0, wv0, wo0 = (w(n, KD) for n in ("wq0", "wk0", "wv0", "wo0"))
        router, wg0, wu0, wd0 = w("router", KD), w("wg0", KD), w("wu0", KD), w("wd0", F0T)
        wq1, wk1, wv1, wo1, gate1 = w("wq1", KD), w("wk1", KD), w("wv1", KD), w("wo1", I1T), w("gate1", KD)
        bq0, bk0, gamma, beta = w("bq0"), w("bk0"), w("gamma"), w("beta")
        bv0, bo0, bo1 = w("bv0"), w("bo0"), w("bo1")

        at = [NW32]

        def part(*shape):
            n = int(np.prod(shape))
            at[0] += n
            assert at[0] <= E1N * WE1
            v = wts[:, at[0] - n:at[0]]
            if len(shape) == 1:
                return v
            names = "abc"[:len(shape)]
            return v.rearrange(f"p ({' '.join(names)}) -> p {' '.join(names)}", **dict(zip(names[1:], shape[1:])))

        x_in = sb("x_in", [P, T, D])
        ctx_in = part(KD, L)
        ctx0 = part(KD, L)
        xb = part(T, D)
        xn = part(T, D)
        xnT = part(KD, L)
        x1 = part(T, D)
        kT0 = part(KD, L)
        qT0 = part(KD, L)
        kpad0 = part(H0, L)
        vpad0 = part(T, H0, P)
        kpad1 = part(H1, L)
        vpad1 = part(T, H1, P)
        big = part(6144)
        e0a = big[:, 0:H0 * P].rearrange("p (h k) -> p h k", h=H0)
        e0b = big[:, H0 * P:3 * H0 * P].rearrange("p (h k) -> p h k", h=H0)
        hid = big[:, 0:T * F0].rearrange("p (t f) -> p t f", t=T)
        hidT = big[:, T * F0:T * F0 + F0T * L].rearrange("p (f t) -> p f t", f=F0T)
        p1 = big[:, 0:2048].rearrange("p (r h k) -> p r h k", r=4, h=2)
        pT1 = big[:, 2048:4096].rearrange("p (r k h q) -> p r k h q", r=2, k=T, h=2)
        avT1 = big[:, 4096:6144].rearrange("p (m t) -> p m t", m=I1T)
        mid = part(3072)
        pT0a = mid[:, 0:2048].rearrange("p (r h q) -> p r h q", r=2, h=HG)
        pT0b = mid[:, 2048:3072].rearrange("p (r h q) -> p r h q", r=2, h=HG)
        qT1 = mid[:, 0:2048].rearrange("p (m t) -> p m t", m=I1T)
        avT0 = part(KD, L)
        hs = sb("hs", [P, 2, 512])
        pay = sb("pay", [P, T, TOP, ROW])
        stats = sb("stats", [P, T, 6])
        mv = sb("mv", [P, T, 2])
        vpe = sb("vpe", [P, T])
        rstd = sb("rstd", [P, T])
        negm0 = sb("negm0", [P, T, H0])
        sums = sb("sums", [P, NBR, T * H0])
        expnm = sb("expnm", [P, T * H0])
        keep = part(NBR, T * H0)
        junk = sb("junk", [P, 1])
        ks = hs[:, 1, 0:NBR * T * H0].rearrange("p (r n) -> p r n", r=NBR)
        den = sb("den", [P, T * H0])
        isz = sb("isz", [P, T * H0])
        rden = sb("rden", [P, T * H0])
        coef = part(NBR, T * H0)
        cfa, cfb = (hs[:, 0, i * T * H0 * 4:(i + 1) * T * H0 * 4].rearrange("p (n c) -> p n c", c=4) for i in range(2))
        negm1 = sb("negm1", [P, 4, 2])
        z1 = sb("z1", [P, 4, 2])
        r1 = sb("r1", [P, 4, 2])
        lg = sb("lg", [P, T, 16])
        pr = sb("pr", [P, T, 16])
        lnm = sb("lnm", [P, T])
        lsum = sb("lsum", [P, T])
        top8 = sb("top8", [P, T, 8])
        idx8 = sb("idx8", [P, T, 8], U32)
        idxf = sb("idxf", [P, T, TOP])
        wsum = sb("wsum", [P, T])
        wtop = sb("wtop", [P, T, TOP])
        comb = sb("comb", [P, T, E0N])
        comb2 = sb("comb2", [P, T, E0N])
        hot = sb("hot", [P, T, TOP, E1N])
        both = sb("both", [P, T, E1N], BF16)
        rank = sb("rank", [P, T, E1N])
        hotr = sb("hotr", [P, T, TOP, E1N])
        posf = sb("posf", [P, T, TOP])
        pos = sb("pos", [P, T, TOP], I32)
        run = sb("run", [P, E1N])
        tok = sb("tok", [P, T], I32)
        tgate = sb("tgate", [P, 1])
        gbo1 = bo1

        score_banks = [bank(f"score{i}") for i in range(2)]
        turn_a, turn_d = bank("turn_a"), bank("turn_d")
        prod_d = [bank(f"prod_d{i}") for i in range(2)]
        prod_a = score_banks + [bank(f"prod_a{i}") for i in range(2)]

        def signal(name, per, start=None):
            return Signal(sem(name), per, start)

        x_loaded = signal("x_loaded", 16)
        ctx_loaded = signal("ctx_loaded", 16)
        ctx0_loaded = signal("ctx0_loaded", 16)
        stored = signal("stored", 16)
        pd = Ring(prod_d, signal("prod_d_full", N_PD), signal("prod_d_empty", N_PD))
        pa = Ring(prod_a, signal("prod_a_full", N_PA), signal("prod_a_empty", N_PA))
        ta = Ring([turn_a], signal("turn_a_full", N_TA), signal("turn_a_empty", N_TA))
        td = Ring([turn_d], signal("turn_d_full", N_TD), signal("turn_d_empty", N_TD))
        av0_used = signal("av0_used", 3)
        maxed = signal("maxed", N_S)
        x_used = signal("x_used", 1)
        var_ready = signal("var_ready", 4)
        rstd_ready = signal("rstd_ready", 4)
        normed = signal("normed", 4)
        guard_exp = signal("guard_exp", 1)
        coef_ready = signal("coef_ready", 1)
        weighed_d = signal("weighed_d", HG + 2)
        weighed_p = signal("weighed_p", 2)
        kpadded = signal("kpadded", KD)
        lexp = signal("lexp", 2)
        comb_ready = signal("comb_ready", 1)
        hid_weighed = signal("hid_weighed", 4)
        recip1 = signal("recip1", N_S1)
        p1_ready = signal("p1_ready", N_S1)
        both_ready = signal("both_ready", 1)
        pos_ready = signal("pos_ready", 1)
        scattered = signal("scattered", 16 * T * TOP, 16)
        step = signal("step", N_STEP)
        kraw = signal("kraw", 1)

        c_loaded, w0_loaded, w_loaded, setup_act, setup_dve = (
            sem(n) for n in ("c_loaded", "w0_loaded", "w_loaded", "setup_act", "setup_dve"))
        pads = sem("pads")
        spare = sem("spare")

        block = ctx.enter_context(nc.Block())

        @block.sync
        def _(sp):
            def batch(b, main=True):
                if main:
                    sp.wait_ge(x_used.sem, x_used.at(b, 0))
                sp.dma_start(x_in[:, :, :], x[bass.ds(b + 1, 1)].rearrange("b (t p) d -> p (b t) d", p=P)).then_inc(x_loaded.sem, 16)
                if main:
                    sp.wait_ge(pd.full.sem, pd.full.at(b, PD_V0 - N_PD))
                sp.dma_start(ctx0[:, :, :], ctxT[bass.ds(b + 1, 1)].rearrange("b (k p) t -> p (b k) t", p=P)).then_inc(ctx0_loaded.sem, 16)
                if main:
                    sp.wait_ge(pa.full.sem, pa.full.at(b, PA_V1 + 1))
                sp.dma_start(ctx_in[:, :, :], ctxT[bass.ds(b + 1, 1)].rearrange("b (k p) t -> p (b k) t", p=P)).then_inc(ctx_loaded.sem, 16)

            sp.dma_start(cst[:, :], cf32).then_inc(c_loaded, 16)
            batch(-1, main=False)
            sp.dma_start(wts[:, NW_BIAS:NW32], w32[:, NW_BIAS:]).then_inc(w0_loaded, 16)
            sp.dma_start(wts[:, 0:NW_L0], w32[:, 0:NW_L0]).then_inc(w0_loaded, 16)
            sp.dma_start(cbf[:, :], cb16).then_inc(c_loaded, 16)
            sp.dma_start(wts[:, NW_L0:NW_BIAS], w32[:, NW_L0:NW_BIAS]).then_inc(w_loaded, 16)
            with sp.Fori(0, B - 1) as b:
                batch(b)
            sp.wait_ge(pd.full.sem, pd.full.at(B - 1, PD_DOWN))
            sp.dma_start(wts[:, 0:WE1], we1[0]).then_inc(expert_loaded[0], 16)
            sp.wait_ge(pa.full.sem, pa.full.at(B - 1, PA_V1 + 1))
            sp.dma_start(wts[:, WE1:2 * WE1], we1[1]).then_inc(expert_loaded[1], 16)

        @block.gpsimd
        def _(pool):
            def batch(b, main=True, ahead=True):
                n_rstd = [0]

                def rsqrt():
                    n_rstd[0] += 1
                    pool.wait_ge(var_ready.sem, var_ready.at(b, n_rstd[0]))
                    nc.gpsimd.tensor_tensor(rstd[:, :], vpe[:, :], c("neghalf"), ALU.pow).then_inc(rstd_ready.sem, 1)

                if main:
                    pool.wait_ge(coef_ready.sem, coef_ready.at(b, 1))
                    for g in range(2, H0 // HG):
                        v = e0b[:, g * HG:(g + 1) * HG, :].rearrange("p h (k c) -> p h k c", c=4)
                        cf = cfa[:, H0 + g * HG:H0 + (g + 1) * HG, :]
                        nc.gpsimd.tensor_tensor(v, v, cf.rearrange("p h (o c) -> p h o c", o=1).to_broadcast([P, HG, L // 4, 4]),
                                                ALU.mult).then_inc(weighed_p.sem, 1)
                    rsqrt()
                else:
                    skip(pool, weighed_p, b, 0, 2)
                    skip(pool, rstd_ready, b, 0, 2)
                    n_rstd[0] += 2
                    rsqrt()
                if ahead:
                    for k in range(KD):
                        pool.wait_ge(*((kraw.sem, kraw.at(b, 1)) if k == 0 else (pd.empty.sem, pd.empty.at(b, PD_K0))))
                        if k == 0 and main:
                            pool.wait_ge(pa.full.sem, pa.full.at(b, 0))
                        pool.sem_inc(spare, 1)
                        for h in range(G0):
                            ins = nc.gpsimd.tensor_scalar(kpad0[:, k * G0 + h, :], kT0[:, k, :], c("head")[:, h:h + 1], 1.0,
                                                          ALU.mult, ALU.mult)
                        ins.then_inc(kpadded.sem, 1)
                else:
                    skip(pool, kpadded, b, 0, KD)
                if main:
                    n = 0
                    for t in range(T):
                        for ci, (f0, fn) in enumerate(CH0[:2]):
                            n += 1
                            pool.wait_ge(pd.empty.sem, pd.empty.at(b, PD_U + t * 3 + ci))
                            pool.wait_ge(comb_ready.sem, comb_ready.at(b, 1))
                            v = hid[:, t, f0:f0 + fn].rearrange("p (e m) -> p e m", m=M0R)
                            ne = fn // M0R
                            cw = comb[:, t, f0 // M0R:f0 // M0R + ne]
                            nc.gpsimd.tensor_tensor(v, v, cw.rearrange("p (e o) -> p e o", o=1).to_broadcast([P, ne, M0R]),
                                                    ALU.mult).then_inc(hid_weighed.sem, 1)
                    rsqrt()
                else:
                    skip(pool, hid_weighed, b, 0, 4)
                for i in range(N_S1):
                    if main:
                        pool.wait_ge(recip1.sem, recip1.at(b, i + 1))
                        pool.sem_inc(spare, 1)
                        for h in range(2):
                            ins = nc.gpsimd.tensor_scalar(p1[:, i % 4, h, :], p1[:, i % 4, h, :], r1[:, i % 4, h:h + 1], 1.0,
                                                          ALU.mult, ALU.mult)
                        ins.then_inc(p1_ready.sem, 1)
                    if main and i == AHEAD_NORM + 1:
                        if ahead:
                            rsqrt()
                        else:
                            skip(pool, rstd_ready, b, 2, 1)
                            n_rstd[0] += 1
                if main:
                    rsqrt()
                else:
                    skip(pool, p1_ready, b, 0, N_S1)
                    skip(pool, rstd_ready, b, 3, 1)
                    pool.wait_ge(w0_loaded, 32)
                if ahead:
                    pool.wait_ge(pd.empty.sem, pd.empty.at(b, PD_O1))
                    if not main:
                        pool.wait_ge(x_loaded.sem, x_loaded.at(b, 16))
                    nc.gpsimd.tensor_tensor(xb[:, :, :], x_in[:, :, :], bo0.rearrange("p (o n) -> p o n", o=1).to_broadcast([P, T, D]), ALU.add).then_inc(x_used.sem, 1)
                if not main:
                    return
                pool.wait_ge(pos_ready.sem, pos_ready.at(b, 1))
                pool.sem_inc(spare, 1)
                for t in range(T):
                    for k in range(TOP):
                        pool.indirect_dma_start(rows, bass.IndirectOffsetOnAxis(ap=pos[:, t, k:k + 1], axis=0),
                                                pay[:, t, k, :], None).then_inc(scattered.sem, 16)

            pool.dma_start(tok[:, :], tok0).then_inc(scattered.sem, 16)
            nc.gpsimd.memset(vpad0[:, :, :, :], 0.0).then_inc(pads, 1)
            pool.wait_ge(c_loaded, 32)
            batch(-1, main=False)
            nc.gpsimd.memset(kpad1[:, :, :], 0.0).then_inc(pads, 1)
            nc.gpsimd.memset(vpad1[:, :, :, :], 0.0).then_inc(pads, 1)
            with pool.Fori(0, B - 1) as b:
                batch(b)
            batch(B - 1, ahead=False)
            pool.wait_ge(scattered.sem, 16 * T * TOP * B + 16)

        @block.scalar
        def _(act):
            def batch(b, main=True, ahead=True):
                tra, proda = Turn(act, ta, b), Turn(act, pa, b)

                def copy_turned(dst):
                    src = tra.take()
                    nc.scalar.activation(dst, src[:, 0:512].rearrange("p (a n) -> p a n", n=dst.shape[-1]), ACT.Copy).then_inc(ta.empty.sem, 1)

                def copy_p1(i):
                    pair, t = i // 2, i % 2
                    src = tra.take()
                    if pair >= 2:
                        act.wait_ge(pd.full.sem, pd.full.at(b, PD_AV1 + pair - 2))
                    nc.scalar.activation(pT1[:, pair % 2, :, :, t * P:(t + 1) * P],
                                         src[:, :].rearrange("p (k h n) -> p k h n", k=2, h=2), ACT.Copy).then_inc(ta.empty.sem, 1)

                def attention1(i):
                    src = proda.take()
                    act.wait_ge(maxed.sem, maxed.at(b, i + 1))
                    if i >= 4:
                        j = i - 4
                        r, n = (ta, ta_p1(j)) if j % 2 == 0 else (td, TD_P1 + j // 2)
                        act.wait_ge(r.full.sem, r.full.at(b, n))
                        act.wait_ge(recip1.sem, recip1.at(b, j + 1))
                    for h in range(2):
                        ins = nc.scalar.activation(p1[:, i % 4, h, :], src[:, h * L:(h + 1) * L], ACT.Exp,
                                                   bias=negm1[:, i % 4, h:h + 1], accum_out=z1[:, i % 4, h:h + 1])
                    ins.then_inc(pa.empty.sem, 1)

                def values1(t):
                    for half in range(2):
                        src = proda.take()
                        if t == 0 and half == 0:
                            act.wait_ge(pd.full.sem, pd.full.at(b, PD_AV7 - N_PD))
                        dst = vpad1[:, t, :, :].rearrange("p (m e) (f n) -> p m e f n", e=2, f=2)
                        v = src[:, :].rearrange("p (m e n) -> p m e n", e=2, n=DH1)
                        nc.scalar.activation(dst[:, half * 4:half * 4 + 4, 0, 0, :], v[:, :, 0, :], ACT.Copy)
                        nc.scalar.activation(dst[:, half * 4:half * 4 + 4, 1, 1, :], v[:, :, 1, :], ACT.Copy).then_inc(pa.empty.sem, 1)

                def exps0(i):
                    src = proda.take()
                    act.wait_ge(maxed.sem, maxed.at(b, N_S1 + i + 1))
                    if i == 0 or i == H0 // HG:
                        act.wait_ge(pd.full.sem, pd.full.at(b, PD_O1))
                    t, nh = (0, HG) if i < H0 // HG else (1, 2)
                    h0 = i * HG if t == 0 else (i - H0 // HG) * 2
                    for h in range(nh):
                        e = e0a[:, h0 + h, :] if t == 0 else e0b[:, h0 + h, :]
                        n = (t + 1) * P
                        ins = nc.scalar.activation(e, src[:, h * n:(h + 1) * n], ACT.Exp, bias=negm0[:, t, h0 + h:h0 + h + 1],
                                                   accum_out=sums[:, 0, t * H0 + h0 + h:t * H0 + h0 + h + 1])
                    ins.then_inc(pa.empty.sem, 1)

                if main:
                    for m in range(0, I1T, 2):
                        src = proda.take()
                        if m == 0:
                            act.wait_ge(pa.full.sem, pa.full.at(b, 0))
                        v = src[:, :].rearrange("p (m n) -> p m n", m=2)
                        kp = kpad1[:, :, :].rearrange("p (m e) n -> p m e n", e=2)
                        nc.scalar.activation(kp[0:64, m:m + 2, 0, :], v[0:64], ACT.Copy)
                        nc.scalar.activation(kp[64:P, m:m + 2, 1, :], v[64:P], ACT.Copy).then_inc(pa.empty.sem, 1)
                    values1(0)
                    for i in range(0, 12, 2):
                        g, seg = i // 3, i % 3
                        if g >= 2:
                            act.wait_ge(av0_used.sem, av0_used.at(b, g - 1))
                        dst = pT0b[:, g % 2] if seg == 2 else pT0a[:, g % 2, :, seg * P:(seg + 1) * P]
                        copy_turned(dst)
                    act.wait_ge(pd.full.sem, pd.full.at(b, PD_Q0 - N_PD))
                    copy_turned(xnT[:, :, :])
                    act.wait_ge(pd.empty.sem, pd.empty.at(b, PD_ROUTER))
                    nc.scalar.activation(pr[:, :, :], lg[:, :, :], ACT.Exp).then_inc(lexp.sem, 1)
                    def silu(i):
                        t, (f0, fn) = i // 3, CH0[i % 3]
                        src = proda.take()
                        if i >= 2:
                            act.wait_ge(pd.empty.sem, pd.empty.at(b, PD_U + i - 2))
                        nc.scalar.activation(hs[:, i % 2, 0:fn], src[:, 0:fn], ACT.Silu).then_inc(pa.empty.sem, 1)

                    def copy_hid(i):
                        t, (f0, fn) = i // 3, CH0[i % 3]
                        src = tra.take()
                        nf = fn // P
                        nc.scalar.activation(hidT[:, f0 // P:f0 // P + nf, t * P:(t + 1) * P],
                                             src[:, 0:fn].rearrange("p (f n) -> p f n", n=P), ACT.Copy).then_inc(ta.empty.sem, 1)

                    for i in range(5):
                        silu(i)
                    copy_hid(1)
                    silu(5)
                    copy_hid(3)
                    nc.scalar.activation(junk[:, :], w("gate"), ACT.Exp)
                    copy_hid(5)
                    src = tra.take()
                    act.wait_ge(pa.full.sem, pa.full.at(b, PA_G + 5))
                    act.wait_ge(pd.full.sem, pd.full.at(b, PD_U + 5))
                    nc.scalar.activation(xnT[:, 0, :], src[:, 0:L], ACT.Identity, bias=beta[:, 0:1], scale=gamma[:, 0:1])
                    nc.scalar.activation(xnT[:, 1, :], src[:, L:2 * L], ACT.Identity, bias=beta[:, 1:2], scale=gamma[:, 1:2]).then_inc(ta.empty.sem, 1)
                    values1(1)
                    for _k in range(2):
                        src = proda.take()
                        nc.scalar.activation(qT1[:, 4 * _k:4 * _k + 2, :], src[:, :].rearrange("p (m n) -> p m n", m=2),
                                             ACT.Copy, scale=DH1 ** -0.5).then_inc(pa.empty.sem, 1)
                else:
                    proda.skip(pa.empty, PA_S1 - 1)
                    tra.skip(ta.empty, ta_p1(0) - 1)
                    skip(act, lexp, b, 0, 1)

                for i in range(N_S1 + 3):
                    if i < N_S1 and main:
                        attention1(i)
                    if i == AHEAD_TURN:
                        if not main:
                            proda.skip(pa.empty, N_S1)
                            tra.skip(ta.empty, 6)
                        if ahead:
                            if main:
                                act.wait_ge(pd.full.sem, pd.full.at(b, PD_Q1 + 1))
                                act.wait_ge(pa.full.sem, pa.full.at(b, PA_Q1 + 1))
                            copy_turned(xnT[:, :, :])
                        else:
                            tra.skip(ta.empty, 1)
                    if i >= 3 and i % 2 == 1 and main:
                        copy_p1(i - 3)
                if main:
                    act.wait_ge(pd.empty.sem, pd.empty.at(b, PD_O1))
                    act.dma_start(acc[bass.ds(b, 1)].rearrange("b (t p) d -> p (b t) d", p=P), x1[:, :, :]).then_inc(stored.sem, 16)
                else:
                    skip(act, stored, b, 0, 16)
                    tra.skip(ta.empty, 3)
                    skip(act, lexp, b, 1, 1)
                for i in range(N_S0):
                    if ahead:
                        exps0(i)
                    if i == 1 and main:
                        act.wait_ge(pd.full.sem, pd.full.at(b, PD_Q0))
                        copy_turned(xnT[:, :, :])
                    if i == 2 and main:
                        act.wait_ge(pd.empty.sem, pd.empty.at(b, PD_LOGIT))
                        nc.scalar.activation(pr[:, :, 0:E1N], lg[:, :, 0:E1N], ACT.Exp).then_inc(lexp.sem, 1)
                if ahead:
                    nc.scalar.activation(expnm[:, :], negm0[:, :, :].rearrange("p t h -> p (t h)"), ACT.Exp).then_inc(guard_exp.sem, 1)
                    assert (tra.n, proda.n) == (N_TA, N_PA), (tra.n, proda.n)

            act.wait_ge(w0_loaded, 32)
            nc.scalar.activation(tgate[:, :], w("gate"), ACT.Tanh).then_inc(setup_act, 1)
            batch(-1, main=False)
            act.wait_ge(pads, 3)
            act.wait_ge(w_loaded, 16)
            with act.Fori(0, B - 1) as b:
                batch(b)
            batch(B - 1, ahead=False)
            act.wait_ge(stored.sem, 16 * (B + 1))

        @block.vector
        def _(dve):
            def batch(b, main=True, ahead=True):
                trd, prodd, score = Turn(dve, td, b), Turn(dve, pd, b), Turn(dve, pa, b)
                n_step, n_rstd, n_l = [0], [0], [0]

                def then(ins, meanwhile=None):
                    n_step[0] += 1
                    ins.then_inc(step.sem, 1)
                    if meanwhile is not None:
                        meanwhile()
                    dve.wait_ge(step.sem, step.at(b, n_step[0]))

                def apart():
                    dve.sem_inc(spare, 1)

                def release(ins, place):
                    ins.then_inc(place.ring.empty.sem, 1)
                    dve.wait_ge(place.ring.empty.sem, place.ring.empty.at(b, place.n))

                def norm_sums(src):
                    nc.vector.bn_stats(stats[:, 0, :], src[:, 0, :])
                    then(nc.vector.bn_stats(stats[:, 1, :], src[:, 1, :]))

                def norm_var(twice=False):
                    apart()
                    nc.vector.bn_aggr(mv[:, 0, :], stats[:, 0, :])
                    then(nc.vector.bn_aggr(mv[:, 1, :], stats[:, 1, :]))
                    if twice:
                        ins = nc.vector.tensor_scalar(vpe[:, :], mv[:, :, 1], 1 + EPS, EPS * EPS, ALU.mult, ALU.add)
                    else:
                        ins = nc.vector.tensor_scalar(vpe[:, :], mv[:, :, 1], EPS, None, ALU.add)
                    ins.then_inc(var_ready.sem, 1)
                    n_rstd[0] += 1

                def norm_scale(src, dst, t):
                    if t == 0:
                        dve.wait_ge(rstd_ready.sem, rstd_ready.at(b, n_rstd[0]))
                    return nc.vector.tensor_scalar(dst[:, t, :], src[:, t, :], mv[:, t, 0:1], rstd[:, t:t + 1], ALU.subtract, ALU.mult)

                def norm(src, dst, signal_, meanwhile=None, twice=False):
                    norm_sums(src)
                    norm_var(twice)
                    if meanwhile is not None:
                        meanwhile()
                    for t in range(T):
                        ins = norm_scale(src, dst, t)
                    ins.then_inc(signal_.sem, 1)

                def choose(n_experts, eps, meanwhile=(None,) * 5):
                    n_l[0] += 1
                    src = prodd.take()
                    v = src[:, 0:T * n_experts].rearrange("p (t e) -> p t e", t=T)
                    then(nc.vector.tensor_reduce(lnm[:, :], v, AX.X, ALU.max, negate=True))
                    release(nc.vector.tensor_tensor(lg[:, :, 0:n_experts], v, lnm[:, :].rearrange("p (t o) -> p t o", o=1).to_broadcast([P, T, n_experts]), ALU.add), prodd)
                    if meanwhile[0] is not None:
                        meanwhile[0]()
                    dve.wait_ge(lexp.sem, lexp.at(b, n_l[0]))
                    p = pr[:, :, 0:n_experts]
                    then(nc.vector.tensor_reduce(lsum[:, :], p, AX.X, ALU.add))
                    then(nc.vector.reciprocal(lsum[:, :], lsum[:, :]), meanwhile[1])
                    then(nc.vector.tensor_tensor(p, p, lsum[:, :].rearrange("p (t o) -> p t o", o=1).to_broadcast([P, T, n_experts]), ALU.mult))
                    apart()
                    nc.vector.max(top8[:, 0, :], pr[:, 0, 0:n_experts])
                    then(nc.vector.max(top8[:, 1, :], pr[:, 1, 0:n_experts]), meanwhile[2])
                    apart()
                    nc.vector.max_index(idx8[:, 0, :], top8[:, 0, :], pr[:, 0, 0:n_experts])
                    then(nc.vector.max_index(idx8[:, 1, :], top8[:, 1, :], pr[:, 1, 0:n_experts]), meanwhile[3])
                    nc.vector.tensor_copy(idxf[:, :, :], idx8[:, :, 0:TOP])
                    then(nc.vector.tensor_reduce(wsum[:, :], top8[:, :, 0:TOP], AX.X, ALU.add))
                    if eps:
                        then(nc.vector.tensor_scalar(wsum[:, :], wsum[:, :], eps, None, ALU.add))
                    then(nc.vector.reciprocal(wsum[:, :], wsum[:, :]))
                    then(nc.vector.tensor_tensor(wtop[:, :, :], top8[:, :, 0:TOP], wsum[:, :].rearrange("p (t o) -> p t o", o=1).to_broadcast([P, T, TOP]), ALU.mult), meanwhile[4])

                def copy_turned(dst, n=512, inner=P):
                    src = trd.take()
                    v = src[:, 0:n]
                    v = v.rearrange("p (a n) -> p a n", n=inner) if len(dst.shape) == 3 else v.rearrange("p (k h n) -> p k h n", k=2, h=2)
                    nc.vector.tensor_copy(dst, v).then_inc(td.empty.sem, 1)

                def keys0():
                    if not ahead:
                        prodd.skip(pd.empty, 1)
                        skip(dve, kraw, b, 0, 1)
                        return
                    src = prodd.take()
                    if main:
                        dve.wait_ge(kpadded.sem, kpadded.at(b, 0))
                    for k, done in enumerate((kraw, pd.empty)):
                        nc.vector.tensor_scalar(kT0[:, k, :], src[:, k * L:(k + 1) * L], bk0[:, k:k + 1], None, ALU.add).then_inc(done.sem, 1)

                def values0():
                    if not ahead:
                        prodd.skip(pd.empty, 1)
                        return
                    src = prodd.take()
                    if not main:
                        dve.wait_ge(pads, 1)
                    for t in range(T):
                        for k in range(KD):
                            dst = vpad0[:, t, k * G0:(k + 1) * G0, :].rearrange("p h (g n) -> p (h g) n", n=DH0)[:, 0:G0 * G0:G0 + 1, :]
                            v = src[:, t * D + k * P:t * D + (k + 1) * P].rearrange("p (h n) -> p h n", n=DH0)
                            bias = bv0[:, k * P:(k + 1) * P].rearrange("p (h n) -> p h n", n=DH0)
                            ins = nc.vector.tensor_tensor(dst, v, bias, ALU.add)
                    ins.then_inc(pd.empty.sem, 1)

                def queries0():
                    if not ahead:
                        prodd.skip(pd.empty, 1)
                        return
                    src = prodd.take()
                    for k in range(KD):
                        ins = nc.vector.tensor_scalar(qT0[:, k, :], src[:, k * L:(k + 1) * L], bq0[:, k:k + 1], DH0 ** -0.5, ALU.add, ALU.mult)
                    ins.then_inc(pd.empty.sem, 1)

                def av1(pair):
                    src = prodd.take()
                    nc.vector.tensor_copy(avT1[:, pair, :], src[:, 0:L]).then_inc(pd.empty.sem, 1)

                def recip(j):
                    dve.wait_ge(pa.empty.sem, pa.empty.at(b, PA_S1 + j))
                    if j >= 4:
                        dve.wait_ge(p1_ready.sem, p1_ready.at(b, j - 3))
                    nc.vector.reciprocal(r1[:, j % 4, :], z1[:, j % 4, :]).then_inc(recip1.sem, 1)

                def max1(i):
                    src = score.take()
                    if i >= 4:
                        dve.wait_ge(pa.empty.sem, pa.empty.at(b, PA_S1 + i - 4))
                    nc.vector.tensor_reduce(negm1[:, i % 4, :], src[:, :].rearrange("p (h n) -> p h n", h=2), AX.X, ALU.max,
                                            negate=True).then_inc(maxed.sem, 1)

                def heads0(i):
                    t, nh = (0, HG) if i < H0 // HG else (1, 2)
                    return t, nh, i * HG if t == 0 else (i - H0 // HG) * 2

                def max0(i):
                    src = score.take()
                    t, nh, h0 = heads0(i)
                    nc.vector.tensor_reduce(negm0[:, t, h0:h0 + nh], src[:, :].rearrange("p (h n) -> p h n", h=nh), AX.X, ALU.max,
                                            negate=True).then_inc(maxed.sem, 1)

                def sums0(i):
                    t, nh, h0 = heads0(i)
                    dve.wait_ge(pa.empty.sem, pa.empty.at(b, PA_S0 + i))
                    for r, dil in ((1, 2), (2, 4)):
                        v = (e0a, e0b)[t][:, h0:h0 + nh, :].rearrange("p h (k c) -> p h k c", c=dil)[:, :, :, h0 // (H0 // dil)]
                        ins = nc.vector.tensor_reduce(sums[:, r, t * H0 + h0:t * H0 + h0 + nh], v, AX.X, ALU.add)
                    return ins

                io = c("iota")
                if main:
                    dve.wait_ge(guard_exp.sem, guard_exp.at(b, 0))
                    bc = lambda ap: ap.rearrange("p (o n) -> p o n", o=1).to_broadcast([P, NBR, T * H0])
                    then(nc.vector.tensor_tensor(keep[:, :, :], sums[:, :, :], bc(expnm[:, :]), ALU.not_equal))
                    nc.vector.tensor_scalar(coef[:, :, :], sums[:, :, :], 1e-30, float(NBR), ALU.max, ALU.mult)
                    then(nc.vector.tensor_tensor(keep[:, :, :], keep[:, :, :], cover, ALU.mult))
                    then(nc.vector.tensor_tensor(ks[:, :, :], keep[:, :, :], sums[:, :, :], ALU.mult))
                    then(nc.vector.tensor_reduce(den[:, :], ks[:, :, :].rearrange("p r n -> p n r"), AX.X, ALU.add))
                    then(nc.vector.tensor_scalar(isz[:, :], den[:, :], 0.0, None, ALU.is_equal))
                    then(nc.vector.tensor_tensor(den[:, :], den[:, :], isz[:, :], ALU.add))
                    nc.vector.reciprocal(rden[:, :], den[:, :])
                    then(nc.vector.reciprocal(ks[:, :, :], coef[:, :, :]))
                    nc.vector.tensor_tensor(coef[:, :, :], keep[:, :, :], bc(rden[:, :]), ALU.mult)
                    then(nc.vector.tensor_tensor(ks[:, :, :], ks[:, :, :], bc(isz[:, :]), ALU.mult))
                    then(nc.vector.tensor_tensor(ks[:, :, :], ks[:, :, :], cover, ALU.mult))
                    then(nc.vector.tensor_tensor(coef[:, :, :], coef[:, :, :], ks[:, :, :], ALU.add))
                    c4 = lambda r: coef[:, r, :].rearrange("p (t h o) -> p t h o", t=T, o=1).to_broadcast([P, T, H0, 4])
                    c2 = lambda ap: ap.rearrange("p (t h) c -> p t h c", t=1).to_broadcast([P, T, H0, 4])
                    ct = lambda ap: ap.rearrange("p (t h) c -> p t h c", t=T)
                    nc.vector.tensor_tensor(ct(cfa), c2(class2), c4(1), ALU.mult)
                    then(nc.vector.tensor_tensor(ct(cfb), c2(class4), c4(2), ALU.mult))
                    then(nc.vector.tensor_tensor(cfa, cfa, cfb, ALU.add))
                    nc.vector.tensor_tensor(ct(cfa), ct(cfa), c4(0), ALU.add).then_inc(coef_ready.sem, 1)
                    dve.wait_ge(coef_ready.sem, coef_ready.at(b, 1))

                    def weigh(t, g):
                        e = (e0a, e0b)[t]
                        v = e[:, g * HG:(g + 1) * HG, :].rearrange("p h (k c) -> p h k c", c=4)
                        cf = cfa[:, t * H0 + g * HG:t * H0 + (g + 1) * HG, :]
                        nc.vector.tensor_tensor(v, v, cf.rearrange("p h (o c) -> p h o c", o=1).to_broadcast([P, HG, (t + 1) * P // 4, 4]),
                                                ALU.mult).then_inc(weighed_d.sem, 1)

                    def copy_p0(i):
                        g, seg = i // 3, i % 3
                        if g >= 2:
                            dve.wait_ge(av0_used.sem, av0_used.at(b, g - 1))
                        copy_turned(pT0b[:, g % 2] if seg == 2 else pT0a[:, g % 2, :, seg * P:(seg + 1) * P])

                    weigh(0, 0)
                    weigh(1, 0)
                    weigh(0, 1)
                    copy_p0(1)
                    weigh(1, 1)
                    copy_p0(3)
                    weigh(0, 2)
                    weigh(0, 3)
                    for i in range(5, 12, 2):
                        copy_p0(i)
                    src = prodd.take()
                    nc.vector.tensor_copy(avT0[:, :, :], src[:, :].rearrange("p (k n) -> p k n", k=KD)).then_inc(pd.empty.sem, 1)
                    src = prodd.take()
                    dve.wait_ge(stored.sem, stored.at(b, 0))
                    dve.wait_ge(x_used.sem, x_used.at(b, 0))
                    release(nc.vector.tensor_tensor(x1[:, :, :], src[:, :].rearrange("p (t n) -> p t n", t=T), xb[:, :, :], ALU.add), prodd)
                    norm(x1, xn, normed, keys0)
                    values0()
                    choose(E0N, 1e-9)
                    for t in range(T):
                        nc.vector.tensor_scalar(comb[:, t, :], io, idxf[:, t, 0:1], wtop[:, t, 0:1], ALU.is_equal, ALU.mult)
                        ins = nc.vector.tensor_scalar(comb2[:, t, :], io, idxf[:, t, 1:2], wtop[:, t, 1:2], ALU.is_equal, ALU.mult)
                    then(ins)
                    nc.vector.tensor_tensor(comb[:, :, :], comb[:, :, :], comb2[:, :, :], ALU.add).then_inc(comb_ready.sem, 1)
                    def product(i):
                        t, (f0, fn) = i // 3, CH0[i % 3]
                        src = prodd.take()
                        dve.wait_ge(pa.empty.sem, pa.empty.at(b, PA_G + i))
                        nc.vector.tensor_tensor(hid[:, t, f0:f0 + fn], src[:, 0:fn], hs[:, i % 2, 0:fn], ALU.mult).then_inc(pd.empty.sem, 1)

                    def copy_hid(i):
                        t, (f0, fn) = i // 3, CH0[i % 3]
                        copy_turned(hidT[:, f0 // P:(f0 + fn) // P, t * P:(t + 1) * P], fn)

                    for i in range(4):
                        product(i)
                    copy_hid(0)
                    product(4)
                    product(5)
                    copy_hid(2)
                    copy_hid(4)
                    src = prodd.take()
                    release(nc.vector.tensor_tensor(x1[:, :, :], src[:, :].rearrange("p (t n) -> p t n", t=T), x1[:, :, :], ALU.add), prodd)
                    norm(x1, xn, normed, twice=True)
                    nc.vector.tensor_tensor(xb[:, :, :], x1[:, :, :], gbo1.rearrange("p (o n) -> p o n", o=1).to_broadcast([P, T, D]), ALU.add)
                    for _k in range(2):
                        src = prodd.take()
                        nc.vector.tensor_scalar(qT1[:, 4 * _k + 2:4 * _k + 4, :], src[:, :].rearrange("p (m n) -> p m n", m=2),
                                                DH1 ** -0.5, None, ALU.mult).then_inc(pd.empty.sem, 1)
                else:
                    prodd.skip(pd.empty, PD_K0 - 1)
                    for signal_ in (var_ready, normed):
                        skip(dve, signal_, b, 0, 2)
                    n_rstd[0] += 2
                    dve.wait_ge(x_loaded.sem, x_loaded.at(b, 16))
                    norm(x_in, xn, normed)
                    dve.wait_ge(w0_loaded, 32)
                    keys0()
                    values0()
                    prodd.skip(pd.empty, PD_AV1 - PD_V0 - 1)
                    trd.skip(td.empty, N_TD)
                    for signal_, n in ((coef_ready, 1), (weighed_d, HG + 2), (comb_ready, 1), (recip1, N_S1), (maxed, N_S1)):
                        skip(dve, signal_, b, 0, n)
                score.n = PA_S1 - 1

                for i in range(N_S1 + 4):
                    if main:
                        if i % 2 == 1 and i <= N_S1:
                            recip(i - 1)
                        if i < N_S1:
                            max1(i)
                        if i % 2 == 0 and 1 <= i <= N_S1:
                            recip(i - 1)
                    if not main:
                        continue
                    if i == AHEAD_NORM - 2:
                        if ahead:
                            dve.wait_ge(x_loaded.sem, x_loaded.at(b, 16))
                            norm_sums(x_in)
                    if i == AHEAD_NORM:
                        if ahead:
                            norm_var()
                        else:
                            skip(dve, var_ready, b, 2, 1)
                            n_rstd[0] += 1
                    if i == AHEAD_NORM + 2:
                        if ahead:
                            norm_scale(x_in, xn, 0)
                    if i == AHEAD_NORM + 3:
                        if ahead:
                            norm_scale(x_in, xn, 1).then_inc(normed.sem, 1)
                        else:
                            skip(dve, normed, b, 2, 1)
                    if i >= 4 and i % 2 == 0 and i - 3 < N_S1:
                        j = i - 3
                        pair = j // 2
                        if pair >= 2:
                            dve.wait_ge(pd.full.sem, pd.full.at(b, PD_AV1 + pair - 2))
                        copy_turned(pT1[:, pair % 2, :, :, (j % 2) * P:(j % 2 + 1) * P])
                    if i >= 7 and i % 2 == 1 and (i - 7) // 2 < I1T - 1:
                        if (i - 7) // 2 == I1T - 2:
                            queries0()
                        av1((i - 7) // 2)
                if not main:
                    prodd.skip(pd.empty, I1T - 2)
                    queries0()
                score.n = PA_S0 - 1
                if main:
                    av1(I1T - 1)
                    src = prodd.take()
                    release(nc.vector.scalar_tensor_tensor(out=x1[:, :, :], in0=src[:, :].rearrange("p (t n) -> p t n", t=T), scalar=tgate[:, 0:1],
                                                           in1=xb[:, :, :], op0=ALU.mult, op1=ALU.add), prodd)
                    dve.wait_ge(scattered.sem, scattered.at(b, 0))
                    norm(x1, pay[:, :, 0, 0:D], normed, (lambda: max0(0)) if ahead else None)
                    if ahead:
                        max0(1)
                    nc.vector.tensor_scalar(pay[:, 0, 1, 0:D], x1[:, 0, :], mv[:, 0, 0:1], rstd[:, 0:1], ALU.subtract, ALU.mult)
                    nc.vector.tensor_scalar(pay[:, 1, 1, 0:D], x1[:, 1, :], mv[:, 1, 0:1], rstd[:, 1:2], ALU.subtract, ALU.mult)
                else:
                    prodd.skip(pd.empty, 3)
                    max0(0)
                    max0(1)
                    for signal_, done in ((normed, 3), (var_ready, 3), (both_ready, 0), (pos_ready, 0)):
                        skip(dve, signal_, b, done, 1)
                if ahead:
                    max0(2)
                if main:
                    choose(E1N, 0.0, (lambda: max0(3), lambda: sums0(0), lambda: max0(4), lambda: sums0(1), lambda: max0(5)) if ahead else (None,) * 5)
                    for t in range(T):
                        for k in range(TOP):
                            ins = nc.vector.tensor_scalar(hot[:, t, k, :], io[:, 0:E1N], idxf[:, t, k:k + 1], None, ALU.is_equal)
                    then(ins)
                    nc.vector.tensor_tensor(both[:, :, :], hot[:, :, 0, :], hot[:, :, 1, :], ALU.add).then_inc(both_ready.sem, 1)
                    payi = pay[:, :, :, :].bitcast(I32)
                    for k in range(TOP):
                        nc.vector.tensor_copy(pay[:, :, k, D], wtop[:, :, k])
                        then(nc.vector.tensor_copy(payi[:, :, k, D + 1], tok[:, :]))
                    then(nc.vector.tensor_scalar(tok[:, :], tok[:, :], L, None, ALU.add))

                def place():
                    src = prodd.take()
                    then(nc.vector.tensor_tensor(rank[:, :, :], src[:, 0:T * E1N].rearrange("p (t e) -> p t e", t=T),
                                                 run[:, :].rearrange("p (o e) -> p o e", o=1).to_broadcast([P, T, E1N]), ALU.add))
                    for k in range(TOP):
                        ins = nc.vector.tensor_tensor(hotr[:, :, k, :], hot[:, :, k, :], rank[:, :, :], ALU.mult)
                    then(ins)
                    nc.vector.tensor_tensor(run[:, :], src[:, T * E1N:(T + 1) * E1N], run[:, :], ALU.add).then_inc(pd.empty.sem, 1)
                    then(nc.vector.tensor_reduce(posf[:, :, :], hotr[:, :, :, :], AX.X, ALU.add))
                    nc.vector.tensor_copy(pos[:, :, :], posf[:, :, :]).then_inc(pos_ready.sem, 1)

                if not main:
                    max0(3)
                    sums0(0)
                    max0(4)
                    sums0(1)
                    max0(5)
                for i in range(N_S0 + 2):
                    if ahead and 6 <= i < N_S0:
                        max0(i)
                    if main and i == RANK_AFTER + 1:
                        place()
                    if ahead and i >= 4:
                        ins = sums0(i - 2)
                if ahead:
                    then(ins)
                if main and ahead:
                    assert (trd.n, prodd.n) == (N_TD, N_PD), (trd.n, prodd.n)
                    assert n_step[0] == N_STEP, n_step
                if not main:
                    prodd.skip(pd.empty, 2)
                    skip(dve, step, b, n_step[0], N_STEP - n_step[0])

            dve.wait_ge(c_loaded, 16)
            dve.wait_ge(w0_loaded, 32)
            dve.wait_ge(setup_act, 1)
            nc.vector.tensor_scalar(gbo1, bo1, tgate[:, 0:1], None, ALU.mult).then_inc(setup_dve, 1)
            nc.vector.tensor_copy(run[:, :], c("region")).then_inc(setup_dve, 1)
            dve.wait_ge(setup_dve, 2)
            batch(-1, main=False)
            dve.wait_ge(pads, 3)
            with dve.Fori(0, B - 1) as b:
                batch(b)
            batch(B - 1, ahead=False)
            dve.wait_ge(pd.empty.sem, pd.empty.at(B - 1, N_PD))
            nc.vector.tensor_tensor(counts_sb[:, :], run[:, :], c("region"), ALU.subtract).then_inc(setup_dve, 1)
            dve.wait_ge(setup_dve, 3)

        @block.tensor
        def _(pe):
            mm = nc.tensor.matmul

            def batch(b, main=True, ahead=True):
                tra, trd, prodd, proda = (Turn(pe, r, b) for r in (ta, td, pd, pa))

                def turn(ring, tiles):
                    dst = ring.claim()
                    for i, src in enumerate(tiles):
                        ins = nc.tensor.transpose(dst[:, i * P:(i + 1) * P], src, ident)
                    ins.then_inc(ring.ring.full.sem, 1)

                def features_out(ring, wk, xT, ms):
                    dst = ring.claim()
                    for i, m in enumerate(ms):
                        for k in range(KD):
                            ins = mm(dst[:, i * L:(i + 1) * L], wk[:, k, m * P:(m + 1) * P], xT[:, k, :], start=(k == 0), stop=(k == KD - 1))
                    ins.then_inc(ring.ring.full.sem, 1)

                def tokens_out(ring, xT, wk, nk, n, ts=range(T), c0=0):
                    dst = ring.claim()
                    for i, t in enumerate(ts):
                        for k in range(nk):
                            ins = mm(dst[:, i * n:(i + 1) * n], xT[:, k, t * P:(t + 1) * P], wk[:, k, c0:c0 + n], start=(k == 0), stop=(k == nk - 1))
                    ins.then_inc(ring.ring.full.sem, 1)

                def turn_p0(g):
                    hh = range(g * HG, (g + 1) * HG)
                    for seg in range(3):
                        if seg == 0:
                            pe.wait_ge(weighed_d.sem, weighed_d.at(b, (1, 3, 5, 6)[g]))
                        elif seg == 1 and g < 2:
                            pe.wait_ge(weighed_d.sem, weighed_d.at(b, (2, 4)[g]))
                        elif seg == 1:
                            pe.wait_ge(weighed_p.sem, weighed_p.at(b, g - 1))
                        src = e0a if seg == 0 else e0b
                        k0 = P if seg == 2 else 0
                        turn((tra, trd)[(g * 3 + seg) % 2], [src[:, h, k0:k0 + P] for h in hh])

                def av_p0(g, dst):
                    last = 3 * g + 2
                    for i in (last - 1, last):
                        r, n = (ta, TA_P0 + i // 2) if i % 2 == 0 else (td, TD_P0 + i // 2)
                        pe.wait_ge(r.empty.sem, r.empty.at(b, n))
                    k = g // 2
                    for i in range(HG):
                        h = g * HG + i
                        mm(dst[:, k * L:(k + 1) * L], vpad0[:, 0, h, :], pT0a[:, g % 2, i, :], start=(h % G0 == 0), stop=(h % G0 == G0 - 1), skip_group_check=True)
                        ins = mm(dst[:, k * L + P:(k + 1) * L], vpad0[:, 1, h, :], pT0b[:, g % 2, i, :], start=False, stop=(h % G0 == G0 - 1), skip_group_check=True)
                    if g < 3:
                        ins.then_inc(av0_used.sem, 1)
                    else:
                        ins.then_inc(pd.full.sem, 1)

                def av_p1(pair, dst):
                    for r, n in ((ta, ta_p1(2 * pair)), (td, TD_P1 + pair)):
                        pe.wait_ge(r.empty.sem, r.empty.at(b, n))
                    for e in range(2):
                        for k in range(T):
                            ins = mm(dst[:, 0:L], vpad1[:, k, 2 * pair + e, :], pT1[:, pair % 2, k, e, :],
                                     start=(e == 0 and k == 0), stop=(e == 1 and k == T - 1))
                    ins.then_inc(pd.full.sem, 1)

                def values1(t):
                    for half in range(2):
                        tokens_out(proda, ctx_in, wv1, KD, 512, ts=(t,), c0=half * 512)

                def scores0(i):
                    t, nh = (0, HG) if i < H0 // HG else (1, 2)
                    h0 = i * HG if t == 0 else (i - H0 // HG) * 2
                    k = h0 // G0
                    pe.wait_ge(kpadded.sem, kpadded.at(b, k + 1))
                    dst = proda.claim()
                    n = (t + 1) * P
                    v = dst[:, :].rearrange("p (h n) -> p h n", h=nh)
                    mm(v, qT0[:, k, t * P:(t + 1) * P], kpad0[:, h0:h0 + nh, 0:n], start=True, stop=True)
                    for h in range(nh):
                        ins = mm(v[:, h, t * P:(t + 1) * P], identb, causal, start=False, stop=True, skip_group_check=True)
                    ins.then_inc(pa.full.sem, 1)

                if main:
                    pe.wait_ge(ctx_loaded.sem, ctx_loaded.at(b, 0))
                    for m in range(0, I1T, 2):
                        features_out(proda, wk1, ctx_in, (m, m + 1))
                    values1(0)
                    turn_p0(0)
                    turn_p0(1)
                    dst = prodd.claim()
                    av_p0(0, dst)
                    turn_p0(2)
                    av_p0(1, dst)
                    turn_p0(3)
                    av_p0(2, dst)
                    av_p0(3, dst)
                    pe.wait_ge(pd.empty.sem, pd.empty.at(b, PD_AV0))
                    tokens_out(prodd, avT0, wo0, KD, D)
                else:
                    prodd.skip(pd.full, PD_K0 - 1)
                    tra.skip(ta.full, ta_p1(12) - 2)
                    proda.skip(pa.full, PA_S0 - 1)
                    trd.skip(td.full, N_TD)
                    skip(pe, av0_used, b, 0, 3)
                if ahead:
                    pe.wait_ge(ctx0_loaded.sem, ctx0_loaded.at(b, 16))
                    features_out(prodd, wk0, ctx0, (0, 1))
                    tokens_out(prodd, ctx0, wv0, KD, D)
                else:
                    prodd.skip(pd.full, 2)
                if main:
                    pe.wait_ge(normed.sem, normed.at(b, 1))
                    turn(tra, [xn[:, t, k * P:(k + 1) * P] for k in range(KD) for t in range(T)])
                    pe.wait_ge(ta.empty.sem, ta.empty.at(b, TA_X1))
                    tokens_out(prodd, xnT, router, KD, E0N)
                    def gate_up(i):
                        t, (f0, fn) = i // 3, CH0[i % 3]
                        tokens_out(proda, xnT, wg0, KD, fn, ts=(t,), c0=f0)
                        tokens_out(prodd, xnT, wu0, KD, fn, ts=(t,), c0=f0)

                    def turn_hid(i):
                        t, (f0, fn) = i // 3, CH0[i % 3]
                        if i % 3 < 2:
                            pe.wait_ge(hid_weighed.sem, hid_weighed.at(b, 2 * t + i % 3 + 1))
                        else:
                            pe.wait_ge(pd.empty.sem, pd.empty.at(b, PD_U + i))
                        turn((trd, tra)[i % 2], [hid[:, t, f0 + j * P:f0 + (j + 1) * P] for j in range(fn // P)])

                    def down(t, dst):
                        for r, n in ((ta, TA_H + t), (td, TD_H + 1)) if t == 0 else ((ta, TA_H + 2), (td, TD_H + 2)):
                            pe.wait_ge(r.empty.sem, r.empty.at(b, n))
                        for k in range(F0T):
                            ins = mm(dst[:, t * D:(t + 1) * D], hidT[:, k, t * P:(t + 1) * P], wd0[:, k, :], start=(k == 0), stop=(k == F0T - 1))
                        return ins

                    for i in range(4):
                        gate_up(i)
                    turn_hid(0)
                    gate_up(4)
                    turn_hid(1)
                    gate_up(5)
                    for i in (2, 3):
                        turn_hid(i)
                    dst = prodd.claim()
                    down(0, dst)
                    for i in (4, 5):
                        turn_hid(i)
                    down(1, dst).then_inc(pd.full.sem, 1)
                    values1(1)
                    pe.wait_ge(normed.sem, normed.at(b, 2))
                    turn(tra, [xn[:, t, k * P:(k + 1) * P] for k in range(KD) for t in range(T)])
                    pe.wait_ge(ta.empty.sem, ta.empty.at(b, TA_X2))
                    for m in range(4):
                        features_out((proda, prodd)[m % 2], wq1, xnT, (2 * m, 2 * m + 1))
                else:
                    prodd.skip(pd.full, PD_Q0 - PD_V0 - 1)

                for i in range(N_S1 + 3):
                    if main and i < N_S1:
                        pair, t = i // 2, i % 2
                        if i % 4 == 0:
                            r, n = (pa, PA_Q1 + i // 8) if i % 8 == 0 else (pd, PD_Q1 + i // 8)
                            pe.wait_ge(r.empty.sem, r.empty.at(b, n))
                        dst = proda.claim()
                        mm(dst[:, :], qT1[:, pair, t * P:(t + 1) * P], kpad1[:, 2 * pair:2 * pair + 2, :], start=True, stop=True).then_inc(pa.full.sem, 1)
                    if main and 3 <= i:
                        j = i - 3
                        pe.wait_ge(p1_ready.sem, p1_ready.at(b, j + 1))
                        turn((tra, trd)[j % 2], [p1[:, j % 4, e, k * P:(k + 1) * P] for k in range(T) for e in range(2)])
                    if i == AHEAD_TURN:
                        if ahead:
                            pe.wait_ge(normed.sem, normed.at(b, 3))
                            turn(tra, [xn[:, t, k * P:(k + 1) * P] for k in range(KD) for t in range(T)])
                        else:
                            tra.skip(ta.full, 1)
                    if i == N_S1 + 1:
                        if ahead:
                            pe.wait_ge(ta.empty.sem, ta.empty.at(b, ta_p1(12) - 1))
                            features_out(prodd, wq0, xnT, (0, 1))
                        else:
                            prodd.skip(pd.full, 1)
                    if main and i >= 6 and i % 2 == 0:
                        av_p1((i - 6) // 2, prodd.claim())
                if main:
                    av_dst, dst = prodd.claim(), prodd.claim()

                    def output(t, ks):
                        for k in ks:
                            ins = mm(dst[:, t * D:(t + 1) * D], avT1[:, k, t * P:(t + 1) * P], wo1[:, k, :],
                                     start=(k == 0), stop=(k == I1T - 1))
                        return ins

                    output(0, range(0, I1T // 2))
                    av_p1(I1T - 1, av_dst)
                    output(0, range(I1T // 2, I1T - 1))
                    pe.wait_ge(pd.empty.sem, pd.empty.at(b, PD_AV7))
                    output(0, (I1T - 1,))
                    output(1, range(I1T)).then_inc(pd.full.sem, 1)
                else:
                    prodd.skip(pd.full, 3)
                if ahead:
                    pe.wait_ge(pd.empty.sem, pd.empty.at(b, PD_Q0))
                    for i in range(4):
                        scores0(i)
                if main:
                    pe.wait_ge(normed.sem, normed.at(b, 4))
                    turn(tra, [pay[:, t, 0, k * P:(k + 1) * P] for k in range(KD) for t in range(T)])
                    pe.wait_ge(ta.empty.sem, ta.empty.at(b, TA_X3))
                    tokens_out(prodd, xnT, gate1, KD, E1N)
                else:
                    prodd.skip(pd.full, 2)
                    tra.skip(ta.full, 3)
                for i in range(4, N_S0):
                    if ahead:
                        scores0(i)
                    if main and i == RANK_AFTER:
                        pe.wait_ge(both_ready.sem, both_ready.at(b, 1))
                        dst = prodd.claim()
                        mm(dst[:, 0:E1N], below, both[:, 0, :], start=True, stop=True)
                        mm(dst[:, E1N:2 * E1N], below, both[:, 1, :], start=True, stop=False)
                        mm(dst[:, E1N:2 * E1N], onesb, both[:, 0, :], start=False, stop=True)
                        mm(dst[:, 2 * E1N:3 * E1N], onesb, both[:, 0, :], start=True, stop=False)
                        mm(dst[:, 2 * E1N:3 * E1N], onesb, both[:, 1, :], start=False, stop=True).then_inc(pd.full.sem, 1)
                if ahead:
                    assert (tra.n, trd.n, prodd.n, proda.n) == (N_TA, N_TD, N_PD, N_PA), (tra.n, trd.n, prodd.n, proda.n)

            pe.wait_ge(c_loaded, 32)
            pe.wait_ge(w0_loaded, 32)
            batch(-1, main=False)
            pe.wait_ge(w_loaded, 16)
            pe.wait_ge(pads, 3)
            with pe.Fori(0, B - 1) as b:
                batch(b)
            batch(B - 1, ahead=False)


def experts(nc, cst, wts, counts_sb, expert_loaded, pad_ids, we1, rows, acc, out):
    with ExitStack() as ctx:
        def sb(name, shape, dt=F32):
            return ctx.enter_context(nc.sbuf_tensor(name, shape, dt))

        def sem(name):
            return ctx.enter_context(nc.semaphore(name))

        def bank(name):
            return ctx.enter_context(nc.psum_tensor(name, [P, 512], F32))

        def c(name):
            return cst[:, C_F32[name][0]:sum(C_F32[name])]

        N = NBLK + 1
        ident = c("ident")
        xs = sb("xs", [P, ROW])
        xT = sb("xT", [P, KD, P])
        hs = sb("hs_e", [P, 512])
        hid = sb("hid_e", [P, F1])
        hidT = sb("hidT_e", [P, F1T, P])
        pad = hidT.rearrange("p f n -> p (f n)")[:, 0:ROW]
        y = sb("y", [P, D])
        wt_next, wt_now = sb("wt_next", [P, 1]), sb("wt_now", [P, 1])
        id_next, id_now = sb("id_next", [P, 1], I32), sb("id_now", [P, 1], I32)
        fl, nb, cum, prior = (sb(n, [P, E1N]) for n in ("fl", "nb", "cum", "prior"))
        cnt_i = sb("cnt_i", [P, E1N], I32)
        tail_i = sb("tail_i", [P, E1N], I32)
        at = [0]

        def scratch(*shape):
            n = int(np.prod(shape))
            at[0] += n
            v = hid[:, at[0] - n:at[0]]
            return v if len(shape) == 1 else v.rearrange("p (a b) -> p a b", b=shape[1])

        le, le2, upto = scratch(N, E1N), scratch(N, E1N), scratch(E1N, E1N)
        eid, rowf, tmp = scratch(N), scratch(N), scratch(N)
        row_i, eid_i = sb("row_i", [P, N], I32), sb("eid_i", [P, N], I32)

        turns_a = [bank(f"turn_a2{i}") for i in range(2)]
        turn_d, acc_bank = bank("turn_d2"), bank("acc_bank")
        prod_d = [bank(f"prod_d2{i}") for i in range(2)]
        prod_a = [bank(f"prod_a2{i}") for i in range(2)]
        signals = {}

        def signal(name, per, owner):
            s = Signal(sem(name), per)
            signals.setdefault(owner, []).append(s)
            return s

        pd = Ring(prod_d, signal("up_full", 2 * STEPS, "pe"), signal("up_empty", 2 * STEPS, "dve"))
        pa = Ring(prod_a, signal("gate_full", 2 * STEPS, "pe"), signal("gate_empty", 2 * STEPS, "act"))
        ta = Ring(turns_a, Signal(sem("turn_a2_full"), 2 * STEPS, 2), Signal(sem("turn_a2_empty"), 2 * STEPS, 2))
        td = Ring([turn_d], signal("turn_d2_full", STEPS, "pe"), signal("turn_d2_empty", STEPS, "dve"))
        ya = Ring([acc_bank], signal("y_full", STEPS, "pe"), signal("y_empty", STEPS, "dve"))
        xs_loaded = Signal(sem("xs_loaded"), 16 * STEPS, 16)
        added = Signal(sem("added"), 16 * STEPS, 16)
        meta = Signal(sem("meta"), STEPS, 1)
        moved = signal("moved", STEPS, "dve")
        expert_ready = sem("expert_ready")
        pad_loaded, tables, tail_ready, eid_ready, tails, chain, copied = (sem(n) for n in ("pad_loaded", "tables", "tail_ready", "eid_ready", "tails", "chain", "copied"))
        spare = sem("spare2")

        def prime(eng, owner):
            for s in signals[owner]:
                eng.sem_inc(s.sem, s.per)

        block = ctx.enter_context(nc.Block())

        @block.sync
        def _(sp):
            sp.dma_start(pad[:, :], pad_ids).then_inc(pad_loaded, 16)
            sp.wait_ge(pad_loaded, 16)
            sp.wait_ge(tail_ready, 1)
            for e in range(0, E1N // 2):
                at = sp.value_load(tail_i[0:1, e:e + 1], min_val=0, max_val=E1N * CAP - P)
                sp.dma_start(rows[bass.ds(at, P), :], pad[:, :]).then_inc(tails, 16)
            for e in range(E1N):
                if e >= 2:
                    part = WE1 // 6
                    for i in range(6):
                        sp.dma_start(wts[:, e * WE1 + i * part:e * WE1 + (i + 1) * part], we1[e][:, i * part:(i + 1) * part]).then_inc(expert_loaded[e], 16)
                        sp.wait_ge(expert_loaded[e], 16 * (i + 1))
                else:
                    sp.wait_ge(expert_loaded[e], 16)
                sp.sem_inc(expert_ready, 1)
            sp.wait_ge(added.sem, 16 * (NBLK + 1))
            sp.dma_start(out.rearrange("b t d -> (b t) d"), acc[0:NTOK, :]).then_inc(copied, 16)
            sp.wait_ge(copied, 16)

        @block.gpsimd
        def _(pool):
            pool.dma_start(y[:, :], pad_ids[:, 0:D]).then_inc(added.sem, 16)
            pool.wait_ge(tables, 1)
            pool.wait_ge(tails, 16 * (E1N + 2))
            at = pool.value_load(row_i[0:1, 0:1], min_val=0, max_val=E1N * CAP)
            pool.dma_start(xs[:, :], rows[bass.ds(at, P), :]).then_inc(xs_loaded.sem, 16)
            with pool.Fori(0, NBLK // STEPS) as j:
                for u in range(STEPS):
                    pool.wait_ge(meta.sem, meta.at(j, u))
                    pool.wait_ge(ta.full.sem, ta.full.at(j, 2 * u - 1))
                    at = pool.value_load(row_i[0:1, bass.ds(j * STEPS + u + 1, 1)], min_val=0, max_val=E1N * CAP)
                    pool.dma_start(xs[:, :], rows[bass.ds(at, P), :]).then_inc(xs_loaded.sem, 16)
                    pool.wait_ge(ya.empty.sem, ya.empty.at(j, u + 1))
                    pool.sem_inc(spare, 1)
                    pool.indirect_dma_start(acc, bass.IndirectOffsetOnAxis(ap=id_now[:, 0:1], axis=0), y[:, :], None,
                                            compute_op=ALU.add).then_inc(added.sem, 16)
            pool.wait_ge(added.sem, 16 * (NBLK + 1))

        @block.scalar
        def _(act):
            prime(act, "act")
            act.wait_ge(pad_loaded, 16)
            act.dma_start(rows[E1N * CAP:, :], pad[:, :]).then_inc(tails, 16)
            act.dma_start(acc[NTOK:, :], pad[:, 0:D]).then_inc(tails, 16)
            act.wait_ge(tail_ready, 1)
            for e in range(E1N // 2, E1N):
                at = act.value_load(tail_i[0:1, e:e + 1], min_val=0, max_val=E1N * CAP - P)
                act.dma_start(rows[bass.ds(at, P), :], pad[:, :]).then_inc(tails, 16)
            act.wait_ge(ta.full.sem, 2)
            nc.scalar.activation(xT[:, :, :], turns_a[0][:, 0:KD * P].rearrange("p (k n) -> p k n", k=KD), ACT.Copy).then_inc(ta.empty.sem, 2)
            with act.Fori(0, NBLK // STEPS) as j:
                tra, proda = Turn(act, ta, j), Turn(act, pa, j)
                for u in range(STEPS):
                    for i in range(2):
                        src = proda.take()
                        act.wait_ge(pd.empty.sem, pd.empty.at(j, 2 * u + i))
                        nc.scalar.activation(hs[:, :], src[:, :], ACT.Silu).then_inc(pa.empty.sem, 1)
                    src = tra.take()
                    nc.scalar.activation(xT[:, :, :], src[:, 0:KD * P].rearrange("p (k n) -> p k n", k=KD), ACT.Copy).then_inc(ta.empty.sem, 1)
                    src = tra.take()
                    nc.scalar.activation(hidT[:, 4:8, :], src[:, :].rearrange("p (f n) -> p f n", n=P), ACT.Copy).then_inc(ta.empty.sem, 1)

        @block.vector
        def _(dve):
            prime(dve, "dve")
            n = [0]

            def then(ins):
                n[0] += 1
                ins.then_inc(chain, 1)
                dve.wait_ge(chain, n[0])

            then(nc.vector.tensor_scalar(fl[:, :], counts_sb[:, :], float(P - 1), None, ALU.add))
            then(nc.vector.tensor_copy(cnt_i[:, :], fl[:, :]))
            nc.vector.tensor_tensor(fl[:, :], counts_sb[:, :], c("region"), ALU.add)
            then(nc.vector.tensor_single_scalar(cnt_i[:, :], cnt_i[:, :], 7, ALU.arith_shift_right))
            nc.vector.tensor_copy(tail_i[:, :], fl[:, :]).then_inc(tail_ready, 1)
            then(nc.vector.tensor_copy(nb[:, :], cnt_i[:, :]))
            then(nc.vector.tensor_tensor(upto[:, :, :], nb[:, :].rearrange("p (o e) -> p o e", o=1).to_broadcast([P, E1N, E1N]),
                                         c("upto").rearrange("p (n e) -> p n e", e=E1N), ALU.mult))
            then(nc.vector.tensor_reduce(cum[:, :], upto[:, :, :], AX.X, ALU.add))
            row = lambda ap: ap.rearrange("p (o e) -> p o e", o=1).to_broadcast([P, N, E1N])
            then(nc.vector.tensor_tensor(le[:, :, :], row(cum[:, :]), c("blocks").rearrange("p (n o) -> p n o", o=1).to_broadcast([P, N, E1N]), ALU.is_le))
            nc.vector.tensor_tensor(le2[:, :, :], le[:, :, :], row(nb[:, :]), ALU.mult)
            then(nc.vector.tensor_reduce(eid[:, :], le[:, :, :], AX.X, ALU.add))
            nc.vector.tensor_scalar(rowf[:, :], eid[:, :], float(CAP), None, ALU.mult)
            then(nc.vector.tensor_reduce(tmp[:, :], le2[:, :, :], AX.X, ALU.add))
            then(nc.vector.tensor_tensor(tmp[:, :], c("blocks"), tmp[:, :], ALU.subtract))
            then(nc.vector.tensor_scalar(tmp[:, :], tmp[:, :], float(P), None, ALU.mult))
            then(nc.vector.tensor_tensor(rowf[:, :], rowf[:, :], tmp[:, :], ALU.add))
            then(nc.vector.tensor_scalar(rowf[:, :], rowf[:, :], float(E1N * CAP), None, ALU.min))
            nc.vector.tensor_copy(row_i[:, :], rowf[:, :]).then_inc(tables, 1)
            then(nc.vector.tensor_scalar(eid[:, :], eid[:, :], float(E1N - 1), None, ALU.min))
            nc.vector.tensor_copy(eid_i[:, :], eid[:, :]).then_inc(eid_ready, 1)
            dve.wait_ge(xs_loaded.sem, 16)
            then(nc.vector.tensor_copy(wt_next[:, :], xs[:, D:D + 1]))
            nc.vector.tensor_copy(id_next[:, :], xs[:, D + 1:D + 2].bitcast(I32)).then_inc(meta.sem, 1)
            with dve.Fori(0, NBLK // STEPS) as j:
                trd, prodd, acc_t = Turn(dve, td, j), Turn(dve, pd, j), Turn(dve, ya, j)

                def product(i):
                    src = prodd.take()
                    dve.wait_ge(pa.empty.sem, pa.empty.at(j, prodd.n))
                    nc.vector.tensor_tensor(hid[:, i * 512:(i + 1) * 512], src[:, :], hs[:, :], ALU.mult).then_inc(pd.empty.sem, 1)

                for u in range(STEPS):
                    product(0)
                    src = trd.take()
                    nc.vector.tensor_copy(hidT[:, 0:4, :], src[:, :].rearrange("p (f n) -> p f n", n=P)).then_inc(td.empty.sem, 1)
                    product(1)
                    dve.wait_ge(added.sem, added.at(j, 16 * u))
                    dve.wait_ge(meta.sem, meta.at(j, u))
                    nc.vector.tensor_copy(wt_now[:, :], wt_next[:, :])
                    nc.vector.tensor_copy(id_now[:, :], id_next[:, :]).then_inc(moved.sem, 1)
                    dve.wait_ge(moved.sem, moved.at(j, u + 1))
                    dve.wait_ge(xs_loaded.sem, xs_loaded.at(j, 16 * (u + 1)))
                    nc.vector.tensor_copy(wt_next[:, :], xs[:, D:D + 1])
                    nc.vector.tensor_copy(id_next[:, :], xs[:, D + 1:D + 2].bitcast(I32)).then_inc(meta.sem, 1)
                    src = acc_t.take()
                    nc.vector.tensor_scalar(y[:, :], src[:, 0:D], wt_now[:, 0:1], None, ALU.mult).then_inc(ya.empty.sem, 1)

        @block.tensor
        def _(pe):
            prime(pe, "pe")
            mm = nc.tensor.matmul
            pe.wait_ge(xs_loaded.sem, 16)
            for k in range(KD):
                ins = nc.tensor.transpose(turns_a[0][:, k * P:(k + 1) * P], xs[:, k * P:(k + 1) * P], ident)
            ins.then_inc(ta.full.sem, 2)
            pe.wait_ge(eid_ready, 1)
            with pe.Fori(0, NBLK // STEPS) as j:
                tra, trd, prodd, proda, acc_t = (Turn(pe, r, j) for r in (ta, td, pd, pa, ya))

                def half(ring, base, which, i):
                    dst = ring.claim()
                    for k in range(KD):
                        ins = mm(dst[:, :], xT[:, k, :], wts[:, bass.ds(base + (which * KD + k) * F1 + i * 512, 512)], start=(k == 0), stop=(k == KD - 1))
                    ins.then_inc(ring.ring.full.sem, 1)

                def turn(ring, tiles):
                    dst = ring.claim()
                    for i, src in enumerate(tiles):
                        ins = nc.tensor.transpose(dst[:, i * P:(i + 1) * P], src, ident)
                    ins.then_inc(ring.ring.full.sem, 1)

                def down(dst, base, f0, f1):
                    for f in range(f0, f1):
                        ins = mm(dst[:, 0:D], hidT[:, f, :], wts[:, bass.ds(base + 2 * KD * F1 + f * D, D)], start=(f == 0), stop=(f == F1T - 1))
                    return ins

                for u in range(STEPS):
                    e = pe.value_load(eid_i[0:1, bass.ds(j * STEPS + u, 1)], min_val=0, max_val=E1N - 1)
                    pe.wait_ge(expert_ready, e + 1)
                    base = e * WE1
                    pe.wait_ge(ta.empty.sem, ta.empty.at(j, 2 * u - 1))
                    half(proda, base, 0, 0)
                    half(prodd, base, 1, 0)
                    half(proda, base, 0, 1)
                    pe.wait_ge(pd.empty.sem, pd.empty.at(j, 2 * u + 1))
                    turn(trd, [hid[:, f * P:(f + 1) * P] for f in range(4)])
                    half(prodd, base, 1, 1)
                    dst = acc_t.claim()
                    pe.wait_ge(td.empty.sem, td.empty.at(j, u + 1))
                    down(dst, base, 0, 2)
                    pe.wait_ge(xs_loaded.sem, xs_loaded.at(j, 16 * (u + 1)))
                    turn(tra, [xs[:, k * P:(k + 1) * P] for k in range(KD)])
                    pe.wait_ge(pd.empty.sem, pd.empty.at(j, 2 * u + 2))
                    turn(tra, [hid[:, f * P:(f + 1) * P] for f in range(4, 8)])
                    down(dst, base, 2, 4)
                    pe.wait_ge(ta.empty.sem, ta.empty.at(j, 2 * u + 2))
                    down(dst, base, 4, 8).then_inc(ya.full.sem, 1)


def build(nc, cf32, cb16, w32, tok0, pad_ids, x, ctxT, we1, out):
    acc = nc.dram_tensor("acc", [NTOK + P, D], F32, kind="Internal").ap()
    rows = nc.dram_tensor("rows", [E1N * CAP + P, ROW], F32, kind="Internal").ap()
    with ExitStack() as ctx:
        cst = ctx.enter_context(nc.sbuf_tensor("cst", [P, NC32], F32))
        counts_sb = ctx.enter_context(nc.sbuf_tensor("counts_sb", [P, E1N], F32))
        wts = ctx.enter_context(nc.sbuf_tensor("wts", [P, E1N * WE1], F32))
        expert_loaded = [ctx.enter_context(nc.semaphore(f"expert_loaded{e}")) for e in range(E1N)]
        layers(nc, cst, wts, counts_sb, expert_loaded, cf32, cb16, w32, tok0, x, ctxT, we1,
               acc[0:NTOK, :].rearrange("(b l) d -> b l d", b=B), rows)
        experts(nc, cst, wts, counts_sb, expert_loaded, pad_ids, we1, rows, acc, out)


def kernel(**inputs):
    import ml_dtypes
    import concourse.bacc as bacc
    from concourse.bass_utils import run_bass_kernel_spmd as run_spmd

    f32 = np.float32
    a = {k: np.asarray(v) for k, v in inputs.items()}

    p = np.arange(P)
    cf = np.zeros((P, NC32), f32)

    def put(table, dst, name, value):
        at, n = table[name]
        dst[:, at:at + n] = np.reshape(value, (-1, n)) if np.ndim(value) else value

    heads = np.arange(H0)
    put(C_F32, cf, "ident", np.eye(P, dtype=f32))
    put(C_F32, cf, "head", p[:, None] // DH0 == np.arange(G0)[None])
    cover = np.zeros((P, NBR, T, H0), f32)
    for r, dil in enumerate((1, 2, 4)):
        cover[:, r] = (p[:, None] % dil == heads[None] // (H0 // dil))[:, None]
    put(C_F32, cf, "cover", cover)
    for name, dil in (("class2", 2), ("class4", 4)):
        put(C_F32, cf, name, np.tile((np.arange(4)[None] % dil == heads[:, None] // (H0 // dil)).reshape(1, -1), (P, 1)))
    put(C_F32, cf, "iota", np.tile(np.arange(16), (P, 1)))
    put(C_F32, cf, "region", np.tile(np.arange(E1N) * CAP, (P, 1)))
    put(C_F32, cf, "neghalf", -0.5)
    put(C_F32, cf, "blocks", np.tile(np.arange(NBLK + 1), (P, 1)))
    put(C_F32, cf, "upto", np.tile((np.arange(E1N)[None] <= np.arange(E1N)[:, None]).reshape(1, -1), (P, 1)))
    cb = np.zeros((P, NCB), ml_dtypes.bfloat16)
    cb[:, 0:P] = np.eye(P)
    cb[:, P:2 * P] = np.where(p[None] <= p[:, None], 0.0, -1e30)
    cb[:, 2 * P:3 * P] = p[:, None] < p[None]
    cb[:, 3 * P:] = 1.0
    pad_ids = np.zeros((P, ROW), f32)
    pad_ids[:, D + 1] = (NTOK + p).astype(np.int32).view(f32)
    tok0 = (p[:, None] + P * np.arange(T)[None]).astype(np.int32)

    w = np.zeros((P, NW32), f32)
    tiles = lambda m: m.reshape(-1, P, m.shape[-1]).transpose(1, 0, 2).reshape(P, -1)
    wide = lambda r, s: np.concatenate([r.transpose(1, 0, 2).reshape(D, -1), s.transpose(1, 0, 2).reshape(D, -1)], 1)
    for name, key in (("wq0", "Wq"), ("wk0", "Wk"), ("wv0", "Wv"), ("wo0", "Wo")):
        put(W_F32, w, name, tiles(a["L0_xattn_" + key].T))
    put(W_F32, w, "router", tiles(a["L0_ffn_router_w"]))
    put(W_F32, w, "wg0", tiles(wide(a["L0_ffn_wg_r"], a["L0_ffn_wg_s"])))
    put(W_F32, w, "wu0", tiles(wide(a["L0_ffn_wu_r"], a["L0_ffn_wu_s"])))
    put(W_F32, w, "wd0", tiles(np.concatenate([a["L0_ffn_wd_r"].reshape(-1, D), a["L0_ffn_wd_s"].reshape(-1, D)])))
    put(W_F32, w, "wq1", tiles(a["L1_xattn_w_q"]))
    put(W_F32, w, "wk1", tiles(a["L1_xattn_w_kv"][:, :I1]))
    put(W_F32, w, "wv1", tiles(a["L1_xattn_w_kv"][:, I1:]))
    put(W_F32, w, "wo1", tiles(a["L1_xattn_w_out"]))
    put(W_F32, w, "gate1", tiles(a["L1_ffn_gate_w"]))
    for name, key in (("bq0", "L0_xattn_bq"), ("bk0", "L0_xattn_bk"), ("gamma", "L1_xattn_ln_gamma"), ("beta", "L1_xattn_ln_beta")):
        put(W_F32, w, name, a[key].reshape(KD, P).T)
    put(W_F32, w, "gate", np.tile(a["L1_xattn_gate"], (P, 1)))
    for name, key in (("bv0", "L0_xattn_bv"), ("bo0", "L0_xattn_bo"), ("bo1", "L1_xattn_b_out")):
        put(W_F32, w, name, np.tile(a[key], (P, 1)))
    we1 = np.concatenate([
        a["L1_ffn_w1"].reshape(E1N, KD, P, F1).transpose(0, 2, 1, 3).reshape(E1N, P, -1),
        a["L1_ffn_w3"].reshape(E1N, KD, P, F1).transpose(0, 2, 1, 3).reshape(E1N, P, -1),
        a["L1_ffn_w2"].reshape(E1N, F1T, P, D).transpose(0, 2, 1, 3).reshape(E1N, P, -1)], 2)
    ctxT = a["ctx_1024"].transpose(0, 2, 1)

    arrays = {"cf32": cf, "cb16": cb, "w32": w, "tok0": tok0, "pad_ids": pad_ids, "x": a["x"], "ctxT": ctxT, "we1": we1}
    arrays = {k: np.ascontiguousarray(v) for k, v in arrays.items()}
    nc = bacc.Bacc("TRN2", target_bir_lowering=False, num_devices=1)
    aps = {k: nc.dram_tensor(k + "_dram", v.shape, mybir.dt.from_np(v.dtype), kind="ExternalInput").ap() for k, v in arrays.items()}
    out = nc.dram_tensor("out_dram", (B, L, D), F32, kind="ExternalOutput").ap()
    build(nc, out=out, **aps)
    r = run_spmd(nc, [{k + "_dram": v for k, v in arrays.items()}], core_ids=[0])
    return r.results[0]["out_dram"]
```

```python
from contextlib import ExitStack

import concourse.bass as bass
import numpy as np
from concourse import mybir

F32 = mybir.dt.float32
BF16 = mybir.dt.bfloat16
I32 = mybir.dt.int32
U32 = mybir.dt.uint32
ALU = mybir.AluOpType
ACT = mybir.ActivationFunctionType
AX = mybir.AxisListType

P = 128
B, L, D = 8, 256, 256
T = L // P
KD = D // P
EPS = 1e-5

H0, DH0 = 16, 16
G0 = P // DH0
HG = 4
NBR = 3
E0N, M0R, M0S = 16, 64, 256
F0 = E0N * M0R + M0S
F0T = F0 // P
CH0 = [(0, 512), (512, 512), (1024, 256)]

H1, DH1 = 16, 64
I1 = H1 * DH1
I1T = I1 // P

E1N, F1 = 8, 1024
F1T = F1 // P
TOP = 2
NTOK = B * L
CAP = NTOK + P
ROW = D + 2
NBLK = (TOP * NTOK) // P + E1N - 1
WE1 = 2 * KD * F1 + F1T * D
STEPS = 3
assert NBLK % STEPS == 0

C_F32 = {}
W_F32 = {}


def columns(table, parts):
    at = 0
    for name, n in parts:
        table[name] = (at, n)
        at += n
    return at


NC32 = columns(C_F32, [("ident", P), ("head", G0), ("cover", NBR * T * H0), ("class2", H0 * 4), ("class4", H0 * 4),
                       ("iota", 16), ("region", E1N), ("neghalf", T), ("blocks", NBLK + 1), ("upto", E1N * E1N)])
NW32 = columns(W_F32, [("wq0", KD * D), ("wk0", KD * D), ("wv0", KD * D), ("wo0", KD * D),
                       ("router", KD * E0N), ("wg0", KD * F0), ("wu0", KD * F0), ("wd0", F0T * D),
                       ("wk1", KD * I1), ("wv1", KD * I1), ("wq1", KD * I1), ("wo1", I1T * D), ("gate1", KD * E1N),
                       ("bq0", KD), ("bk0", KD), ("gamma", KD), ("beta", KD), ("gate", 1),
                       ("bv0", D), ("bo0", D), ("bo1", D)])
NW_L0 = W_F32["router"][0]
NW_BIAS = W_F32["bq0"][0]
assert WE1 <= W_F32["wk1"][0] and 2 * WE1 <= W_F32["wq1"][0]
NCB = 4 * P


class Signal:

    def __init__(self, sem, per, start=None):
        self.sem, self.per, self.start = sem, per, per if start is None else start

    def at(self, turn, n):
        return turn * self.per + (self.start + n)


class Ring:

    def __init__(self, banks, full, empty):
        self.banks, self.full, self.empty = banks, full, empty


class Turn:

    def __init__(self, eng, ring, turn):
        self.eng, self.ring, self.turn, self.n = eng, ring, turn, 0

    def claim(self):
        self.n += 1
        before = self.ring.empty.at(self.turn, self.n - len(self.ring.banks))
        if not isinstance(before, int) or before > 0:
            self.eng.wait_ge(self.ring.empty.sem, before)
        return self.ring.banks[(self.n - 1) % len(self.ring.banks)]

    def take(self):
        self.n += 1
        self.eng.wait_ge(self.ring.full.sem, self.ring.full.at(self.turn, self.n))
        return self.ring.banks[(self.n - 1) % len(self.ring.banks)]

    def skip(self, signal, n):
        skip(self.eng, signal, self.turn, self.n, n)
        self.n += n


def skip(eng, signal, turn, done, n):
    before = signal.at(turn, done)
    if not isinstance(before, int) or before > 0:
        eng.wait_ge(signal.sem, before)
    eng.sem_inc(signal.sem, n)


PD_AV0, PD_O0, PD_K0, PD_V0, PD_ROUTER, PD_U, PD_DOWN, PD_Q1, PD_AV1, PD_Q0, PD_AV7, PD_O1, PD_LOGIT, PD_RANK = (
    1, 3, 4, 5, 6, 7, 13, 14, 16, 22, 24, 25, 26, 27)
N_S0 = H0 // HG + H0 // 2
N_S1 = I1T * T
N_S = N_S0 + N_S1
PA_K1, PA_P0, PA_G, PA_V1, PA_Q1, PA_S1 = 1, 6, 15, 21, 23, 25
PA_S0 = PA_S1 + N_S1
TA_X1, TA_H, TA_X2, TA_X3 = 1, 2, 5, 15
TD_P0, TD_X1, TD_H, TD_X2, TD_P1, TD_X3 = 1, 7, 8, 11, 12, 20
N_PD, N_PA, N_TA, N_TD = 28, 52, 16, 20
N_STEP = 48
AHEAD_NORM, AHEAD_TURN = 7, 14
KEYS_AT, KEYS_COPY_AT = 10, 10
RANK_AFTER = 11


def ta_p1(j):
    return 6 + j // 2 + (j > AHEAD_TURN - 3)


def layers(nc, cst, wts, expert_loaded, cf32, cb16, w32, tok0, pad_ids, x, ctxT, we1, out, rows):
    with ExitStack() as ctx:
        def sb(name, shape, dt=F32):
            return ctx.enter_context(nc.sbuf_tensor(name, shape, dt))

        def sem(name):
            return ctx.enter_context(nc.semaphore(name))

        def bank(name):
            return ctx.enter_context(nc.psum_tensor(name, [P, 512], F32))

        cbf = sb("cbf", [P, NCB], BF16)
        def c(name):
            return cst[:, C_F32[name][0]:sum(C_F32[name])]

        def w(name, k=1):
            ap = wts[:, W_F32[name][0]:sum(W_F32[name])]
            return ap.rearrange("p (k n) -> p k n", k=k) if k > 1 else ap

        ident = c("ident")
        tokens_rows = out[0:NTOK, :].rearrange("(b l) d -> b l d", b=B)
        identb, causal, below, onesb = (cbf[:, i * P:(i + 1) * P] for i in range(4))
        cover = c("cover").rearrange("p (r n) -> p r n", r=NBR)
        class2 = c("class2").rearrange("p (h c) -> p h c", c=4)
        class4 = c("class4").rearrange("p (h c) -> p h c", c=4)
        wq0, wk0, wv0, wo0 = (w(n, KD) for n in ("wq0", "wk0", "wv0", "wo0"))
        router, wg0, wu0, wd0 = w("router", KD), w("wg0", KD), w("wu0", KD), w("wd0", F0T)
        wq1, wk1, wv1, wo1, gate1 = w("wq1", KD), w("wk1", KD), w("wv1", KD), w("wo1", I1T), w("gate1", KD)
        bq0, bk0, gamma, beta = w("bq0"), w("bk0"), w("gamma"), w("beta")
        bv0, bo0, bo1 = w("bv0"), w("bo0"), w("bo1")

        at = [NW32]

        def part(*shape):
            n = int(np.prod(shape))
            at[0] += n
            assert at[0] <= E1N * WE1
            v = wts[:, at[0] - n:at[0]]
            if len(shape) == 1:
                return v
            names = "abc"[:len(shape)]
            return v.rearrange(f"p ({' '.join(names)}) -> p {' '.join(names)}", **dict(zip(names[1:], shape[1:])))

        x_in = sb("x_in", [P, T, D])
        ctx_in = part(KD, L)
        ctx0 = part(KD, L)
        xb = part(T, D)
        xn = part(T, D)
        xnT = part(KD, L)
        x1 = part(T, D)
        kT0 = part(KD, L)
        qT0 = part(KD, L)
        kpad0 = part(H0, L)
        vpad0 = part(T, H0, P)
        kpad1 = part(H1, L)
        vpad1 = part(T, H1, P)
        big = part(6144)
        e0a = big[:, 0:H0 * P].rearrange("p (h k) -> p h k", h=H0)
        e0b = big[:, H0 * P:3 * H0 * P].rearrange("p (h k) -> p h k", h=H0)
        hid = big[:, 0:T * F0].rearrange("p (t f) -> p t f", t=T)
        hidT = big[:, T * F0:T * F0 + F0T * L].rearrange("p (f t) -> p f t", f=F0T)
        p1 = big[:, 0:2048].rearrange("p (r h k) -> p r h k", r=4, h=2)
        pT1 = big[:, 2048:4096].rearrange("p (r k h q) -> p r k h q", r=2, k=T, h=2)
        avT1 = big[:, 4096:6144].rearrange("p (m t) -> p m t", m=I1T)
        mid = part(3072)
        N = NBLK + 1
        flat = kpad0.rearrange("p h n -> p (h n)")
        at0 = [0]

        def scratch(*shape):
            n = int(np.prod(shape))
            at0[0] += n
            v = flat[:, at0[0] - n:at0[0]]
            return v if len(shape) == 1 else v.rearrange("p (a b) -> p a b", b=shape[1])

        pad = scratch(ROW)
        le, le2, upto = scratch(N, E1N), scratch(N, E1N), scratch(E1N, E1N)
        eid, rowf, tmp = scratch(N), scratch(N), scratch(N)
        counts, fl, nb, cum = (scratch(E1N) for _ in range(4))
        cnt_i, tail_i = (scratch(E1N).bitcast(I32) for _ in range(2))
        row_i, eid_i = tables_of(c)
        pT0a = mid[:, 0:2048].rearrange("p (r h q) -> p r h q", r=2, h=HG)
        pT0b = mid[:, 2048:3072].rearrange("p (r h q) -> p r h q", r=2, h=HG)
        qT1 = mid[:, 0:2048].rearrange("p (m t) -> p m t", m=I1T)
        avT0 = part(KD, L)
        hs = sb("hs", [P, 2, 512])
        pay = sb("pay", [P, T, TOP, ROW])
        stats = sb("stats", [P, T, 6])
        mv = sb("mv", [P, T, 2])
        vpe = sb("vpe", [P, T])
        rstd = sb("rstd", [P, T])
        negm0 = sb("negm0", [P, T, H0])
        sums = sb("sums", [P, NBR, T * H0])
        expnm = sb("expnm", [P, T * H0])
        keep = part(NBR, T * H0)
        junk = sb("junk", [P, 1])
        ks = hs[:, 1, 0:NBR * T * H0].rearrange("p (r n) -> p r n", r=NBR)
        den = sb("den", [P, T * H0])
        isz = sb("isz", [P, T * H0])
        rden = sb("rden", [P, T * H0])
        coef = part(NBR, T * H0)
        cfa, cfb = (hs[:, 0, i * T * H0 * 4:(i + 1) * T * H0 * 4].rearrange("p (n c) -> p n c", c=4) for i in range(2))
        negm1 = sb("negm1", [P, 4, 2])
        z1 = sb("z1", [P, 4, 2])
        r1 = sb("r1", [P, 4, 2])
        lg = sb("lg", [P, T, 16])
        pr = sb("pr", [P, T, 16])
        lnm = sb("lnm", [P, T])
        lsum = sb("lsum", [P, T])
        top8 = sb("top8", [P, T, 8])
        idx8 = sb("idx8", [P, T, 8], U32)
        idxf = sb("idxf", [P, T, TOP])
        wsum = sb("wsum", [P, T])
        wtop = sb("wtop", [P, T, TOP])
        comb = sb("comb", [P, T, E0N])
        comb2 = sb("comb2", [P, T, E0N])
        hot = sb("hot", [P, T, TOP, E1N])
        both = sb("both", [P, T, E1N], BF16)
        rank = sb("rank", [P, T, E1N])
        hotr = sb("hotr", [P, T, TOP, E1N])
        posf = sb("posf", [P, T, TOP])
        pos = sb("pos", [P, T, TOP], I32)
        run = sb("run", [P, E1N])
        tok = sb("tok", [P, T], I32)
        tgate = sb("tgate", [P, 1])
        gbo1 = bo1

        score_banks = [bank(f"score{i}") for i in range(2)]
        turn_a, turn_d = bank("turn_a"), bank("turn_d")
        prod_d = [bank(f"prod_d{i}") for i in range(2)]
        prod_a = score_banks + [bank(f"prod_a{i}") for i in range(2)]

        def signal(name, per, start=None):
            return Signal(sem(name), per, start)

        x_loaded = signal("x_loaded", 16)
        ctx_loaded = signal("ctx_loaded", 16)
        ctx0_loaded = signal("ctx0_loaded", 16)
        stored = signal("stored", 16)
        pd = Ring(prod_d, signal("prod_d_full", N_PD), signal("prod_d_empty", N_PD))
        pa = Ring(prod_a, signal("prod_a_full", N_PA), signal("prod_a_empty", N_PA))
        ta = Ring([turn_a], signal("turn_a_full", N_TA), signal("turn_a_empty", N_TA))
        td = Ring([turn_d], signal("turn_d_full", N_TD), signal("turn_d_empty", N_TD))
        av0_used = signal("av0_used", 2)
        maxed = signal("maxed", N_S)
        x_used = signal("x_used", 1)
        var_ready = signal("var_ready", 4)
        rstd_ready = signal("rstd_ready", 4)
        normed = signal("normed", 4)
        guard_exp = signal("guard_exp", 1)
        coef_ready = signal("coef_ready", 1)
        weighed_d = signal("weighed_d", HG + 4)
        weighed_p = signal("weighed_p", 2)
        kpadded = signal("kpadded", KD)
        lexp = signal("lexp", 2)
        comb_ready = signal("comb_ready", 1)
        hid_weighed = signal("hid_weighed", 4)
        recip1 = signal("recip1", N_S1)
        p1_ready = signal("p1_ready", N_S1)
        both_ready = signal("both_ready", 1)
        pos_ready = signal("pos_ready", 1)
        pay_copied = signal("pay_copied", 1)
        scattered = signal("scattered", 16 * T * TOP, 16)
        step = signal("step", N_STEP)
        kraw = signal("kraw", 1)

        c_loaded, w0_loaded, wl0_loaded, w1_loaded, w_loaded, setup_act, setup_dve = (
            sem(n) for n in ("c_loaded", "w0_loaded", "wl0_loaded", "w1_loaded", "w_loaded", "setup_act", "setup_dve"))
        pads = sem("pads")
        pad_loaded, tail_ready, chain, tails = (sem(n) for n in ("pad_loaded", "tail_ready", "chain", "tails"))
        spare = sem("spare")

        block = ctx.enter_context(nc.Block())

        @block.sync
        def _(sp):
            def batch(b, main=True):
                if main:
                    sp.wait_ge(x_used.sem, x_used.at(b, 0))
                sp.dma_start(x_in[:, :, :], x[bass.ds(b + 1, 1)].rearrange("b (t p) d -> p (b t) d", p=P)).then_inc(x_loaded.sem, 16)
                if main:
                    sp.wait_ge(pd.full.sem, pd.full.at(b, PD_V0 - N_PD))
                else:
                    sp.dma_start(cst[:, :], cf32).then_inc(c_loaded, 16)
                    sp.dma_start(cbf[:, :], cb16).then_inc(c_loaded, 16)
                sp.dma_start(ctx0[:, :, :], ctxT[bass.ds(b + 1, 1)].rearrange("b (k p) t -> p (b k) t", p=P)).then_inc(ctx0_loaded.sem, 16)
                if not main:
                    return
                sp.wait_ge(pa.full.sem, pa.full.at(b, PA_V1 + 1))
                sp.dma_start(ctx_in[:, :, :], ctxT[bass.ds(b + 1, 1)].rearrange("b (k p) t -> p (b k) t", p=P)).then_inc(ctx_loaded.sem, 16)

            batch(-1, main=False)
            sp.dma_start(wts[:, 0:NW_L0], w32[:, 0:NW_L0]).then_inc(wl0_loaded, 16)
            sp.dma_start(wts[:, NW_BIAS:NW32], w32[:, NW_BIAS:]).then_inc(w0_loaded, 16)
            at, n = W_F32["wk1"]
            sp.dma_start(ctx_in[:, :, :], ctxT[0:1].rearrange("b (k p) t -> p (b k) t", p=P)).then_inc(ctx_loaded.sem, 16)
            sp.dma_start(wts[:, at:at + n], w32[:, at:at + n]).then_inc(w1_loaded, 16)
            sp.dma_start(wts[:, NW_L0:at], w32[:, NW_L0:at]).then_inc(w_loaded, 16)
            sp.dma_start(wts[:, at + n:NW_BIAS], w32[:, at + n:NW_BIAS]).then_inc(w_loaded, 16)
            with sp.Fori(0, B - 1) as b:
                batch(b)
            sp.wait_ge(pd.full.sem, pd.full.at(B - 1, PD_DOWN))
            sp.dma_start(wts[:, 0:WE1], we1[0]).then_inc(expert_loaded[0], 16)
            sp.wait_ge(pa.full.sem, pa.full.at(B - 1, PA_V1 + 1))
            sp.dma_start(wts[:, WE1:2 * WE1], we1[1]).then_inc(expert_loaded[1], 16)
            sp.dma_start(pad, pad_ids).then_inc(pad_loaded, 16)
            sp.wait_ge(pad_loaded, 16)
            sp.dma_start(rows[E1N * CAP:, :], pad).then_inc(tails, 16)
            sp.dma_start(out[NTOK:, :], pad[:, 0:D]).then_inc(tails, 16)
            sp.wait_ge(tail_ready, 1)
            for e in range(0, E1N // 2):
                at = sp.value_load(tail_i[0:1, e:e + 1], min_val=0, max_val=E1N * CAP - P)
                sp.dma_start(rows[bass.ds(at, P), :], pad).then_inc(tails, 16)
            sp.wait_ge(tails, 16 * (E1N + 2))

        @block.gpsimd
        def _(pool):
            def batch(b, main=True, ahead=True):
                n_rstd = [0]

                def rsqrt():
                    n_rstd[0] += 1
                    pool.wait_ge(var_ready.sem, var_ready.at(b, n_rstd[0]))
                    nc.gpsimd.tensor_tensor(rstd[:, :], vpe[:, :], c("neghalf"), ALU.pow).then_inc(rstd_ready.sem, 1)

                if main:
                    pool.wait_ge(coef_ready.sem, coef_ready.at(b, 1))
                    for g in range(2, H0 // HG):
                        v = e0b[:, g * HG:(g + 1) * HG, :].rearrange("p h (k c) -> p h k c", c=4)
                        cf = cfa[:, H0 + g * HG:H0 + (g + 1) * HG, :]
                        nc.gpsimd.tensor_tensor(v, v, cf.rearrange("p h (o c) -> p h o c", o=1).to_broadcast([P, HG, L // 4, 4]),
                                                ALU.mult).then_inc(weighed_p.sem, 1)
                    rsqrt()
                else:
                    skip(pool, weighed_p, b, 0, 2)
                    skip(pool, rstd_ready, b, 0, 2)
                    n_rstd[0] += 2
                    rsqrt()
                if ahead:
                    for k in range(KD):
                        pool.wait_ge(*((kraw.sem, kraw.at(b, 1)) if k == 0 else (pd.empty.sem, pd.empty.at(b, PD_K0))))
                        if k == 0 and main:
                            pool.wait_ge(pa.full.sem, pa.full.at(b, 0))
                        pool.sem_inc(spare, 1)
                        for h in range(G0):
                            ins = nc.gpsimd.tensor_scalar(kpad0[:, k * G0 + h, :], kT0[:, k, :], c("head")[:, h:h + 1], 1.0,
                                                          ALU.mult, ALU.mult)
                        ins.then_inc(kpadded.sem, 1)
                else:
                    skip(pool, kpadded, b, 0, KD)
                if main:
                    n = 0
                    for t in range(T):
                        for ci, (f0, fn) in enumerate(CH0[:2]):
                            n += 1
                            pool.wait_ge(pd.empty.sem, pd.empty.at(b, PD_U + t * 3 + ci))
                            pool.wait_ge(comb_ready.sem, comb_ready.at(b, 1))
                            v = hid[:, t, f0:f0 + fn].rearrange("p (e m) -> p e m", m=M0R)
                            ne = fn // M0R
                            cw = comb[:, t, f0 // M0R:f0 // M0R + ne]
                            nc.gpsimd.tensor_tensor(v, v, cw.rearrange("p (e o) -> p e o", o=1).to_broadcast([P, ne, M0R]),
                                                    ALU.mult).then_inc(hid_weighed.sem, 1)
                    rsqrt()
                else:
                    skip(pool, hid_weighed, b, 0, 4)
                for i in range(N_S1):
                    if main:
                        pool.wait_ge(recip1.sem, recip1.at(b, i + 1))
                        pool.sem_inc(spare, 1)
                        for h in range(2):
                            ins = nc.gpsimd.tensor_scalar(p1[:, i % 4, h, :], p1[:, i % 4, h, :], r1[:, i % 4, h:h + 1], 1.0,
                                                          ALU.mult, ALU.mult)
                        ins.then_inc(p1_ready.sem, 1)
                    if main and i == AHEAD_NORM + 1:
                        if ahead:
                            rsqrt()
                        else:
                            skip(pool, rstd_ready, b, 2, 1)
                            n_rstd[0] += 1
                if main:
                    rsqrt()
                else:
                    skip(pool, p1_ready, b, 0, N_S1)
                    skip(pool, rstd_ready, b, 3, 1)
                    pool.wait_ge(w0_loaded, 16)
                if ahead:
                    pool.wait_ge(pd.empty.sem, pd.empty.at(b, PD_O1))
                    if not main:
                        pool.wait_ge(x_loaded.sem, x_loaded.at(b, 16))
                    nc.gpsimd.tensor_tensor(xb[:, :, :], x_in[:, :, :], bo0.rearrange("p (o n) -> p o n", o=1).to_broadcast([P, T, D]), ALU.add).then_inc(x_used.sem, 1)
                if not main:
                    return
                pool.wait_ge(pos_ready.sem, pos_ready.at(b, 1))
                pool.wait_ge(pay_copied.sem, pay_copied.at(b, 1))
                pool.sem_inc(spare, 1)
                for t in range(T):
                    for k in range(TOP):
                        pool.indirect_dma_start(rows, bass.IndirectOffsetOnAxis(ap=pos[:, t, k:k + 1], axis=0),
                                                pay[:, t, k, :], None).then_inc(scattered.sem, 16)

            pool.dma_start(tok[:, :], tok0).then_inc(scattered.sem, 16)
            nc.gpsimd.memset(vpad0[:, :, :, :], 0.0).then_inc(pads, 1)
            nc.gpsimd.memset(kpad1[:, :, :], 0.0).then_inc(pads, 1)
            pool.wait_ge(c_loaded, 32)
            batch(-1, main=False)
            nc.gpsimd.memset(vpad1[:, :, :, :], 0.0).then_inc(pads, 1)
            with pool.Fori(0, B - 1) as b:
                batch(b)
            batch(B - 1, ahead=False)
            pool.wait_ge(scattered.sem, 16 * T * TOP * B + 16)

        @block.scalar
        def _(act):
            def batch(b, main=True, ahead=True):
                tra, proda = Turn(act, ta, b), Turn(act, pa, b)

                def copy_turned(dst):
                    src = tra.take()
                    nc.scalar.activation(dst, src[:, 0:512].rearrange("p (a n) -> p a n", n=dst.shape[-1]), ACT.Copy).then_inc(ta.empty.sem, 1)

                def copy_p1(i):
                    pair, t = i // 2, i % 2
                    src = tra.take()
                    if pair >= 2:
                        act.wait_ge(pd.full.sem, pd.full.at(b, PD_AV1 + pair - 2))
                    nc.scalar.activation(pT1[:, pair % 2, :, :, t * P:(t + 1) * P],
                                         src[:, :].rearrange("p (k h n) -> p k h n", k=2, h=2), ACT.Copy).then_inc(ta.empty.sem, 1)

                def attention1(i):
                    src = proda.take()
                    act.wait_ge(maxed.sem, maxed.at(b, i + 1))
                    if i >= 4:
                        j = i - 4
                        r, n = (ta, ta_p1(j)) if j % 2 == 0 else (td, TD_P1 + j // 2)
                        act.wait_ge(r.full.sem, r.full.at(b, n))
                        act.wait_ge(recip1.sem, recip1.at(b, j + 1))
                    for h in range(2):
                        ins = nc.scalar.activation(p1[:, i % 4, h, :], src[:, h * L:(h + 1) * L], ACT.Exp,
                                                   bias=negm1[:, i % 4, h:h + 1], accum_out=z1[:, i % 4, h:h + 1])
                    ins.then_inc(pa.empty.sem, 1)

                def keys1(ring, m):
                    src = ring.take()
                    if m == 0 and main:
                        act.wait_ge(pa.full.sem, pa.full.at(b, PA_S0 - 1))
                    v = src[:, :].rearrange("p (m n) -> p m n", m=2)
                    kp = kpad1[:, :, :].rearrange("p (m e) n -> p m e n", e=2)
                    nc.scalar.activation(kp[0:64, m:m + 2, 0, :], v[0:64], ACT.Copy)
                    nc.scalar.activation(kp[64:P, m:m + 2, 1, :], v[64:P], ACT.Copy).then_inc(ring.ring.empty.sem, 1)

                def values1(t):
                    for half in range(2):
                        src = proda.take()
                        if t == 0 and half == 0:
                            act.wait_ge(pd.full.sem, pd.full.at(b, PD_AV7 - N_PD))
                        dst = vpad1[:, t, :, :].rearrange("p (m e) (f n) -> p m e f n", e=2, f=2)
                        v = src[:, :].rearrange("p (m e n) -> p m e n", e=2, n=DH1)
                        nc.scalar.activation(dst[:, half * 4:half * 4 + 4, 0, 0, :], v[:, :, 0, :], ACT.Copy)
                        nc.scalar.activation(dst[:, half * 4:half * 4 + 4, 1, 1, :], v[:, :, 1, :], ACT.Copy).then_inc(pa.empty.sem, 1)

                def exps0(i):
                    src = proda.take()
                    act.wait_ge(maxed.sem, maxed.at(b, N_S1 + i + 1))
                    if i == 0 or i == H0 // HG:
                        act.wait_ge(pd.full.sem, pd.full.at(b, PD_O1))
                    t, nh = (0, HG) if i < H0 // HG else (1, 2)
                    h0 = i * HG if t == 0 else (i - H0 // HG) * 2
                    for h in range(nh):
                        e = e0a[:, h0 + h, :] if t == 0 else e0b[:, h0 + h, :]
                        n = (t + 1) * P
                        ins = nc.scalar.activation(e, src[:, h * n:(h + 1) * n], ACT.Exp, bias=negm0[:, t, h0 + h:h0 + h + 1],
                                                   accum_out=sums[:, 0, t * H0 + h0 + h:t * H0 + h0 + h + 1])
                    ins.then_inc(pa.empty.sem, 1)

                if main:
                    for m in range(2, I1T, 2):
                        keys1(proda, m)
                    values1(0)
                    for i in range(0, 12, 2):
                        g, seg = i // 3, i % 3
                        if g >= 2:
                            r, n = (av0_used, 1) if g == 2 else (pd.full, PD_AV0)
                            act.wait_ge(r.sem, r.at(b, n))
                        dst = pT0b[:, g % 2] if seg == 2 else pT0a[:, g % 2, :, seg * P:(seg + 1) * P]
                        src = proda.take()
                        nc.scalar.activation(dst, src[:, :].rearrange("p (a n) -> p a n", n=P), ACT.Copy).then_inc(pa.empty.sem, 1)
                    proda.skip(pa.empty, 3)
                    act.wait_ge(pd.full.sem, pd.full.at(b, PD_Q0 - N_PD))
                    src = tra.take()
                    nc.scalar.activation(xnT[:, 0, :], src[:, 0:L], ACT.Copy).then_inc(ta.empty.sem, 1)
                    act.wait_ge(pd.empty.sem, pd.empty.at(b, PD_ROUTER))
                    nc.scalar.activation(pr[:, :, :], lg[:, :, :], ACT.Exp).then_inc(lexp.sem, 1)
                    def silu(i):
                        t, (f0, fn) = i // 3, CH0[i % 3]
                        src = proda.take()
                        if i >= 2:
                            act.wait_ge(pd.empty.sem, pd.empty.at(b, PD_U + i - 2))
                        nc.scalar.activation(hs[:, i % 2, 0:fn], src[:, 0:fn], ACT.Silu).then_inc(pa.empty.sem, 1)

                    def copy_hid(i):
                        t, (f0, fn) = i // 3, CH0[i % 3]
                        src = tra.take()
                        nf = fn // P
                        nc.scalar.activation(hidT[:, f0 // P:f0 // P + nf, t * P:(t + 1) * P],
                                             src[:, 0:fn].rearrange("p (f n) -> p f n", n=P), ACT.Copy).then_inc(ta.empty.sem, 1)

                    for i in range(5):
                        silu(i)
                    copy_hid(1)
                    silu(5)
                    copy_hid(3)
                    nc.scalar.activation(junk[:, :], w("gate"), ACT.Exp)
                    copy_hid(5)
                    src = tra.take()
                    act.wait_ge(pa.full.sem, pa.full.at(b, PA_G + 5))
                    act.wait_ge(pd.full.sem, pd.full.at(b, PD_U + 5))
                    nc.scalar.activation(xnT[:, 0, :], src[:, 0:L], ACT.Identity, bias=beta[:, 0:1], scale=gamma[:, 0:1]).then_inc(ta.empty.sem, 1)
                    values1(1)
                    for _k in range(2):
                        src = proda.take()
                        nc.scalar.activation(qT1[:, 4 * _k:4 * _k + 2, :], src[:, :].rearrange("p (m n) -> p m n", m=2),
                                             ACT.Copy, scale=DH1 ** -0.5).then_inc(pa.empty.sem, 1)
                else:
                    proda.skip(pa.empty, PA_S1 - 1)
                    tra.skip(ta.empty, ta_p1(0) - 1)
                    skip(act, lexp, b, 0, 1)

                for i in range(N_S1 + 3):
                    if i < N_S1 and main:
                        attention1(i)
                    if i == AHEAD_TURN:
                        if not main:
                            proda.skip(pa.empty, N_S1)
                            tra.skip(ta.empty, 6)
                        if ahead:
                            if main:
                                act.wait_ge(pd.full.sem, pd.full.at(b, PD_Q1 + 1))
                                act.wait_ge(pa.full.sem, pa.full.at(b, PA_Q1 + 1))
                            copy_turned(xnT[:, :, :])
                        else:
                            tra.skip(ta.empty, 1)
                    if i >= 3 and i % 2 == 1 and main:
                        copy_p1(i - 3)
                if main:
                    act.wait_ge(pd.empty.sem, pd.empty.at(b, PD_O1))
                    act.dma_start(tokens_rows[bass.ds(b, 1)].rearrange("b (t p) d -> p (b t) d", p=P), x1[:, :, :]).then_inc(stored.sem, 16)
                else:
                    skip(act, stored, b, 0, 16)
                    tra.skip(ta.empty, 3)
                    skip(act, lexp, b, 1, 1)
                    skip(act, pay_copied, b, 0, 1)
                for i in range(N_S0 + 1):
                    if ahead and i == KEYS_COPY_AT:
                        if not main:
                            act.wait_ge(pads, 2)
                        keys1(tra, 0)
                    if ahead and i < N_S0:
                        exps0(i)
                    if i == 0 and main:
                        act.wait_ge(pd.full.sem, pd.full.at(b, PD_Q0))
                        src = tra.take()
                        nc.scalar.activation(xnT[:, 0, :], src[:, 0:L], ACT.Copy).then_inc(ta.empty.sem, 1)
                    if i == 1 and main:
                        act.wait_ge(pd.empty.sem, pd.empty.at(b, PD_LOGIT))
                        nc.scalar.activation(pr[:, :, 0:E1N], lg[:, :, 0:E1N], ACT.Exp).then_inc(lexp.sem, 1)
                        act.wait_ge(normed.sem, normed.at(b, 4))
                        nc.scalar.activation(pay[:, :, 1, 0:D], pay[:, :, 0, 0:D], ACT.Copy).then_inc(pay_copied.sem, 1)
                if ahead:
                    nc.scalar.activation(expnm[:, :], negm0[:, :, :].rearrange("p t h -> p (t h)"), ACT.Exp).then_inc(guard_exp.sem, 1)
                    assert (tra.n, proda.n) == (N_TA, N_PA), (tra.n, proda.n)

            act.wait_ge(w0_loaded, 16)
            nc.scalar.activation(tgate[:, :], w("gate"), ACT.Tanh).then_inc(setup_act, 1)
            batch(-1, main=False)
            act.wait_ge(pads, 3)
            act.wait_ge(w_loaded, 32)
            with act.Fori(0, B - 1) as b:
                batch(b)
            batch(B - 1, ahead=False)
            act.wait_ge(pad_loaded, 16)
            act.wait_ge(tail_ready, 1)
            for e in range(E1N // 2, E1N):
                at = act.value_load(tail_i[0:1, e:e + 1], min_val=0, max_val=E1N * CAP - P)
                act.dma_start(rows[bass.ds(at, P), :], pad).then_inc(tails, 16)
            act.wait_ge(stored.sem, 16 * (B + 1))

        @block.vector
        def _(dve):
            def batch(b, main=True, ahead=True):
                trd, prodd, score = Turn(dve, td, b), Turn(dve, pd, b), Turn(dve, pa, b)
                n_step, n_rstd, n_l = [0], [0], [0]

                def then(ins, meanwhile=None):
                    n_step[0] += 1
                    ins.then_inc(step.sem, 1)
                    if meanwhile is not None:
                        meanwhile()
                    dve.wait_ge(step.sem, step.at(b, n_step[0]))

                def apart():
                    dve.sem_inc(spare, 1)

                def release(ins, place):
                    ins.then_inc(place.ring.empty.sem, 1)
                    dve.wait_ge(place.ring.empty.sem, place.ring.empty.at(b, place.n))

                def norm_sums(src):
                    nc.vector.bn_stats(stats[:, 0, :], src[:, 0, :])
                    then(nc.vector.bn_stats(stats[:, 1, :], src[:, 1, :]))

                def norm_var(twice=False):
                    apart()
                    nc.vector.bn_aggr(mv[:, 0, :], stats[:, 0, :])
                    then(nc.vector.bn_aggr(mv[:, 1, :], stats[:, 1, :]))
                    if twice:
                        ins = nc.vector.tensor_scalar(vpe[:, :], mv[:, :, 1], 1 + EPS, EPS * EPS, ALU.mult, ALU.add)
                    else:
                        ins = nc.vector.tensor_scalar(vpe[:, :], mv[:, :, 1], EPS, None, ALU.add)
                    ins.then_inc(var_ready.sem, 1)
                    n_rstd[0] += 1

                def norm_scale(src, dst, t):
                    if t == 0:
                        dve.wait_ge(rstd_ready.sem, rstd_ready.at(b, n_rstd[0]))
                    return nc.vector.tensor_scalar(dst[:, t, :], src[:, t, :], mv[:, t, 0:1], rstd[:, t:t + 1], ALU.subtract, ALU.mult)

                def norm(src, dst, signal_, meanwhile=None, twice=False):
                    norm_sums(src)
                    norm_var(twice)
                    if meanwhile is not None:
                        meanwhile()
                    for t in range(T):
                        ins = norm_scale(src, dst, t)
                    ins.then_inc(signal_.sem, 1)

                def choose(n_experts, eps, meanwhile=(None,) * 5):
                    n_l[0] += 1
                    src = prodd.take()
                    v = src[:, 0:T * n_experts].rearrange("p (t e) -> p t e", t=T)
                    then(nc.vector.tensor_reduce(lnm[:, :], v, AX.X, ALU.max, negate=True))
                    release(nc.vector.tensor_tensor(lg[:, :, 0:n_experts], v, lnm[:, :].rearrange("p (t o) -> p t o", o=1).to_broadcast([P, T, n_experts]), ALU.add), prodd)
                    if meanwhile[0] is not None:
                        meanwhile[0]()
                    dve.wait_ge(lexp.sem, lexp.at(b, n_l[0]))
                    p = pr[:, :, 0:n_experts]
                    then(nc.vector.tensor_reduce(lsum[:, :], p, AX.X, ALU.add))
                    then(nc.vector.reciprocal(lsum[:, :], lsum[:, :]), meanwhile[1])
                    then(nc.vector.tensor_tensor(p, p, lsum[:, :].rearrange("p (t o) -> p t o", o=1).to_broadcast([P, T, n_experts]), ALU.mult))
                    apart()
                    nc.vector.max(top8[:, 0, :], pr[:, 0, 0:n_experts])
                    then(nc.vector.max(top8[:, 1, :], pr[:, 1, 0:n_experts]), meanwhile[2])
                    apart()
                    nc.vector.max_index(idx8[:, 0, :], top8[:, 0, :], pr[:, 0, 0:n_experts])
                    then(nc.vector.max_index(idx8[:, 1, :], top8[:, 1, :], pr[:, 1, 0:n_experts]), meanwhile[3])
                    nc.vector.tensor_copy(idxf[:, :, :], idx8[:, :, 0:TOP])
                    then(nc.vector.tensor_reduce(wsum[:, :], top8[:, :, 0:TOP], AX.X, ALU.add))
                    if eps:
                        then(nc.vector.tensor_scalar(wsum[:, :], wsum[:, :], eps, None, ALU.add))
                    then(nc.vector.reciprocal(wsum[:, :], wsum[:, :]))
                    then(nc.vector.tensor_tensor(wtop[:, :, :], top8[:, :, 0:TOP], wsum[:, :].rearrange("p (t o) -> p t o", o=1).to_broadcast([P, T, TOP]), ALU.mult), meanwhile[4])

                def copy_turned(dst, n=512, inner=P):
                    src = trd.take()
                    v = src[:, 0:n]
                    v = v.rearrange("p (a n) -> p a n", n=inner) if len(dst.shape) == 3 else v.rearrange("p (k h n) -> p k h n", k=2, h=2)
                    nc.vector.tensor_copy(dst, v).then_inc(td.empty.sem, 1)

                def keys0():
                    if not ahead:
                        prodd.skip(pd.empty, 1)
                        skip(dve, kraw, b, 0, 1)
                        return
                    src = prodd.take()
                    if main:
                        dve.wait_ge(kpadded.sem, kpadded.at(b, 0))
                    for k, done in enumerate((kraw, pd.empty)):
                        nc.vector.tensor_scalar(kT0[:, k, :], src[:, k * L:(k + 1) * L], bk0[:, k:k + 1], None, ALU.add).then_inc(done.sem, 1)

                def values0():
                    if not ahead:
                        prodd.skip(pd.empty, 1)
                        return
                    src = prodd.take()
                    if not main:
                        dve.wait_ge(pads, 1)
                    for t in range(T):
                        for k in range(KD):
                            dst = vpad0[:, t, k * G0:(k + 1) * G0, :].rearrange("p h (g n) -> p (h g) n", n=DH0)[:, 0:G0 * G0:G0 + 1, :]
                            v = src[:, t * D + k * P:t * D + (k + 1) * P].rearrange("p (h n) -> p h n", n=DH0)
                            bias = bv0[:, k * P:(k + 1) * P].rearrange("p (h n) -> p h n", n=DH0)
                            ins = nc.vector.tensor_tensor(dst, v, bias, ALU.add)
                    ins.then_inc(pd.empty.sem, 1)

                def queries0():
                    if not ahead:
                        prodd.skip(pd.empty, 1)
                        return
                    src = prodd.take()
                    for k in range(KD):
                        ins = nc.vector.tensor_scalar(qT0[:, k, :], src[:, k * L:(k + 1) * L], bq0[:, k:k + 1], DH0 ** -0.5, ALU.add, ALU.mult)
                    ins.then_inc(pd.empty.sem, 1)

                def av1(pair):
                    src = prodd.take()
                    nc.vector.tensor_copy(avT1[:, pair, :], src[:, 0:L]).then_inc(pd.empty.sem, 1)

                def recip(j):
                    dve.wait_ge(pa.empty.sem, pa.empty.at(b, PA_S1 + j))
                    if j >= 4:
                        dve.wait_ge(p1_ready.sem, p1_ready.at(b, j - 3))
                    nc.vector.reciprocal(r1[:, j % 4, :], z1[:, j % 4, :]).then_inc(recip1.sem, 1)

                def max1(i):
                    src = score.take()
                    if i >= 4:
                        dve.wait_ge(pa.empty.sem, pa.empty.at(b, PA_S1 + i - 4))
                    nc.vector.tensor_reduce(negm1[:, i % 4, :], src[:, :].rearrange("p (h n) -> p h n", h=2), AX.X, ALU.max,
                                            negate=True).then_inc(maxed.sem, 1)

                def heads0(i):
                    t, nh = (0, HG) if i < H0 // HG else (1, 2)
                    return t, nh, i * HG if t == 0 else (i - H0 // HG) * 2

                def max0(i):
                    src = score.take()
                    t, nh, h0 = heads0(i)
                    nc.vector.tensor_reduce(negm0[:, t, h0:h0 + nh], src[:, :].rearrange("p (h n) -> p h n", h=nh), AX.X, ALU.max,
                                            negate=True).then_inc(maxed.sem, 1)

                def sums0(i):
                    t, nh, h0 = heads0(i)
                    dve.wait_ge(pa.empty.sem, pa.empty.at(b, PA_S0 + i))
                    for r, dil in ((1, 2), (2, 4)):
                        v = (e0a, e0b)[t][:, h0:h0 + nh, :].rearrange("p h (k c) -> p h k c", c=dil)[:, :, :, h0 // (H0 // dil)]
                        ins = nc.vector.tensor_reduce(sums[:, r, t * H0 + h0:t * H0 + h0 + nh], v, AX.X, ALU.add)
                    return ins

                io = c("iota")
                if main:
                    dve.wait_ge(guard_exp.sem, guard_exp.at(b, 0))
                    bc = lambda ap: ap.rearrange("p (o n) -> p o n", o=1).to_broadcast([P, NBR, T * H0])
                    then(nc.vector.tensor_tensor(keep[:, :, :], sums[:, :, :], bc(expnm[:, :]), ALU.not_equal))
                    nc.vector.tensor_scalar(coef[:, :, :], sums[:, :, :], 1e-30, float(NBR), ALU.max, ALU.mult)
                    then(nc.vector.tensor_tensor(keep[:, :, :], keep[:, :, :], cover, ALU.mult))
                    then(nc.vector.tensor_tensor(ks[:, :, :], keep[:, :, :], sums[:, :, :], ALU.mult))
                    then(nc.vector.tensor_reduce(den[:, :], ks[:, :, :].rearrange("p r n -> p n r"), AX.X, ALU.add))
                    then(nc.vector.tensor_scalar(isz[:, :], den[:, :], 0.0, None, ALU.is_equal))
                    then(nc.vector.tensor_tensor(den[:, :], den[:, :], isz[:, :], ALU.add))
                    nc.vector.reciprocal(rden[:, :], den[:, :])
                    then(nc.vector.reciprocal(ks[:, :, :], coef[:, :, :]))
                    nc.vector.tensor_tensor(coef[:, :, :], keep[:, :, :], bc(rden[:, :]), ALU.mult)
                    then(nc.vector.tensor_tensor(ks[:, :, :], ks[:, :, :], bc(isz[:, :]), ALU.mult))
                    then(nc.vector.tensor_tensor(ks[:, :, :], ks[:, :, :], cover, ALU.mult))
                    then(nc.vector.tensor_tensor(coef[:, :, :], coef[:, :, :], ks[:, :, :], ALU.add))
                    c4 = lambda r: coef[:, r, :].rearrange("p (t h o) -> p t h o", t=T, o=1).to_broadcast([P, T, H0, 4])
                    c2 = lambda ap: ap.rearrange("p (t h) c -> p t h c", t=1).to_broadcast([P, T, H0, 4])
                    ct = lambda ap: ap.rearrange("p (t h) c -> p t h c", t=T)
                    nc.vector.tensor_tensor(ct(cfa), c2(class2), c4(1), ALU.mult)
                    then(nc.vector.tensor_tensor(ct(cfb), c2(class4), c4(2), ALU.mult))
                    then(nc.vector.tensor_tensor(cfa, cfa, cfb, ALU.add))
                    nc.vector.tensor_tensor(ct(cfa), ct(cfa), c4(0), ALU.add).then_inc(coef_ready.sem, 1)
                    dve.wait_ge(coef_ready.sem, coef_ready.at(b, 1))

                    def weigh(t, g):
                        for k in range(t + 1):
                            v = (e0a, e0b)[t][:, g * HG:(g + 1) * HG, k * P:(k + 1) * P].rearrange("p h (k c) -> p h k c", c=4)
                            cf = cfa[:, t * H0 + g * HG:t * H0 + (g + 1) * HG, :]
                            nc.vector.tensor_tensor(v, v, cf.rearrange("p h (o c) -> p h o c", o=1).to_broadcast([P, HG, P // 4, 4]),
                                                    ALU.mult).then_inc(weighed_d.sem, 1)

                    def copy_p0(i):
                        g, seg = i // 3, i % 3
                        if g >= 2:
                            r, n = (av0_used, 1) if g == 2 else (pd.full, PD_AV0)
                            dve.wait_ge(r.sem, r.at(b, n))
                        copy_turned(pT0b[:, g % 2] if seg == 2 else pT0a[:, g % 2, :, seg * P:(seg + 1) * P])

                    weigh(0, 0)
                    weigh(1, 0)
                    weigh(0, 1)
                    copy_p0(1)
                    weigh(1, 1)
                    copy_p0(3)
                    weigh(0, 2)
                    weigh(0, 3)
                    def av0(k):
                        src = prodd.take()
                        nc.vector.tensor_copy(avT0[:, k, :], src[:, 0:L]).then_inc(pd.empty.sem, 1)

                    for i in range(5, 12, 2):
                        copy_p0(i)
                        if i == 7:
                            av0(0)
                    av0(1)
                    src = prodd.take()
                    dve.wait_ge(stored.sem, stored.at(b, 0))
                    dve.wait_ge(x_used.sem, x_used.at(b, 0))
                    release(nc.vector.tensor_tensor(x1[:, :, :], src[:, :].rearrange("p (t n) -> p t n", t=T), xb[:, :, :], ALU.add), prodd)
                    norm(x1, xn, normed, keys0)
                    dve.wait_ge(pd.full.sem, pd.full.at(b, PD_Q0 - N_PD))
                    src = trd.take()
                    nc.vector.tensor_copy(xnT[:, 1, :], src[:, 0:L]).then_inc(td.empty.sem, 1)
                    values0()
                    choose(E0N, 1e-9)
                    for t in range(T):
                        nc.vector.tensor_scalar(comb[:, t, :], io, idxf[:, t, 0:1], wtop[:, t, 0:1], ALU.is_equal, ALU.mult)
                        ins = nc.vector.tensor_scalar(comb2[:, t, :], io, idxf[:, t, 1:2], wtop[:, t, 1:2], ALU.is_equal, ALU.mult)
                    then(ins)
                    nc.vector.tensor_tensor(comb[:, :, :], comb[:, :, :], comb2[:, :, :], ALU.add).then_inc(comb_ready.sem, 1)
                    def product(i):
                        t, (f0, fn) = i // 3, CH0[i % 3]
                        src = prodd.take()
                        dve.wait_ge(pa.empty.sem, pa.empty.at(b, PA_G + i))
                        nc.vector.tensor_tensor(hid[:, t, f0:f0 + fn], src[:, 0:fn], hs[:, i % 2, 0:fn], ALU.mult).then_inc(pd.empty.sem, 1)

                    def copy_hid(i):
                        t, (f0, fn) = i // 3, CH0[i % 3]
                        copy_turned(hidT[:, f0 // P:(f0 + fn) // P, t * P:(t + 1) * P], fn)

                    for i in range(4):
                        product(i)
                    copy_hid(0)
                    product(4)
                    product(5)
                    copy_hid(2)
                    copy_hid(4)
                    src = prodd.take()
                    release(nc.vector.tensor_tensor(x1[:, :, :], src[:, :].rearrange("p (t n) -> p t n", t=T), x1[:, :, :], ALU.add), prodd)
                    norm(x1, xn, normed, twice=True)
                    src = trd.take()
                    nc.vector.tensor_scalar(xnT[:, 1, :], src[:, 0:L], gamma[:, 1:2], beta[:, 1:2], ALU.mult, ALU.add).then_inc(td.empty.sem, 1)
                    nc.vector.tensor_tensor(xb[:, :, :], x1[:, :, :], gbo1.rearrange("p (o n) -> p o n", o=1).to_broadcast([P, T, D]), ALU.add)
                    for _k in range(2):
                        src = prodd.take()
                        nc.vector.tensor_scalar(qT1[:, 4 * _k + 2:4 * _k + 4, :], src[:, :].rearrange("p (m n) -> p m n", m=2),
                                                DH1 ** -0.5, None, ALU.mult).then_inc(pd.empty.sem, 1)
                else:
                    prodd.skip(pd.empty, PD_K0 - 1)
                    for signal_ in (var_ready, normed):
                        skip(dve, signal_, b, 0, 2)
                    n_rstd[0] += 2
                    dve.wait_ge(x_loaded.sem, x_loaded.at(b, 16))
                    norm(x_in, xn, normed)
                    dve.wait_ge(w0_loaded, 16)
                    keys0()
                    values0()
                    prodd.skip(pd.empty, PD_AV1 - PD_V0 - 1)
                    trd.skip(td.empty, N_TD)
                    for signal_, n in ((coef_ready, 1), (weighed_d, HG + 4), (comb_ready, 1), (recip1, N_S1), (maxed, N_S1)):
                        skip(dve, signal_, b, 0, n)
                score.n = PA_S1 - 1

                for i in range(N_S1 + 4):
                    if main:
                        if i % 2 == 1 and i <= N_S1:
                            recip(i - 1)
                        if i < N_S1:
                            max1(i)
                        if i % 2 == 0 and 1 <= i <= N_S1:
                            recip(i - 1)
                    if not main:
                        continue
                    if i == AHEAD_NORM - 2:
                        if ahead:
                            dve.wait_ge(x_loaded.sem, x_loaded.at(b, 16))
                            norm_sums(x_in)
                    if i == AHEAD_NORM:
                        if ahead:
                            norm_var()
                        else:
                            skip(dve, var_ready, b, 2, 1)
                            n_rstd[0] += 1
                    if i == AHEAD_NORM + 2:
                        if ahead:
                            norm_scale(x_in, xn, 0)
                    if i == AHEAD_NORM + 3:
                        if ahead:
                            norm_scale(x_in, xn, 1).then_inc(normed.sem, 1)
                        else:
                            skip(dve, normed, b, 2, 1)
                    if i >= 4 and i % 2 == 0 and i - 3 < N_S1:
                        j = i - 3
                        pair = j // 2
                        if pair >= 2:
                            dve.wait_ge(pd.full.sem, pd.full.at(b, PD_AV1 + pair - 2))
                        copy_turned(pT1[:, pair % 2, :, :, (j % 2) * P:(j % 2 + 1) * P])
                    if i >= 7 and i % 2 == 1 and (i - 7) // 2 < I1T - 1:
                        if (i - 7) // 2 == I1T - 2:
                            queries0()
                        av1((i - 7) // 2)
                if not main:
                    prodd.skip(pd.empty, I1T - 2)
                    queries0()
                score.n = PA_S0 - 1
                if main:
                    av1(I1T - 1)
                    src = prodd.take()
                    release(nc.vector.scalar_tensor_tensor(out=x1[:, :, :], in0=src[:, :].rearrange("p (t n) -> p t n", t=T), scalar=tgate[:, 0:1],
                                                           in1=xb[:, :, :], op0=ALU.mult, op1=ALU.add), prodd)
                    dve.wait_ge(scattered.sem, scattered.at(b, 0))
                    norm(x1, pay[:, :, 0, 0:D], normed, (lambda: max0(0)) if ahead else None)
                    if ahead:
                        max0(1)
                else:
                    prodd.skip(pd.empty, 3)
                    max0(0)
                    max0(1)
                    for signal_, done in ((normed, 3), (var_ready, 3), (both_ready, 0), (pos_ready, 0)):
                        skip(dve, signal_, b, done, 1)
                if ahead:
                    max0(2)
                if main:
                    src = trd.take()
                    nc.vector.tensor_copy(xnT[:, 1, :], src[:, 0:L]).then_inc(td.empty.sem, 1)
                    choose(E1N, 0.0, (lambda: max0(3), lambda: sums0(0), lambda: max0(4), lambda: sums0(1), lambda: max0(5)) if ahead else (None,) * 5)
                    for t in range(T):
                        for k in range(TOP):
                            ins = nc.vector.tensor_scalar(hot[:, t, k, :], io[:, 0:E1N], idxf[:, t, k:k + 1], None, ALU.is_equal)
                    then(ins)
                    nc.vector.tensor_tensor(both[:, :, :], hot[:, :, 0, :], hot[:, :, 1, :], ALU.add).then_inc(both_ready.sem, 1)
                    payi = pay[:, :, :, :].bitcast(I32)
                    for k in range(TOP):
                        nc.vector.tensor_copy(pay[:, :, k, D], wtop[:, :, k])
                        then(nc.vector.tensor_copy(payi[:, :, k, D + 1], tok[:, :]))
                    then(nc.vector.tensor_scalar(tok[:, :], tok[:, :], L, None, ALU.add))

                def place():
                    src = prodd.take()
                    then(nc.vector.tensor_tensor(rank[:, :, :], src[:, 0:T * E1N].rearrange("p (t e) -> p t e", t=T),
                                                 run[:, :].rearrange("p (o e) -> p o e", o=1).to_broadcast([P, T, E1N]), ALU.add))
                    for k in range(TOP):
                        ins = nc.vector.tensor_tensor(hotr[:, :, k, :], hot[:, :, k, :], rank[:, :, :], ALU.mult)
                    then(ins)
                    nc.vector.tensor_tensor(run[:, :], src[:, T * E1N:(T + 1) * E1N], run[:, :], ALU.add).then_inc(pd.empty.sem, 1)
                    then(nc.vector.tensor_reduce(posf[:, :, :], hotr[:, :, :, :], AX.X, ALU.add))
                    nc.vector.tensor_copy(pos[:, :, :], posf[:, :, :]).then_inc(pos_ready.sem, 1)

                if not main:
                    max0(3)
                    sums0(0)
                    max0(4)
                    sums0(1)
                    max0(5)
                for i in range(N_S0 + 2):
                    if ahead and 6 <= i < N_S0:
                        max0(i)
                    if main and i == RANK_AFTER + 1:
                        place()
                    if ahead and i >= 4:
                        ins = sums0(i - 2)
                if ahead:
                    then(ins)
                if main:
                    prodd.skip(pd.empty, 1)
                if main and ahead:
                    assert (trd.n, prodd.n) == (N_TD, N_PD), (trd.n, prodd.n)
                    assert n_step[0] == N_STEP, n_step
                if not main:
                    prodd.skip(pd.empty, 3)
                    skip(dve, step, b, n_step[0], N_STEP - n_step[0])

            batch(-1, main=False)
            dve.wait_ge(c_loaded, 32)
            dve.wait_ge(setup_act, 1)
            nc.vector.tensor_scalar(gbo1, bo1, tgate[:, 0:1], None, ALU.mult).then_inc(setup_dve, 1)
            nc.vector.tensor_copy(run[:, :], c("region")).then_inc(setup_dve, 1)
            dve.wait_ge(setup_dve, 2)
            dve.wait_ge(pads, 3)
            with dve.Fori(0, B - 1) as b:
                batch(b)
            batch(B - 1, ahead=False)
            dve.wait_ge(pd.empty.sem, pd.empty.at(B - 1, N_PD))
            nc.vector.tensor_tensor(counts, run[:, :], c("region"), ALU.subtract).then_inc(setup_dve, 1)
            dve.wait_ge(setup_dve, 3)
            n = [0]

            def then(ins):
                n[0] += 1
                ins.then_inc(chain, 1)
                dve.wait_ge(chain, n[0])

            then(nc.vector.tensor_scalar(fl, counts, float(P - 1), None, ALU.add))
            then(nc.vector.tensor_copy(cnt_i, fl))
            nc.vector.tensor_tensor(fl, counts, c("region"), ALU.add)
            then(nc.vector.tensor_single_scalar(cnt_i, cnt_i, 7, ALU.arith_shift_right))
            nc.vector.tensor_copy(tail_i, fl).then_inc(tail_ready, 1)
            then(nc.vector.tensor_copy(nb, cnt_i))
            then(nc.vector.tensor_tensor(upto[:, :, :], nb.rearrange("p (o e) -> p o e", o=1).to_broadcast([P, E1N, E1N]),
                                         c("upto").rearrange("p (n e) -> p n e", e=E1N), ALU.mult))
            then(nc.vector.tensor_reduce(cum, upto[:, :, :], AX.X, ALU.add))
            row = lambda ap: ap.rearrange("p (o e) -> p o e", o=1).to_broadcast([P, N, E1N])
            then(nc.vector.tensor_tensor(le[:, :, :], row(cum), c("blocks").rearrange("p (n o) -> p n o", o=1).to_broadcast([P, N, E1N]), ALU.is_le))
            nc.vector.tensor_tensor(le2[:, :, :], le[:, :, :], row(nb), ALU.mult)
            then(nc.vector.tensor_reduce(eid, le[:, :, :], AX.X, ALU.add))
            nc.vector.tensor_scalar(rowf, eid, float(CAP), None, ALU.mult)
            then(nc.vector.tensor_reduce(tmp, le2[:, :, :], AX.X, ALU.add))
            then(nc.vector.tensor_tensor(tmp, c("blocks"), tmp, ALU.subtract))
            then(nc.vector.tensor_scalar(tmp, tmp, float(P), None, ALU.mult))
            then(nc.vector.tensor_tensor(rowf, rowf, tmp, ALU.add))
            then(nc.vector.tensor_scalar(rowf, rowf, float(E1N * CAP), None, ALU.min))
            nc.vector.tensor_copy(row_i, rowf)
            then(nc.vector.tensor_scalar(eid, eid, float(E1N - 1), None, ALU.min))
            then(nc.vector.tensor_copy(eid_i, eid))

        @block.tensor
        def _(pe):
            mm = nc.tensor.matmul

            def batch(b, main=True, ahead=True):
                tra, trd, prodd, proda = (Turn(pe, r, b) for r in (ta, td, pd, pa))

                def turn(ring, tiles):
                    dst = ring.claim()
                    for i, src in enumerate(tiles):
                        ins = nc.tensor.transpose(dst[:, i * P:(i + 1) * P], src, ident)
                    ins.then_inc(ring.ring.full.sem, 1)

                def turn_both(src, n_a, n_d):
                    for k, ring in enumerate((tra, trd)):
                        turn(ring, [src[:, t, k * P:(k + 1) * P] for t in range(T)])
                    pe.wait_ge(ta.empty.sem, ta.empty.at(b, n_a))
                    pe.wait_ge(td.empty.sem, td.empty.at(b, n_d))

                def features_out(ring, wk, xT, ms):
                    dst = ring.claim()
                    for i, m in enumerate(ms):
                        for k in range(KD):
                            ins = mm(dst[:, i * L:(i + 1) * L], wk[:, k, m * P:(m + 1) * P], xT[:, k, :], start=(k == 0), stop=(k == KD - 1))
                    ins.then_inc(ring.ring.full.sem, 1)

                def tokens_out(ring, xT, wk, nk, n, ts=range(T), c0=0, each_k=None):
                    dst = ring.claim()
                    for i, t in enumerate(ts):
                        for k in range(nk):
                            if each_k is not None and i == 0:
                                each_k(k)
                            ins = mm(dst[:, i * n:(i + 1) * n], xT[:, k, t * P:(t + 1) * P], wk[:, k, c0:c0 + n], start=(k == 0), stop=(k == nk - 1))
                    ins.then_inc(ring.ring.full.sem, 1)

                def turn_p0(g):
                    hh = range(g * HG, (g + 1) * HG)
                    for seg in range(3):
                        if seg == 0:
                            pe.wait_ge(weighed_d.sem, weighed_d.at(b, (1, 4, 7, 8)[g]))
                        elif g < 2:
                            pe.wait_ge(weighed_d.sem, weighed_d.at(b, (1, 4)[g] + seg))
                        elif seg == 1:
                            pe.wait_ge(weighed_p.sem, weighed_p.at(b, g - 1))
                        src = e0a if seg == 0 else e0b
                        k0 = P if seg == 2 else 0
                        turn((proda, trd)[(g * 3 + seg) % 2], [src[:, h, k0:k0 + P] for h in hh])

                def av_p0(g, dst):
                    last = 3 * g + 2
                    for i in (last - 1, last):
                        r, n = (pa, PA_P0 + i // 2) if i % 2 == 0 else (td, TD_P0 + i // 2)
                        pe.wait_ge(r.empty.sem, r.empty.at(b, n))
                    for i in range(HG):
                        h = g * HG + i
                        mm(dst[:, 0:L], vpad0[:, 0, h, :], pT0a[:, g % 2, i, :], start=(h % G0 == 0), stop=(h % G0 == G0 - 1), skip_group_check=True)
                        ins = mm(dst[:, P:L], vpad0[:, 1, h, :], pT0b[:, g % 2, i, :], start=False, stop=(h % G0 == G0 - 1), skip_group_check=True)
                    ins.then_inc((av0_used, pd.full)[g % 2].sem, 1)

                def av_p1(pair, dst):
                    for r, n in ((ta, ta_p1(2 * pair)), (td, TD_P1 + pair)):
                        pe.wait_ge(r.empty.sem, r.empty.at(b, n))
                    for e in range(2):
                        for k in range(T):
                            ins = mm(dst[:, 0:L], vpad1[:, k, 2 * pair + e, :], pT1[:, pair % 2, k, e, :],
                                     start=(e == 0 and k == 0), stop=(e == 1 and k == T - 1))
                    ins.then_inc(pd.full.sem, 1)

                def values1(t):
                    for half in range(2):
                        tokens_out(proda, ctx_in, wv1, KD, 512, ts=(t,), c0=half * 512)

                def scores0(i):
                    t, nh = (0, HG) if i < H0 // HG else (1, 2)
                    h0 = i * HG if t == 0 else (i - H0 // HG) * 2
                    k = h0 // G0
                    pe.wait_ge(kpadded.sem, kpadded.at(b, k + 1))
                    dst = proda.claim()
                    n = (t + 1) * P
                    v = dst[:, :].rearrange("p (h n) -> p h n", h=nh)
                    mm(v, qT0[:, k, t * P:(t + 1) * P], kpad0[:, h0:h0 + nh, 0:n], start=True, stop=True)
                    for h in range(nh):
                        ins = mm(v[:, h, t * P:(t + 1) * P], identb, causal, start=False, stop=True, skip_group_check=True)
                    ins.then_inc(pa.full.sem, 1)

                if main:
                    pe.wait_ge(ctx_loaded.sem, ctx_loaded.at(b, 0))
                    for m in range(2, I1T, 2):
                        features_out(proda, wk1, ctx_in, (m, m + 1))
                    values1(0)
                    turn_p0(0)
                    turn_p0(1)
                    dst = prodd.claim()
                    av_p0(0, dst)
                    turn_p0(2)
                    av_p0(1, dst)
                    turn_p0(3)
                    dst = prodd.claim()
                    av_p0(2, dst)
                    av_p0(3, dst)
                    proda.skip(pa.full, 3)
                    tokens_out(prodd, avT0, wo0, KD, D, each_k=lambda k: pe.wait_ge(pd.empty.sem, pd.empty.at(b, PD_AV0 + k)))
                else:
                    prodd.skip(pd.full, PD_K0 - 1)
                    tra.skip(ta.full, ta_p1(12) - 2)
                    proda.skip(pa.full, PA_S0 - 1)
                    trd.skip(td.full, N_TD)
                    skip(pe, av0_used, b, 0, 2)
                if ahead:
                    pe.wait_ge(ctx0_loaded.sem, ctx0_loaded.at(b, 16))
                    features_out(prodd, wk0, ctx0, (0, 1))
                    tokens_out(prodd, ctx0, wv0, KD, D)
                else:
                    prodd.skip(pd.full, 2)
                if main:
                    pe.wait_ge(normed.sem, normed.at(b, 1))
                    turn_both(xn, TA_X1, TD_X1)
                    tokens_out(prodd, xnT, router, KD, E0N)
                    def gate_up(i):
                        t, (f0, fn) = i // 3, CH0[i % 3]
                        tokens_out(proda, xnT, wg0, KD, fn, ts=(t,), c0=f0)
                        tokens_out(prodd, xnT, wu0, KD, fn, ts=(t,), c0=f0)

                    def turn_hid(i):
                        t, (f0, fn) = i // 3, CH0[i % 3]
                        if i % 3 < 2:
                            pe.wait_ge(hid_weighed.sem, hid_weighed.at(b, 2 * t + i % 3 + 1))
                        else:
                            pe.wait_ge(pd.empty.sem, pd.empty.at(b, PD_U + i))
                        turn((trd, tra)[i % 2], [hid[:, t, f0 + j * P:f0 + (j + 1) * P] for j in range(fn // P)])

                    def down(t, ks, *turned):
                        for i in turned:
                            r, n = ((td, TD_H), (ta, TA_H))[i % 2]
                            pe.wait_ge(r.empty.sem, r.empty.at(b, n + i // 2))
                        for k in ks:
                            ins = mm(dst[:, t * D:(t + 1) * D], hidT[:, k, t * P:(t + 1) * P], wd0[:, k, :], start=(k == 0), stop=(k == F0T - 1))
                        return ins

                    for i in range(4):
                        gate_up(i)
                    turn_hid(0)
                    gate_up(4)
                    turn_hid(1)
                    gate_up(5)
                    for i in (2, 3):
                        turn_hid(i)
                    dst = prodd.claim()
                    wide, last = range(F0T - M0S // P), range(F0T - M0S // P, F0T)
                    down(0, wide, 0, 1)
                    for i in (4, 5):
                        turn_hid(i)
                    down(0, last, 2)
                    down(1, wide, 3, 4)
                    down(1, last, 5).then_inc(pd.full.sem, 1)
                    values1(1)
                    pe.wait_ge(normed.sem, normed.at(b, 2))
                    turn_both(xn, TA_X2, TD_X2)
                    for m in range(4):
                        features_out((proda, prodd)[m % 2], wq1, xnT, (2 * m, 2 * m + 1))
                else:
                    prodd.skip(pd.full, PD_Q0 - PD_V0 - 1)

                for i in range(N_S1 + 3):
                    if main and i < N_S1:
                        pair, t = i // 2, i % 2
                        if i % 4 == 0:
                            r, n = (pa, PA_Q1 + i // 8) if i % 8 == 0 else (pd, PD_Q1 + i // 8)
                            pe.wait_ge(r.empty.sem, r.empty.at(b, n))
                        dst = proda.claim()
                        mm(dst[:, :], qT1[:, pair, t * P:(t + 1) * P], kpad1[:, 2 * pair:2 * pair + 2, :], start=True, stop=True).then_inc(pa.full.sem, 1)
                    if main and 3 <= i:
                        j = i - 3
                        pe.wait_ge(p1_ready.sem, p1_ready.at(b, j + 1))
                        turn((tra, trd)[j % 2], [p1[:, j % 4, e, k * P:(k + 1) * P] for k in range(T) for e in range(2)])
                    if i == AHEAD_TURN:
                        if ahead:
                            pe.wait_ge(normed.sem, normed.at(b, 3))
                            turn(tra, [xn[:, t, k * P:(k + 1) * P] for k in range(KD) for t in range(T)])
                        else:
                            tra.skip(ta.full, 1)
                    if i == N_S1 + 1:
                        if ahead:
                            pe.wait_ge(ta.empty.sem, ta.empty.at(b, ta_p1(12) - 1))
                            features_out(prodd, wq0, xnT, (0, 1))
                        else:
                            prodd.skip(pd.full, 1)
                    if main and i >= 6 and i % 2 == 0:
                        av_p1((i - 6) // 2, prodd.claim())
                if main:
                    av_dst, dst = prodd.claim(), prodd.claim()

                    def output(t, ks):
                        for k in ks:
                            ins = mm(dst[:, t * D:(t + 1) * D], avT1[:, k, t * P:(t + 1) * P], wo1[:, k, :],
                                     start=(k == 0), stop=(k == I1T - 1))
                        return ins

                    output(0, range(0, I1T // 2))
                    av_p1(I1T - 1, av_dst)
                    output(0, range(I1T // 2, I1T - 1))
                    pe.wait_ge(pd.empty.sem, pd.empty.at(b, PD_AV7))
                    output(0, (I1T - 1,))
                    output(1, range(I1T)).then_inc(pd.full.sem, 1)
                else:
                    prodd.skip(pd.full, 3)
                if ahead:
                    pe.wait_ge(pd.empty.sem, pd.empty.at(b, PD_Q0))
                    for i in range(4):
                        scores0(i)
                if main:
                    pe.wait_ge(normed.sem, normed.at(b, 4))
                    turn_both(pay[:, :, 0], TA_X3, TD_X3)
                    tokens_out(prodd, xnT, gate1, KD, E1N)
                else:
                    prodd.skip(pd.full, 3)
                    tra.skip(ta.full, 3)
                for i in range(4, N_S0):
                    if ahead and i == KEYS_AT:
                        if not main:
                            pe.wait_ge(w1_loaded, 16)
                        pe.wait_ge(ctx_loaded.sem, ctx_loaded.at(b, 16))
                        features_out(tra, wk1, ctx_in, (0, 1))
                    if ahead:
                        scores0(i)
                    if main and i == RANK_AFTER:
                        pe.wait_ge(both_ready.sem, both_ready.at(b, 1))
                        dst = prodd.claim()
                        mm(dst[:, 0:E1N], below, both[:, 0, :], start=True, stop=True)
                        mm(dst[:, E1N:2 * E1N], below, both[:, 1, :], start=True, stop=False)
                        mm(dst[:, E1N:2 * E1N], onesb, both[:, 0, :], start=False, stop=True)
                        mm(dst[:, 2 * E1N:3 * E1N], onesb, both[:, 0, :], start=True, stop=False)
                        mm(dst[:, 2 * E1N:3 * E1N], onesb, both[:, 1, :], start=False, stop=True).then_inc(pd.full.sem, 1)
                    if main and i == N_S0 - 1:
                        prodd.skip(pd.full, 1)
                if ahead:
                    assert (tra.n, trd.n, prodd.n, proda.n) == (N_TA, N_TD, N_PD, N_PA), (tra.n, trd.n, prodd.n, proda.n)

            pe.wait_ge(c_loaded, 32)
            pe.wait_ge(wl0_loaded, 16)
            batch(-1, main=False)
            pe.wait_ge(w_loaded, 32)
            pe.wait_ge(pads, 3)
            with pe.Fori(0, B - 1) as b:
                batch(b)
            batch(B - 1, ahead=False)


def tables_of(c):
    return tuple(c("cover")[:, i * (NBLK + 1):(i + 1) * (NBLK + 1)].bitcast(I32) for i in range(2))


def experts(nc, cst, wts, expert_loaded, pad_ids, we1, rows, out):
    with ExitStack() as ctx:
        def sb(name, shape, dt=F32):
            return ctx.enter_context(nc.sbuf_tensor(name, shape, dt))

        def sem(name):
            return ctx.enter_context(nc.semaphore(name))

        def bank(name):
            return ctx.enter_context(nc.psum_tensor(name, [P, 512], F32))

        def c(name):
            return cst[:, C_F32[name][0]:sum(C_F32[name])]

        N = NBLK + 1
        ident = c("ident")
        xs = sb("xs", [P, ROW])
        xT = sb("xT", [P, KD, P])
        hs = sb("hs_e", [P, 512])
        hid = sb("hid_e", [P, F1])
        hidT = sb("hidT_e", [P, F1T, P])
        y = sb("y", [P, D])
        wt_next, wt_now = sb("wt_next", [P, 1]), sb("wt_now", [P, 1])
        id_next, id_now = sb("id_next", [P, 1], I32), sb("id_now", [P, 1], I32)
        row_i, eid_i = tables_of(c)

        turns_a = [bank(f"turn_a2{i}") for i in range(2)]
        turn_d, acc_bank = bank("turn_d2"), bank("acc_bank")
        prod_d = [bank(f"prod_d2{i}") for i in range(2)]
        prod_a = [bank(f"prod_a2{i}") for i in range(2)]
        signals = {}

        def signal(name, per, owner):
            s = Signal(sem(name), per)
            signals.setdefault(owner, []).append(s)
            return s

        pd = Ring(prod_d, signal("up_full", 2 * STEPS, "pe"), signal("up_empty", 2 * STEPS, "dve"))
        pa = Ring(prod_a, signal("gate_full", 2 * STEPS, "pe"), signal("gate_empty", 2 * STEPS, "act"))
        ta = Ring(turns_a, Signal(sem("turn_a2_full"), 2 * STEPS, 2), Signal(sem("turn_a2_empty"), 2 * STEPS, 2))
        td = Ring([turn_d], signal("turn_d2_full", STEPS, "pe"), signal("turn_d2_empty", STEPS, "dve"))
        ya = Ring([acc_bank], signal("y_full", STEPS, "pe"), signal("y_empty", STEPS, "dve"))
        xs_loaded = Signal(sem("xs_loaded"), 16 * STEPS, 16)
        added = Signal(sem("added"), 16 * STEPS, 16)
        meta = Signal(sem("meta"), STEPS, 1)
        moved = signal("moved", STEPS, "dve")
        expert_ready = sem("expert_ready")
        chain = sem("chain_e")
        spare = sem("spare2")

        def prime(eng, owner):
            for s in signals[owner]:
                eng.sem_inc(s.sem, s.per)

        block = ctx.enter_context(nc.Block())

        @block.sync
        def _(sp):
            sp.wait_ge(xs_loaded.sem, 16)
            for e in range(E1N):
                if e >= 2:
                    part = WE1 // 6
                    for i in range(6):
                        sp.dma_start(wts[:, e * WE1 + i * part:e * WE1 + (i + 1) * part], we1[e][:, i * part:(i + 1) * part]).then_inc(expert_loaded[e], 16)
                        sp.wait_ge(expert_loaded[e], 16 * (i + 1))
                else:
                    sp.wait_ge(expert_loaded[e], 16)
                sp.sem_inc(expert_ready, 1)

        @block.gpsimd
        def _(pool):
            at = pool.value_load(row_i[0:1, 0:1], min_val=0, max_val=E1N * CAP)
            pool.dma_start(xs[:, :], rows[bass.ds(at, P), :]).then_inc(xs_loaded.sem, 16)
            pool.dma_start(y[:, :], pad_ids[:, 0:D]).then_inc(added.sem, 16)
            with pool.Fori(0, NBLK // STEPS) as j:
                for u in range(STEPS):
                    pool.wait_ge(meta.sem, meta.at(j, u))
                    pool.wait_ge(ta.full.sem, ta.full.at(j, 2 * u - 1))
                    at = pool.value_load(row_i[0:1, bass.ds(j * STEPS + u + 1, 1)], min_val=0, max_val=E1N * CAP)
                    pool.dma_start(xs[:, :], rows[bass.ds(at, P), :]).then_inc(xs_loaded.sem, 16)
                    pool.wait_ge(ya.empty.sem, ya.empty.at(j, u + 1))
                    pool.sem_inc(spare, 1)
                    pool.indirect_dma_start(out, bass.IndirectOffsetOnAxis(ap=id_now[:, 0:1], axis=0), y[:, :], None,
                                            compute_op=ALU.add).then_inc(added.sem, 16)
            pool.wait_ge(added.sem, 16 * (NBLK + 1))

        @block.scalar
        def _(act):
            prime(act, "act")
            act.wait_ge(ta.full.sem, 2)
            nc.scalar.activation(xT[:, :, :], turns_a[0][:, 0:KD * P].rearrange("p (k n) -> p k n", k=KD), ACT.Copy).then_inc(ta.empty.sem, 2)
            with act.Fori(0, NBLK // STEPS) as j:
                tra, proda = Turn(act, ta, j), Turn(act, pa, j)
                for u in range(STEPS):
                    for i in range(2):
                        src = proda.take()
                        act.wait_ge(pd.empty.sem, pd.empty.at(j, 2 * u + i))
                        nc.scalar.activation(hs[:, :], src[:, :], ACT.Silu).then_inc(pa.empty.sem, 1)
                    src = tra.take()
                    nc.scalar.activation(xT[:, :, :], src[:, 0:KD * P].rearrange("p (k n) -> p k n", k=KD), ACT.Copy).then_inc(ta.empty.sem, 1)
                    src = tra.take()
                    nc.scalar.activation(hidT[:, 4:8, :], src[:, :].rearrange("p (f n) -> p f n", n=P), ACT.Copy).then_inc(ta.empty.sem, 1)

        @block.vector
        def _(dve):
            prime(dve, "dve")
            n = [0]

            def then(ins):
                n[0] += 1
                ins.then_inc(chain, 1)
                dve.wait_ge(chain, n[0])

            dve.wait_ge(xs_loaded.sem, 16)
            then(nc.vector.tensor_copy(wt_next[:, :], xs[:, D:D + 1]))
            nc.vector.tensor_copy(id_next[:, :], xs[:, D + 1:D + 2].bitcast(I32)).then_inc(meta.sem, 1)
            with dve.Fori(0, NBLK // STEPS) as j:
                trd, prodd, acc_t = Turn(dve, td, j), Turn(dve, pd, j), Turn(dve, ya, j)

                def product(i):
                    src = prodd.take()
                    dve.wait_ge(pa.empty.sem, pa.empty.at(j, prodd.n))
                    nc.vector.tensor_tensor(hid[:, i * 512:(i + 1) * 512], src[:, :], hs[:, :], ALU.mult).then_inc(pd.empty.sem, 1)

                for u in range(STEPS):
                    product(0)
                    src = trd.take()
                    nc.vector.tensor_copy(hidT[:, 0:4, :], src[:, :].rearrange("p (f n) -> p f n", n=P)).then_inc(td.empty.sem, 1)
                    product(1)
                    dve.wait_ge(added.sem, added.at(j, 16 * u))
                    dve.wait_ge(meta.sem, meta.at(j, u))
                    nc.vector.tensor_copy(wt_now[:, :], wt_next[:, :])
                    nc.vector.tensor_copy(id_now[:, :], id_next[:, :]).then_inc(moved.sem, 1)
                    dve.wait_ge(moved.sem, moved.at(j, u + 1))
                    dve.wait_ge(xs_loaded.sem, xs_loaded.at(j, 16 * (u + 1)))
                    nc.vector.tensor_copy(wt_next[:, :], xs[:, D:D + 1])
                    nc.vector.tensor_copy(id_next[:, :], xs[:, D + 1:D + 2].bitcast(I32)).then_inc(meta.sem, 1)
                    src = acc_t.take()
                    nc.vector.tensor_scalar(y[:, :], src[:, 0:D], wt_now[:, 0:1], None, ALU.mult).then_inc(ya.empty.sem, 1)

        @block.tensor
        def _(pe):
            prime(pe, "pe")
            mm = nc.tensor.matmul
            pe.wait_ge(xs_loaded.sem, 16)
            for k in range(KD):
                ins = nc.tensor.transpose(turns_a[0][:, k * P:(k + 1) * P], xs[:, k * P:(k + 1) * P], ident)
            ins.then_inc(ta.full.sem, 2)
            with pe.Fori(0, NBLK // STEPS) as j:
                tra, trd, prodd, proda, acc_t = (Turn(pe, r, j) for r in (ta, td, pd, pa, ya))

                def half(ring, base, which, i):
                    dst = ring.claim()
                    for k in range(KD):
                        ins = mm(dst[:, :], xT[:, k, :], wts[:, bass.ds(base + (which * KD + k) * F1 + i * 512, 512)], start=(k == 0), stop=(k == KD - 1))
                    ins.then_inc(ring.ring.full.sem, 1)

                def turn(ring, tiles):
                    dst = ring.claim()
                    for i, src in enumerate(tiles):
                        ins = nc.tensor.transpose(dst[:, i * P:(i + 1) * P], src, ident)
                    ins.then_inc(ring.ring.full.sem, 1)

                def down(dst, base, f0, f1):
                    for f in range(f0, f1):
                        ins = mm(dst[:, 0:D], hidT[:, f, :], wts[:, bass.ds(base + 2 * KD * F1 + f * D, D)], start=(f == 0), stop=(f == F1T - 1))
                    return ins

                for u in range(STEPS):
                    e = pe.value_load(eid_i[0:1, bass.ds(j * STEPS + u, 1)], min_val=0, max_val=E1N - 1)
                    pe.wait_ge(expert_ready, e + 1)
                    base = e * WE1
                    pe.wait_ge(ta.empty.sem, ta.empty.at(j, 2 * u - 1))
                    half(proda, base, 0, 0)
                    half(prodd, base, 1, 0)
                    half(proda, base, 0, 1)
                    pe.wait_ge(pd.empty.sem, pd.empty.at(j, 2 * u + 1))
                    turn(trd, [hid[:, f * P:(f + 1) * P] for f in range(4)])
                    half(prodd, base, 1, 1)
                    dst = acc_t.claim()
                    pe.wait_ge(td.empty.sem, td.empty.at(j, u + 1))
                    down(dst, base, 0, 2)
                    pe.wait_ge(xs_loaded.sem, xs_loaded.at(j, 16 * (u + 1)))
                    turn(tra, [xs[:, k * P:(k + 1) * P] for k in range(KD)])
                    pe.wait_ge(pd.empty.sem, pd.empty.at(j, 2 * u + 2))
                    turn(tra, [hid[:, f * P:(f + 1) * P] for f in range(4, 8)])
                    down(dst, base, 2, 4)
                    pe.wait_ge(ta.empty.sem, ta.empty.at(j, 2 * u + 2))
                    down(dst, base, 4, 8).then_inc(ya.full.sem, 1)


def build(nc, cf32, cb16, w32, tok0, pad_ids, x, ctxT, we1, out):
    rows = nc.dram_tensor("rows", [E1N * CAP + P, ROW], F32, kind="Internal").ap()
    with ExitStack() as ctx:
        cst = ctx.enter_context(nc.sbuf_tensor("cst", [P, NC32], F32))
        wts = ctx.enter_context(nc.sbuf_tensor("wts", [P, E1N * WE1], F32))
        expert_loaded = [ctx.enter_context(nc.semaphore(f"expert_loaded{e}")) for e in range(E1N)]
        layers(nc, cst, wts, expert_loaded, cf32, cb16, w32, tok0, pad_ids, x, ctxT, we1, out, rows)
        experts(nc, cst, wts, expert_loaded, pad_ids, we1, rows, out)


def kernel(**inputs):
    import ml_dtypes
    import concourse.bacc as bacc
    from concourse.bass_utils import run_bass_kernel_spmd as run_spmd

    f32 = np.float32
    a = {k: np.asarray(v) for k, v in inputs.items()}

    p = np.arange(P)
    cf = np.zeros((P, NC32), f32)

    def put(table, dst, name, value):
        at, n = table[name]
        dst[:, at:at + n] = np.reshape(value, (-1, n)) if np.ndim(value) else value

    heads = np.arange(H0)
    put(C_F32, cf, "ident", np.eye(P, dtype=f32))
    put(C_F32, cf, "head", p[:, None] // DH0 == np.arange(G0)[None])
    cover = np.zeros((P, NBR, T, H0), f32)
    for r, dil in enumerate((1, 2, 4)):
        cover[:, r] = (p[:, None] % dil == heads[None] // (H0 // dil))[:, None]
    put(C_F32, cf, "cover", cover)
    for name, dil in (("class2", 2), ("class4", 4)):
        put(C_F32, cf, name, np.tile((np.arange(4)[None] % dil == heads[:, None] // (H0 // dil)).reshape(1, -1), (P, 1)))
    put(C_F32, cf, "iota", np.tile(np.arange(16), (P, 1)))
    put(C_F32, cf, "region", np.tile(np.arange(E1N) * CAP, (P, 1)))
    put(C_F32, cf, "neghalf", -0.5)
    put(C_F32, cf, "blocks", np.tile(np.arange(NBLK + 1), (P, 1)))
    put(C_F32, cf, "upto", np.tile((np.arange(E1N)[None] <= np.arange(E1N)[:, None]).reshape(1, -1), (P, 1)))
    cb = np.zeros((P, NCB), ml_dtypes.bfloat16)
    cb[:, 0:P] = np.eye(P)
    cb[:, P:2 * P] = np.where(p[None] <= p[:, None], 0.0, -1e30)
    cb[:, 2 * P:3 * P] = p[:, None] < p[None]
    cb[:, 3 * P:] = 1.0
    pad_ids = np.zeros((P, ROW), f32)
    pad_ids[:, D + 1] = (NTOK + p).astype(np.int32).view(f32)
    tok0 = (p[:, None] + P * np.arange(T)[None]).astype(np.int32)

    w = np.zeros((P, NW32), f32)
    tiles = lambda m: m.reshape(-1, P, m.shape[-1]).transpose(1, 0, 2).reshape(P, -1)
    wide = lambda r, s: np.concatenate([r.transpose(1, 0, 2).reshape(D, -1), s.transpose(1, 0, 2).reshape(D, -1)], 1)
    for name, key in (("wq0", "Wq"), ("wk0", "Wk"), ("wv0", "Wv"), ("wo0", "Wo")):
        put(W_F32, w, name, tiles(a["L0_xattn_" + key].T))
    put(W_F32, w, "router", tiles(a["L0_ffn_router_w"]))
    put(W_F32, w, "wg0", tiles(wide(a["L0_ffn_wg_r"], a["L0_ffn_wg_s"])))
    put(W_F32, w, "wu0", tiles(wide(a["L0_ffn_wu_r"], a["L0_ffn_wu_s"])))
    put(W_F32, w, "wd0", tiles(np.concatenate([a["L0_ffn_wd_r"].reshape(-1, D), a["L0_ffn_wd_s"].reshape(-1, D)])))
    put(W_F32, w, "wq1", tiles(a["L1_xattn_w_q"]))
    put(W_F32, w, "wk1", tiles(a["L1_xattn_w_kv"][:, :I1]))
    put(W_F32, w, "wv1", tiles(a["L1_xattn_w_kv"][:, I1:]))
    put(W_F32, w, "wo1", tiles(a["L1_xattn_w_out"]))
    put(W_F32, w, "gate1", tiles(a["L1_ffn_gate_w"]))
    for name, key in (("bq0", "L0_xattn_bq"), ("bk0", "L0_xattn_bk"), ("gamma", "L1_xattn_ln_gamma"), ("beta", "L1_xattn_ln_beta")):
        put(W_F32, w, name, a[key].reshape(KD, P).T)
    put(W_F32, w, "gate", np.tile(a["L1_xattn_gate"], (P, 1)))
    for name, key in (("bv0", "L0_xattn_bv"), ("bo0", "L0_xattn_bo"), ("bo1", "L1_xattn_b_out")):
        put(W_F32, w, name, np.tile(a[key], (P, 1)))
    we1 = np.concatenate([
        a["L1_ffn_w1"].reshape(E1N, KD, P, F1).transpose(0, 2, 1, 3).reshape(E1N, P, -1),
        a["L1_ffn_w3"].reshape(E1N, KD, P, F1).transpose(0, 2, 1, 3).reshape(E1N, P, -1),
        a["L1_ffn_w2"].reshape(E1N, F1T, P, D).transpose(0, 2, 1, 3).reshape(E1N, P, -1)], 2)
    ctxT = a["ctx_1024"].transpose(0, 2, 1)

    arrays = {"cf32": cf, "cb16": cb, "w32": w, "tok0": tok0, "pad_ids": pad_ids, "x": a["x"], "ctxT": ctxT, "we1": we1}
    arrays = {k: np.ascontiguousarray(v) for k, v in arrays.items()}
    nc = bacc.Bacc("TRN2", target_bir_lowering=False, num_devices=1)
    aps = {k: nc.dram_tensor(k + "_dram", v.shape, mybir.dt.from_np(v.dtype), kind="ExternalInput").ap() for k, v in arrays.items()}
    out = nc.dram_tensor("out_dram", (NTOK + P, D), F32, kind="ExternalOutput").ap()
    build(nc, out=out, **aps)
    r = run_spmd(nc, [{k + "_dram": v for k, v in arrays.items()}], core_ids=[0])
    return r.results[0]["out_dram"][0:NTOK].reshape(B, L, D)
```
